# Optimizing a Trainium2 kernel written in Bass

```python
import numpy as np
import jax
import jax.numpy as jnp

def _softmax(x, axis=-1):
    return jax.nn.softmax(x, axis=axis)

def _gelu(x):
    return jax.nn.gelu(x, approximate=True)

def _silu(x):
    return jax.nn.silu(x)

def _sigmoid(x):
    return jax.nn.sigmoid(x)

def _layernorm(x, axis=-1, eps=1e-05):
    m = jnp.mean(x, axis=axis, keepdims=True)
    v = jnp.var(x, axis=axis, keepdims=True)
    return (x - m) / jnp.sqrt(v + eps)

def _scatter_add(tgt, idx, src, axis=0):
    return tgt.at[idx].add(src)

def _segment_sum(src, seg, n):
    return jax.ops.segment_sum(src, seg, n)
kernel_name = 'mk_adj_preln_d4_adj_r2_90b9a8'

def setup_inputs(seed: int=0):
    np.random.seed(seed)
    _w = jnp.asarray

    def _rec_inputs():
        import jax
        import jax.numpy as jnp
        _gk = jax.random.key(seed)
        x = -0.000929 + 1 * jax.random.normal(jax.random.fold_in(_gk, 1), (1354, 128), jnp.float32)
        _a = jax.random.bernoulli(jax.random.fold_in(_gk, 2), 0.00295421, (1354, 1354))
        _a = jnp.logical_or(_a, jnp.eye(1354, dtype=bool))
        _af = _a.astype(jnp.float32)
        _af = _af * jax.random.uniform(jax.random.fold_in(_gk, 3), (1354, 1354), jnp.float32, 0.05, 1)
        adj = _af
        return (x, adj)
    x, adj = _rec_inputs()

    def _L0_gnn_setup():
        import jax, jax.numpy as jnp
        import numpy as np
        NEG_SLOPE = 0.01
        N_U, N_V = (4096, 4096)
        U_F, V_F = (128, 128)
        HIDS = [128, 128]
        NUM_ROUNDS = 3

        def _glorot(key, fan_in, fan_out):
            lim = np.sqrt(6.0 / (fan_in + fan_out)).astype(np.float32)
            return jax.random.uniform(key, (fan_in, fan_out), jnp.float32, -lim, lim)

        def _mlp(x, W1, b1, W2, b2, W3, b3):
            a = jax.nn.leaky_relu
            x = a(x @ W1 + b1, NEG_SLOPE)
            x = a(x @ W2 + b2, NEG_SLOPE)
            return a(x @ W3 + b3, NEG_SLOPE)
        key = jax.random.key(seed)
        ks = jax.random.split(key, 12)
        inp = {'u_node_feats': jax.random.normal(ks[0], (N_U, U_F), jnp.float32), 'v_node_feats': jax.random.normal(ks[1], (N_V, V_F), jnp.float32), 'uv_adj_mat': jax.random.uniform(ks[2], (N_V, N_U), jnp.float32), 'vu_adj_mat': jax.random.uniform(ks[3], (N_U, N_V), jnp.float32)}
        dims_uv = [U_F] + HIDS + [V_F]
        dims_vu = [V_F] + HIDS + [U_F]
        k = 4
        for tag, dims in (('uv', dims_uv), ('vu', dims_vu)):
            for i in range(3):
                inp[f'{tag}_W{i + 1}'] = _glorot(ks[k], dims[i], dims[i + 1])
                k += 1
                inp[f'{tag}_b{i + 1}'] = jnp.zeros((dims[i + 1],), jnp.float32)
        return inp
    _L0_gnn_all = _L0_gnn_setup()
    _L0_gnn_in = {k: v for k, v in _L0_gnn_all.items() if k in ('v_node_feats', 'uv_W1', 'uv_b1', 'uv_W2', 'uv_b2', 'uv_W3', 'uv_b3', 'vu_W1', 'vu_b1', 'vu_W2', 'vu_b2', 'vu_W3', 'vu_b3')}
    del _L0_gnn_all

    def _L1_gnn_setup():
        import jax, jax.numpy as jnp
        import numpy as np
        N = 4096
        DIN = 128
        DOUT = 128
        EPS = 1e-07
        GAMMA_MAX = 10000000.0

        def _mobius_scalar_mul(r, x):
            n = jnp.linalg.norm(x, axis=-1, keepdims=True)
            n_safe = jnp.clip(n, EPS, 1.0 - EPS)
            return jnp.tanh(r * jnp.arctanh(n_safe)) * x / n_safe

        def _logmap0(x):
            n = jnp.linalg.norm(x, axis=-1, keepdims=True)
            n_safe = jnp.clip(n, EPS, 1.0 - EPS)
            return jnp.arctanh(n_safe) * x / n_safe

        def _expmap0(v):
            n = jnp.linalg.norm(v, axis=-1, keepdims=True)
            n_safe = jnp.maximum(n, EPS)
            return jnp.tanh(n_safe) * v / n_safe
        key = jax.random.key(seed)
        k1, k2, k3, k4 = jax.random.split(key, 4)
        x = 0.01 * jax.random.normal(k1, (N, DIN), dtype=jnp.float32)
        adj = (jax.random.uniform(k2, (N, N)) < 0.004).astype(jnp.float32)
        W = 0.05 * jax.random.normal(k3, (DIN, DOUT), dtype=jnp.float32)
        b = 0.05 * jax.random.normal(k4, (DOUT,), dtype=jnp.float32)
        return {'x': x, 'adj': adj, 'W': W, 'b': b}
    _L1_gnn_all = _L1_gnn_setup()
    _L1_gnn_in = {k: v for k, v in _L1_gnn_all.items() if k in ('W', 'b')}
    del _L1_gnn_all

    def _L2_gnn_setup():
        import jax, jax.numpy as jnp
        import numpy as np

        def _lap_mul(A, x):
            d = 1.0 / jnp.sqrt(jnp.sum(A, axis=-1))
            return d[:, None] * (A @ (d[:, None] * x))
        key = jax.random.key(seed)
        k1, k2, k3, k4, k5, k6 = jax.random.split(key, 6)
        N, D_IN, D_OUT = (2048, 128, 128)
        x = jax.random.normal(k1, (N, D_IN), dtype=jnp.float32)
        A = jax.random.uniform(k2, (N, N), dtype=jnp.float32)
        s1 = 1.0 / np.sqrt(D_IN)
        W1 = jax.random.uniform(k3, (D_IN, D_OUT), minval=-s1, maxval=s1, dtype=jnp.float32)
        b1 = jax.random.uniform(k4, (D_OUT,), minval=-s1, maxval=s1, dtype=jnp.float32)
        W2 = jax.random.uniform(k5, (D_IN, D_OUT), minval=-s1, maxval=s1, dtype=jnp.float32)
        b2 = jax.random.uniform(k6, (D_OUT,), minval=-s1, maxval=s1, dtype=jnp.float32)
        return {'x': x, 'A': A, 'W1': W1, 'b1': b1, 'W2': W2, 'b2': b2, 'sigma': 1, 'k': 4}
    _L2_gnn_all = _L2_gnn_setup()
    _L2_gnn_in = {k: v for k, v in _L2_gnn_all.items() if k in ('W1', 'b1', 'W2', 'b2')}
    del _L2_gnn_all

    def _L3_gnn_setup():
        import jax, jax.numpy as jnp
        import numpy as np
        N = 512
        IN_DIM = 128
        OUT_DIM = 128
        HEADS = 4

        def _gatv2_head(x, A_shape, w1, w2, a, Wlin):
            x1 = x @ w1
            x2 = x @ w2
            E = jax.nn.leaky_relu(x1[:, None, :] + x2[None, :, :], negative_slope=0.01)
            s = E @ a
            s = jnp.tanh(s / 8.0) * 8.0
            s = jnp.exp(s) * A_shape
            s = s / jnp.sum(s, axis=-1, keepdims=True)
            out = s @ x @ Wlin.T
            return jax.nn.leaky_relu(out, negative_slope=0.01)
        key = jax.random.key(seed)
        ks = jax.random.split(key, 7)
        x = jax.random.normal(ks[0], (N, IN_DIM), dtype=jnp.float32)
        A_shape = jax.random.uniform(ks[1], (N, N), dtype=jnp.float32)
        w1 = jax.random.normal(ks[2], (HEADS, IN_DIM, OUT_DIM), dtype=jnp.float32)
        w2 = jax.random.normal(ks[3], (HEADS, IN_DIM, OUT_DIM), dtype=jnp.float32)
        a = jax.random.normal(ks[4], (HEADS, OUT_DIM), dtype=jnp.float32)
        Wlin = jax.random.normal(ks[5], (HEADS, OUT_DIM, IN_DIM), dtype=jnp.float32) * (1.0 / np.sqrt(IN_DIM))
        w = jax.random.normal(ks[6], (OUT_DIM * HEADS, OUT_DIM), dtype=jnp.float32)
        return {'x': x, 'A_shape': A_shape, 'w1': w1, 'w2': w2, 'a': a, 'Wlin': Wlin, 'w': w}
    _L3_gnn_all = _L3_gnn_setup()
    _L3_gnn_in = {k: v for k, v in _L3_gnn_all.items() if k in ('w1', 'w2', 'a', 'Wlin', 'w')}
    del _L3_gnn_all
    return {'x': x, 'adj': adj, 'L0_gnn_v_node_feats': _L0_gnn_in['v_node_feats'], 'L0_gnn_uv_W1': _L0_gnn_in['uv_W1'], 'L0_gnn_uv_b1': _L0_gnn_in['uv_b1'], 'L0_gnn_uv_W2': _L0_gnn_in['uv_W2'], 'L0_gnn_uv_b2': _L0_gnn_in['uv_b2'], 'L0_gnn_uv_W3': _L0_gnn_in['uv_W3'], 'L0_gnn_uv_b3': _L0_gnn_in['uv_b3'], 'L0_gnn_vu_W1': _L0_gnn_in['vu_W1'], 'L0_gnn_vu_b1': _L0_gnn_in['vu_b1'], 'L0_gnn_vu_W2': _L0_gnn_in['vu_W2'], 'L0_gnn_vu_b2': _L0_gnn_in['vu_b2'], 'L0_gnn_vu_W3': _L0_gnn_in['vu_W3'], 'L0_gnn_vu_b3': _L0_gnn_in['vu_b3'], 'L1_gnn_W': _L1_gnn_in['W'], 'L1_gnn_b': _L1_gnn_in['b'], 'L2_gnn_W1': _L2_gnn_in['W1'], 'L2_gnn_b1': _L2_gnn_in['b1'], 'L2_gnn_W2': _L2_gnn_in['W2'], 'L2_gnn_b2': _L2_gnn_in['b2'], 'L3_gnn_w1': _L3_gnn_in['w1'], 'L3_gnn_w2': _L3_gnn_in['w2'], 'L3_gnn_a': _L3_gnn_in['a'], 'L3_gnn_Wlin': _L3_gnn_in['Wlin'], 'L3_gnn_w': _L3_gnn_in['w']}

def reference(x, adj, L0_gnn_v_node_feats, L0_gnn_uv_W1, L0_gnn_uv_b1, L0_gnn_uv_W2, L0_gnn_uv_b2, L0_gnn_uv_W3, L0_gnn_uv_b3, L0_gnn_vu_W1, L0_gnn_vu_b1, L0_gnn_vu_W2, L0_gnn_vu_b2, L0_gnn_vu_W3, L0_gnn_vu_b3, L1_gnn_W, L1_gnn_b, L2_gnn_W1, L2_gnn_b1, L2_gnn_W2, L2_gnn_b2, L3_gnn_w1, L3_gnn_w2, L3_gnn_a, L3_gnn_Wlin, L3_gnn_w):
    import jax
    import jax.numpy as jnp

    def _L0_gnn_ref(u_node_feats, v_node_feats, uv_adj_mat, vu_adj_mat, uv_W1, uv_b1, uv_W2, uv_b2, uv_W3, uv_b3, vu_W1, vu_b1, vu_W2, vu_b2, vu_W3, vu_b3):
        import jax, jax.numpy as jnp
        import numpy as np
        NEG_SLOPE = 0.01
        N_U, N_V = (4096, 4096)
        U_F, V_F = (128, 128)
        HIDS = [128, 128]
        NUM_ROUNDS = 3

        def _glorot(key, fan_in, fan_out):
            lim = np.sqrt(6.0 / (fan_in + fan_out)).astype(np.float32)
            return jax.random.uniform(key, (fan_in, fan_out), jnp.float32, -lim, lim)

        def _mlp(x, W1, b1, W2, b2, W3, b3):
            a = jax.nn.leaky_relu
            x = a(x @ W1 + b1, NEG_SLOPE)
            x = a(x @ W2 + b2, NEG_SLOPE)
            return a(x @ W3 + b3, NEG_SLOPE)
        u, v = (u_node_feats, v_node_feats)
        for _ in range(NUM_ROUNDS):
            v = _mlp(uv_adj_mat @ u, uv_W1, uv_b1, uv_W2, uv_b2, uv_W3, uv_b3)
            u = _mlp(vu_adj_mat @ v, vu_W1, vu_b1, vu_W2, vu_b2, vu_W3, vu_b3)
        return v

    def _L1_gnn_ref(x, adj, W, b):
        import jax, jax.numpy as jnp
        import numpy as np
        N = 4096
        DIN = 128
        DOUT = 128
        EPS = 1e-07
        GAMMA_MAX = 10000000.0

        def _mobius_scalar_mul(r, x):
            n = jnp.linalg.norm(x, axis=-1, keepdims=True)
            n_safe = jnp.clip(n, EPS, 1.0 - EPS)
            return jnp.tanh(r * jnp.arctanh(n_safe)) * x / n_safe

        def _logmap0(x):
            n = jnp.linalg.norm(x, axis=-1, keepdims=True)
            n_safe = jnp.clip(n, EPS, 1.0 - EPS)
            return jnp.arctanh(n_safe) * x / n_safe

        def _expmap0(v):
            n = jnp.linalg.norm(v, axis=-1, keepdims=True)
            n_safe = jnp.maximum(n, EPS)
            return jnp.tanh(n_safe) * v / n_safe
        n = adj.shape[0]
        a = jnp.eye(n, dtype=adj.dtype) + adj
        D = 1.0 / jnp.sqrt(jnp.sum(a, axis=1))
        a = a * D[:, None] * D[None, :]
        r2 = jnp.sum(x * x, axis=-1, keepdims=True)
        gamma = jnp.minimum(2.0 / (1.0 - r2), GAMMA_MAX)
        num = a * gamma
        den = jnp.sum(a * (gamma - 1.0), axis=-1, keepdims=True)
        coef = num / den
        aggr = coef @ x
        aggr = _mobius_scalar_mul(0.5, aggr)
        u = _logmap0(aggr)
        y = jax.nn.relu(u @ W + b)
        return _expmap0(y)

    def _L2_gnn_ref(x, A, W1, b1, W2, b2, sigma, k):
        import jax, jax.numpy as jnp
        import numpy as np

        def _lap_mul(A, x):
            d = 1.0 / jnp.sqrt(jnp.sum(A, axis=-1))
            return d[:, None] * (A @ (d[:, None] * x))
        z = _lap_mul(A, x) @ W1 + b1
        z = jax.nn.leaky_relu(z, negative_slope=0.1)
        sq = jnp.sum(z * z, axis=-1)
        d2 = sq[:, None] + sq[None, :] - 2.0 * (z @ z.T)
        d2 = jnp.maximum(d2, 0.0)
        S = jnp.sqrt(d2 + 1e-10)
        S = jnp.exp(-S / (2.0 * sigma))
        order = jnp.argsort(-S, axis=-1)
        ranks = jnp.argsort(order, axis=-1)
        S = jnp.where(ranks < k, S, 0.0)
        A2 = S + A
        out = _lap_mul(A2, x) @ W2 + b2
        return out

    def _L3_gnn_ref(x, A_shape, w1, w2, a, Wlin, w):
        import jax, jax.numpy as jnp
        import numpy as np
        N = 512
        IN_DIM = 128
        OUT_DIM = 128
        HEADS = 4

        def _gatv2_head(x, A_shape, w1, w2, a, Wlin):
            x1 = x @ w1
            x2 = x @ w2
            E = jax.nn.leaky_relu(x1[:, None, :] + x2[None, :, :], negative_slope=0.01)
            s = E @ a
            s = jnp.tanh(s / 8.0) * 8.0
            s = jnp.exp(s) * A_shape
            s = s / jnp.sum(s, axis=-1, keepdims=True)
            out = s @ x @ Wlin.T
            return jax.nn.leaky_relu(out, negative_slope=0.01)
        heads = [_gatv2_head(x, A_shape, w1[h], w2[h], a[h], Wlin[h]) for h in range(w1.shape[0])]
        return jnp.concatenate(heads, axis=-1) @ w
    h = jnp.maximum(_layernorm(x, axis=-1), 0.0)
    x = x + _L0_gnn_ref(h, L0_gnn_v_node_feats, adj, adj, L0_gnn_uv_W1, L0_gnn_uv_b1, L0_gnn_uv_W2, L0_gnn_uv_b2, L0_gnn_uv_W3, L0_gnn_uv_b3, L0_gnn_vu_W1, L0_gnn_vu_b1, L0_gnn_vu_W2, L0_gnn_vu_b2, L0_gnn_vu_W3, L0_gnn_vu_b3)
    h = jnp.maximum(_layernorm(x, axis=-1), 0.0)
    x = x + _L1_gnn_ref(h, adj, L1_gnn_W, L1_gnn_b)
    h = jnp.maximum(_layernorm(x, axis=-1), 0.0)
    x = x + _L2_gnn_ref(h, adj, L2_gnn_W1, L2_gnn_b1, L2_gnn_W2, L2_gnn_b2, 1, 4)
    h = jnp.maximum(_layernorm(x, axis=-1), 0.0)
    x = x + _L3_gnn_ref(h, adj, L3_gnn_w1, L3_gnn_w2, L3_gnn_a, L3_gnn_Wlin, L3_gnn_w)
    return x

_drawn_inputs = setup_inputs


def setup_inputs(seed=0):
    import zlib

    import numpy as np

    out = dict(_drawn_inputs(seed))
    spreads = {'L0_gnn_uv_b1': (0.0, 0.1),
     'L0_gnn_uv_b2': (0.0, 0.1),
     'L0_gnn_uv_b3': (0.0, 0.1),
     'L0_gnn_vu_b1': (0.0, 0.1),
     'L0_gnn_vu_b2': (0.0, 0.1),
     'L0_gnn_vu_b3': (0.0, 0.1)}
    factors = {'L1_gnn_W': 4.466}
    for name, (base, spread) in spreads.items():
        noise = np.random.default_rng([zlib.crc32(name.encode()), seed]).standard_normal(out[name].shape)
        drawn = base * np.exp(spread * noise) if base else spread * noise
        out[name] = jnp.asarray(drawn.astype(out[name].dtype))
    for name, factor in factors.items():
        out[name] = (out[name] * factor).astype(out[name].dtype)
    return out
```

```python
import concourse.bass as bass
from concourse import mybir
from contextlib import ExitStack

F32 = mybir.dt.float32
F32R = mybir.dt.float32r
I32 = mybir.dt.int32
U32 = mybir.dt.uint32
ALU = mybir.AluOpType
ACT = mybir.ActivationFunctionType
AX = mybir.AxisListType

N = 1354
D = 128
P = 128
NT = -(-N // P)
NP = NT * P
LAST = N - (NT - 1) * P
ROUNDS = 3
HEADS = 4
HD = HEADS * D
CHUNKS = [(0, 4), (4, 8), (8, NT)]
NC = len(CHUNKS)
TWO = 32
MAIN = 8
NBR = 2 * MAIN
TOPK = 4
GS = 4
TW = HD + D + HEADS
LAST_STAGE = 2 * ROUNDS - 2
N_WEIGHTS = 23
(MEAN, SSQ, VAR, RSTD, ROWSUM, DEG, DEGI, RS2, DL, R2, GAM, GM, GD, AN2, AN, NS, T_A, T_B, T_C, T_D, NN, NSB, SER,
 FAC, QUO, LNQ, YN2, YN, TH, EF, NSQ, SSUM, DD2I, DD, FB, OVF, CUM, POS, T_E) = range(39)
FAR = 1 << 20


EARLY = 6
SLOPE = 0.01
UNITS = 2 * (NT + 1)
EPS = 1e-7
ONE_EPS = 1.0 - 2.0 ** -23
GAMMA_MAX = 1e7


class Link:

    def __init__(self, eng, sem):
        self.eng, self.sem, self.n = eng, sem, 0

    def __call__(self, ins):
        self.n += 1
        ins.then_inc(self.sem, 1)
        self.eng.wait_ge(self.sem, self.n)


def unit(u):
    return (NT if u < 2 else u // 2 - 1), u % 2


def cols(c):
    return CHUNKS[c][0] * P, CHUNKS[c][1] * P


def build(nc, x, adj, v_unused, uW1, ub1, uW2, ub2, uW3, ub3, vW1, vb1, vW2, vb2, vW3, vb3,
          hW, hb, lW1, lb1, lW2, lb2, gw1, gw2, ga, gWlin, gw, out):
    with ExitStack() as ctx:
        def sb(name, shape, dt=F32):
            return ctx.enter_context(nc.sbuf_tensor(name, shape, dt))

        def sem(name):
            return ctx.enter_context(nc.semaphore(name))

        A = sb("A", [P, NT, NP])
        AT = sb("AT", [P, NT, NP])
        X = sb("X", [P, NT, D])
        UH = sb("UH", [P, 2 * NT * D])
        U = UH[:, 0:NT * D].rearrange("p (t d) -> p t d", d=D)
        H = UH[:, NT * D:2 * NT * D].rearrange("p (t d) -> p t d", d=D)
        R = sb("R", [P, 3 * NP])
        Z = R[:, 0:NP]
        T1 = R[:, NP:2 * NP]
        T2 = R[:, 2 * NP:3 * NP]
        NX = R[:, 0:NT * (D + 1)].rearrange("p (t n) -> p t n", n=D + 1)
        XG = sb("XG", [P, NT * (D + 1) + 1 + 3 * TOPK * D])
        XC = XG[:, 0:NT * (D + 1)].rearrange("p (t n) -> p t n", n=D + 1)
        JUNK = sb("JUNK", [P, NP])
        SQ = sb("SQ", [P, NP], F32R)
        OW = sb("OW", [P, P], F32R)
        ident = sb("ident", [P, P])
        ones = sb("ones", [P, P])
        negs = sb("negs", [P, P])
        ltri = sb("ltri", [P, P])
        iota = sb("iota", [P, P])
        padone = sb("padone", [P, NT])
        mhalf = sb("mhalf", [P, NT * TOPK])
        phalf = sb("phalf", [P, NT * TOPK])
        W0 = sb("W0", [P, 6, D])
        bcol = sb("bcol", [P, 4 + 1])
        b3 = sb("b3", [P, 2, D])
        brow = sb("brow", [P, 2, D])
        W12 = sb("W12", [P, 3, D])
        GW = sb("GW", [P, 2, HD])
        aB = sb("aB", [P, HD])
        WPQ = sb("WPQ", [P, 2, HEADS])
        WL = sb("WL", [P, HEADS, D])
        WLT = sb("WLT", [P, HEADS, D])
        WO = sb("WO", [P, HEADS, D])
        WG = sb("WG", [P, NT, NBR])
        IG = sb("IG", [P, NT, NBR], U32)
        IGF = sb("IGF", [P, NT, NBR])
        IGU = sb("IGU", [P, NT + 1, MAIN], U32)
        WGO = sb("WGO", [P, NBR])
        CNT = sb("CNT", [P, NT])
        c16 = sb("c16", [P, NT, NBR])
        st = sb("st", [P, 48, NT])
        V8 = sb("V8", [P, NT, 8])
        I8 = sb("I8", [P, NT, 8], U32)
        S4 = sb("S4", [P, NT, TOPK])
        OH = UH[:, 0:NT*P].rearrange("p (t n) -> p t n", n=P)
        tally = sb("tally", [P, 2])
        within = sb("within", [1, 2])
        away = sb("away", [P, NT, MAIN])
        flag = sb("flag", [1, 1], I32)
        mask = sb("mask", [P, NT], I32)
        SCR = XG[:, NT * (D + 1) + 1:NT * (D + 1) + 1 + N]
        G2 = XG[:, NT * (D + 1) + 1:].rearrange("p (a k d) -> p a k d", a=3, d=D)
        flatAT = AT[:, :, :].rearrange("p t n -> p (t n)")
        o = 0
        X1H = flatAT[:, o:o + NT * HD].rearrange("p (t n) -> p t n", n=HD); o += NT * HD
        NUM = flatAT[:, o:o + NT * HD].rearrange("p (t n) -> p t n", n=HD); o += NT * HD
        Ga = flatAT[:, o:o + GS * TW].rearrange("p (k n) -> p k n", n=TW); o += GS * TW
        OHT = flatAT[:, o:o + NT * P].rearrange("p (t n) -> p t n", n=P); o += NT * P
        assert o <= NT * NP
        Gb = R[:, 0:GS * TW].rearrange("p (k n) -> p k n", n=TW)
        Gc = XG[:, 0:GS * TW].rearrange("p (k n) -> p k n", n=TW)
        GB = [Ga, Gb, Gc]
        EG = R[:, GS * TW:GS * TW + 2 * HD].rearrange("p (k n) -> p k n", n=HD)
        TT = UH[:, 0:GS * HD].rearrange("p (k n) -> p k n", n=HD)
        XO = UH[:, GS * HD:GS * HD + HD]
        AGT = [UH[:, 0:HD], UH[:, HD:2 * HD]]
        LRS = [UH[:, 2 * HD:3 * HD], UH[:, 3 * HD:4 * HD]]
        NO = JUNK[:, 0:HD]
        PQ = sb("PQ", [P, NT, HEADS])
        PO = sb("PO", [P, HEADS])
        DEN = sb("DEN", [P, NT + 1, HEADS])
        sc = sb("sc", [P, 2, 3, GS * HEADS])
        EW = sb("EW", [P, NT + 1, MAIN, HEADS])
        EWF = sb("EWF", [P, GS, HEADS])
        DENF = sb("DENF", [P, HEADS])

        TAB2 = nc.dram_tensor("tab2", [NP, D], F32, kind="Internal").ap()
        TAB3 = nc.dram_tensor("tab3", [NP, TW], F32, kind="Internal").ap()

        PS = ctx.enter_context(nc.psum_tensor("PS", [P, 8, 512], F32))

        def bank(b, n=512):
            return PS[:, b, 0:n]

        ld_x, ld_w, ld_a = sem("ld_x"), sem("ld_w"), [sem(f"ld_a{t}") for t in range(NT)]
        pads, consts = sem("pads"), sem("consts")
        dve_self, act_self, pool_self = sem("dve_self"), sem("act_self"), sem("pool_self")
        st_out = sem("st_out")
        tr_done, tr_evac = sem("tr_done"), sem("tr_evac")
        u_ready = sem("u_ready")
        agg_done, agg_evac = sem("agg_done"), sem("agg_evac")
        l1_done, l1_bias, l1_act = sem("l1_done"), sem("l1_bias"), sem("l1_act")
        l2_done, l2_bias, l2_act = sem("l2_done"), sem("l2_bias"), sem("l2_act")
        l3_done, l3_sum = sem("l3_done"), sem("l3_sum")
        rowsum_ready = sem("rowsum_ready")
        ln_centred, ln_squared, ln_var, ln_rstd, h_ready = (sem("ln_centred"), sem("ln_squared"), sem("ln_var"),
                                                            sem("ln_rstd"), sem("h_ready"))
        deg_ready, degi_ready, dl_ready = sem("deg_ready"), sem("degi_ready"), sem("dl_ready")
        rsq_ready, ye_ready = sem("rsq_ready"), sem("ye_ready")
        ragg_done, ragg_evac = sem("ragg_done"), sem("ragg_evac")
        row_ready, rowT_done, rowT_evac = sem("row_ready"), sem("rowT_done"), sem("rowT_evac")
        n2_ready, pow_in, pow_out = sem("n2_ready"), sem("pow_in"), sem("pow_out")
        q_ready, ln_ready, prod_done = sem("q_ready"), sem("ln_ready"), sem("prod_done")
        y_ready, yn2_ready, yn_ready, tanh_ready = sem("y_ready"), sem("yn2_ready"), sem("yn_ready"), sem("tanh_ready")
        x_ready = sem("x_ready")
        rs2_ready, ys_ready = sem("rs2_ready"), sem("ys_ready")
        z_done, z_bias, z_ready, z2_ready, zsq_ready = (sem("z_done"), sem("z_bias"), sem("z_ready"), sem("z2_ready"),
                                                        sem("zsq_ready"))
        sqb_done, sqb_evac, nsq_done, nsq_evac = sem("sqb_done"), sem("sqb_evac"), sem("nsq_done"), sem("nsq_evac")
        sq_ready, dist_done, key_read = sem("sq_ready"), sem("dist_done"), sem("key_read")
        d4_in, d4_out, s4_ready, ssum_ready, dd_ready = (sem("d4_in"), sem("d4_out"), sem("s4_ready"),
                                                         sem("ssum_ready"), sem("dd_ready"))
        yd_ready, tab2_written, cnt_ready = sem("yd_ready"), sem("tab2_written"), sem("cnt_ready")
        cnt_sign = sem("cnt_sign")
        near_here = [sem(f"near_here{i}") for i in range(3)]
        plan_ready, plan_done, flag_ready, oh_ready, over_done = (sem("plan_ready"), sem("plan_done"),
                                                                  sem("flag_ready"), sem("oh_ready"), sem("over_done"))
        idx_ready = sem("idx_ready")
        wl_done, wl_evac = sem("wl_done"), sem("wl_evac")
        x1_done, x1_evac, x2_done, x2_evac, row3_ready = (sem("x1_done"), sem("x1_evac"), sem("x2_done"),
                                                          sem("x2_evac"), sem("row3_ready"))
        tab3_written = [sem(f"tab3_written{i}") for i in range(2)]
        oht_done, oht_evac, xo_done, g_clear = sem("oht_done"), sem("oht_evac"), sem("xo_done"), sem("g_clear")
        g_here = [sem(f"g_here{i}") for i in range(3)]
        score_ready, exp_ready, ew_ready = sem("score_ready"), sem("exp_ready"), sem("ew_ready")
        eg_ready, eg_used = sem("eg_ready"), sem("eg_used")
        no_ready, num_done = sem("no_ready"), sem("num_done")
        f_used, f_here, f_self, f_score, f_tanh, f_exp = (sem("f_used"), sem("f_here"), sem("f_self"), sem("f_score"),
                                                          sem("f_tanh"), sem("f_exp"))
        num_ready = sem("num_ready")
        numT_done, numT_evac, lin_done, lin_copied, lin_ready, fin_done, out_ready = (
            sem("numT_done"), sem("numT_evac"), sem("lin_done"), sem("lin_copied"), sem("lin_ready"), sem("fin_done"),
            sem("out_ready"))
        block = ctx.enter_context(nc.Block())

        def nth(s, c):
            return NC * s + c

        def pe_agg(pe, s, kind, c, j0, j1, src):
            lo, hi = cols(c)
            for j in range(j0, j1):
                if src is U and j in (0, 4, 8):
                    pe.wait_ge(u_ready, nth(s - 1, j // 4) + 1)
                last = nc.tensor.matmul(bank(3 * kind + c, hi - lo), src[:, j, :], AT[:, j, lo:hi],
                                        start=(j == 0), stop=(j == NT - 1))
            if j1 == NT:
                last.then_inc(agg_done, 1)

        def pe_l1(pe, s, kind, c):
            lo, hi = cols(c)
            pe.wait_ge(agg_evac, nth(s, c) + 1)
            if not (isinstance(s, int) and s == 0 and c == 0):
                pe.wait_ge(l1_bias, nth(s, c))
            nc.tensor.matmul(bank(6, hi - lo), W0[:, 3 * kind, :], Z[:, lo:hi],
                             start=True, stop=True).then_inc(l1_done, 1)

        def pe_l2(pe, s, kind, c):
            lo, hi = cols(c)
            pe.wait_ge(l1_act, nth(s, c) + 1)
            if not (isinstance(s, int) and s == 0 and c == 0):
                pe.wait_ge(l2_bias, nth(s, c))
            nc.tensor.matmul(bank(7, hi - lo), W0[:, 3 * kind + 1, :], T1[:, lo:hi],
                             start=True, stop=True).then_inc(l2_done, 1)

        def pe_l3(pe, s, kind, c):
            pe.wait_ge(l2_act, nth(s, c) + 1)
            a, b = CHUNKS[c]
            for t in range(a, b):
                last = nc.tensor.matmul(PS[:, 3 * kind + c, (t - a) * D:(t - a + 1) * D],
                                        T2[:, t * P:(t + 1) * P], W0[:, 3 * kind + 2, :],
                                        start=True, stop=True)
            last.then_inc(l3_done, 1)

        def act_agg(act, s, kind, c):
            lo, hi = cols(c)
            act.wait_ge(agg_done, nth(s, c) + 1)
            nc.scalar.activation(Z[:, lo:hi], bank(3 * kind + c, hi - lo), ACT.Copy).then_inc(agg_evac, 1)

        def act_bias(act, s, kind, c, layer):
            lo, hi = cols(c)
            done, said, dst = (l1_done, l1_bias, T1) if layer == 1 else (l2_done, l2_bias, T2)
            act.wait_ge(done, nth(s, c) + 1)
            nc.scalar.activation(dst[:, lo:hi], bank(5 + layer, hi - lo), ACT.Identity,
                                 bias=bcol[:, 2 * kind + layer - 1:2 * kind + layer]).then_inc(said, 1)

        def dve_leaky(dve, s, c, layer):
            lo, hi = cols(c)
            given, said, dst = (l1_bias, l1_act, T1) if layer == 1 else (l2_bias, l2_act, T2)
            dve.wait_ge(given, nth(s, c) + 1)
            nc.vector.scalar_tensor_tensor(dst[:, lo:hi], dst[:, lo:hi], 0.01, dst[:, lo:hi],
                                           ALU.mult, ALU.max).then_inc(said, 1)

        def dve_l3(dve, s, kind, c):
            a, b = CHUNKS[c]
            dve.wait_ge(l3_done, nth(s, c) + 1)
            nc.vector.tensor_tensor(XC[:, a:b, 0:D],
                                    bank(3 * kind + c, (b - a) * D).rearrange("p (t d) -> p t d", d=D),
                                    b3[:, kind:kind + 1, :].to_broadcast([P, b - a, D]),
                                    ALU.add).then_inc(l3_sum, 1)
            dve.wait_ge(l3_sum, nth(s, c) + 1)
            nc.vector.scalar_tensor_tensor(U[:, a:b, :], XC[:, a:b, 0:D], 0.01, XC[:, a:b, 0:D],
                                           ALU.mult, ALU.max).then_inc(u_ready, 1)

        def pe_stage(pe, s, kind):
            k = 1 - kind
            pe_agg(pe, s, kind, 0, 0, 1, U)
            pe_l2(pe, s - 1, k, 1)
            pe_agg(pe, s, kind, 0, 1, 2, U)
            pe_l1(pe, s - 1, k, 2)
            pe_agg(pe, s, kind, 0, 2, 3, U)
            pe_l3(pe, s - 1, k, 1)
            pe_agg(pe, s, kind, 0, 3, 4, U)
            pe_l2(pe, s - 1, k, 2)
            pe_agg(pe, s, kind, 1, 0, 3, U)
            pe_l3(pe, s - 1, k, 2)
            pe_agg(pe, s, kind, 1, 3, 4, U)
            pe_agg(pe, s, kind, 0, 4, 8, U)
            pe_agg(pe, s, kind, 1, 4, 8, U)
            pe_agg(pe, s, kind, 0, 8, NT, U)
            pe_agg(pe, s, kind, 2, 0, 4, U)
            pe_l1(pe, s, kind, 0)
            pe_agg(pe, s, kind, 2, 4, 8, U)
            pe_l2(pe, s, kind, 0)
            pe_agg(pe, s, kind, 1, 8, NT, U)
            pe_l3(pe, s, kind, 0)
            pe_agg(pe, s, kind, 2, 8, NT, U)
            pe_l1(pe, s, kind, 1)

        def pe_rest(pe, s, kind):
            pe_l2(pe, s, kind, 1)
            pe_l1(pe, s, kind, 2)
            pe_l3(pe, s, kind, 1)
            pe_l2(pe, s, kind, 2)
            pe_l3(pe, s, kind, 2)

        def act_rest(act, s, kind):
            act_bias(act, s, kind, 1, 2)
            act_bias(act, s, kind, 2, 1)
            act_bias(act, s, kind, 2, 2)

        def act_stage(act, s, kind):
            act_agg(act, s, kind, 0)
            act_bias(act, s, kind, 0, 1)
            act_bias(act, s, kind, 0, 2)
            act_agg(act, s, kind, 1)
            act_agg(act, s, kind, 2)
            act_bias(act, s, kind, 1, 1)

        def dve_rest(dve, s, kind):
            dve_leaky(dve, s, 1, 2)
            dve_leaky(dve, s, 2, 1)
            dve_l3(dve, s, kind, 1)
            dve_leaky(dve, s, 2, 2)
            dve_l3(dve, s, kind, 2)

        def dve_stage(dve, s, kind):
            dve_leaky(dve, s, 0, 1)
            dve_leaky(dve, s, 0, 2)
            dve_l3(dve, s, kind, 0)
            dve_leaky(dve, s, 1, 1)

        def dve_center(link, l, c):
            a, b = CHUNKS[c]
            link(nc.vector.reduce_sum(st[:, MEAN, a:b], X[:, a:b, :], AX.X))
            link(nc.vector.tensor_scalar(st[:, MEAN, a:b], st[:, MEAN, a:b], 1.0 / D, None, ALU.mult))
            nc.vector.tensor_tensor(XC[:, a:b, 0:D], X[:, a:b, :],
                                    st[:, MEAN, a:b].unsqueeze(2).to_broadcast([P, b - a, D]),
                                    ALU.subtract).then_inc(ln_centred, 1)

        def act_square(act, l, c):
            a, b = CHUNKS[c]
            act.wait_ge(ln_centred, nth(l, c) + 1)
            for t in range(a, b):
                last = nc.scalar.activation(JUNK[:, t * D:(t + 1) * D], XC[:, t, 0:D], ACT.Square,
                                            accum_out=st[:, SSQ, t:t + 1])
            last.then_inc(ln_squared, 1)

        def dve_var(dve, l, c):
            a, b = CHUNKS[c]
            dve.wait_ge(ln_squared, nth(l, c) + 1)
            nc.vector.tensor_scalar(st[:, VAR, a:b], st[:, SSQ, a:b], 1.0 / D, 1e-5, ALU.mult,
                                    ALU.add).then_inc(ln_var, 1)

        def pool_rstd(pool, l, c):
            a, b = CHUNKS[c]
            pool.wait_ge(ln_var, nth(l, c) + 1)
            pool.tensor_tensor(st[:, RSTD, a:b], st[:, VAR, a:b], mhalf[:, a:b], ALU.pow).then_inc(ln_rstd, 1)

        def dve_norm(dve, l, c):
            a, b = CHUNKS[c]
            dve.wait_ge(ln_rstd, nth(l, c) + 1)
            for t in range(a, b):
                last = nc.vector.tensor_scalar(H[:, t, :], XC[:, t, 0:D], st[:, RSTD, t:t + 1], 0.0,
                                               ALU.mult, ALU.max)
            last.then_inc(h_ready, 1)

        def dve_layernorm(dve, link, l):
            for c in range(NC):
                dve_center(link, l, c)
            for c in range(NC):
                dve_var(dve, l, c)
                dve_norm(dve, l, c)

        def dve_neighbours(link, t, scratch):
            link(nc.vector.max(WG[:, t, 0:8], A[:, t, 0:N]))
            link(nc.vector.max_index(IG[:, t, 0:8], WG[:, t, 0:8], A[:, t, 0:N]))
            link(nc.vector.match_replace(scratch, WG[:, t, 0:8], A[:, t, 0:N], 0.0))
            link(nc.vector.max(WG[:, t, 8:16], scratch))
            link(nc.vector.max_index(IG[:, t, 8:16], WG[:, t, 8:16], scratch))

        def act_count(act, t):
            at = slice(t, t + 1) if isinstance(t, int) else bass.ds(t, 1)
            nc.scalar.activation(JUNK[:, :].unsqueeze(1), A[:, at, :], ACT.Sign).then_inc(cnt_sign, 1)
            act.wait_ge(cnt_sign, t + 1)
            nc.scalar.activation(JUNK[:, :], JUNK[:, :], ACT.Square,
                                 accum_out=CNT[:, at]).then_inc(cnt_ready, 1)
            act.wait_ge(cnt_ready, t + 1)

        @block.sync
        def _(sp):
            def rows(t):
                return P if t < NT - 1 else LAST

            full = NT - 1
            sp.dma_start(X[:, 0:full, :], x[0:full * P, :].rearrange("(t p) d -> p t d", p=P)).then_inc(ld_x, 16)
            sp.wait_ge(pads, 2)
            sp.dma_start(X[0:LAST, full, :], x[full * P:N, :]).then_inc(ld_x, 16)
            def load_tiles(a, b):
                for t in range(a, b):
                    sp.dma_start(A[0:rows(t), t, 0:N], adj[t * P:t * P + rows(t), :]).then_inc(ld_a[t], 16)

            load_tiles(0, 4)
            for i, w in enumerate((uW1, uW2, uW3, vW1, vW2, vW3)):
                sp.dma_start(W0[:, i, :], w).then_inc(ld_w, 16)
            for i, b in enumerate((ub1, ub2, vb1, vb2, lb1)):
                sp.dma_start(bcol[:, i:i + 1], b.rearrange("(p o) -> p o", o=1)).then_inc(ld_w, 16)
            for i, b in enumerate((ub3, vb3)):
                sp.dma_start(b3[:, i, :], b.rearrange("(o d) -> o d", o=1).to_broadcast([P, D])).then_inc(ld_w, 16)
            load_tiles(4, NT)
            for i, b in enumerate((hb, lb2)):
                sp.dma_start(brow[:, i, :], b.rearrange("(o d) -> o d", o=1).to_broadcast([P, D])).then_inc(ld_w, 16)
            for i, w in enumerate((hW, lW1, lW2)):
                sp.dma_start(W12[:, i, :], w).then_inc(ld_w, 16)
            for i, w in enumerate((gw1, gw2)):
                sp.dma_start(GW[:, i, :].rearrange("p (h d) -> p h d", d=D),
                              w.rearrange("h p d -> p h d")).then_inc(ld_w, 16)
            sp.dma_start(aB[:, :], ga.rearrange("(o h) d -> o (h d)", o=1).to_broadcast([P, HD])).then_inc(ld_w, 16)
            sp.dma_start(WL[:, :, :], gWlin.rearrange("h p d -> p h d")).then_inc(ld_w, 16)
            sp.dma_start(WO[:, :, :], gw.rearrange("(h p) d -> p h d", p=P)).then_inc(ld_w, 16)
            for c, (a, b) in enumerate(CHUNKS):
                sp.wait_ge(yd_ready, c + 1)
                sp.dma_start(TAB2[a * P:b * P, :].rearrange("(t p) d -> p t d", p=P), U[:, a:b, :])\
                  .then_inc(tab2_written, 16)
            for t in range(NT):
                sp.wait_ge(row3_ready, t + 1)
                sp.dma_start(TAB3[t * P:(t + 1) * P, :], JUNK[:, (t % 2) * TW:(t % 2 + 1) * TW])\
                  .then_inc(tab3_written[t % 2], 16)
            sp.wait_ge(flag_ready, 1)
            sparse = sp.value_load(flag[0:1, 0:1], min_val=0, max_val=1)
            with sp.If(sparse < 1):
                sp.wait_ge(tab3_written[0], 16 * ((NT + 1) // 2))
                sp.wait_ge(tab3_written[1], 16 * (NT // 2))
                with sp.Fori(0, NT) as t:
                    with sp.Fori(0, NP // GS) as g:
                        sp.wait_ge(f_used, t * (NP // GS) + g + 1)
                        sp.dma_start(Ga[:, :, :],
                                     TAB3[bass.ds(g * GS, GS), :].rearrange("(o k) n -> o k n", o=1)
                                     .to_broadcast([P, GS, TW])).then_inc(f_here, 16)
            for t in range(NT):
                n = P if t < NT - 1 else LAST
                sp.wait_ge(out_ready, t + 1)
                sp.dma_start(out[t * P:t * P + n, :], X[0:n, t, :]).then_inc(st_out, 16)
            sp.wait_ge(st_out, 16 * NT)

        @block.scalar
        def _(act):
            alink = Link(act, act_self)
            for c in range(NC):
                act_square(act, 0, c)

            def transposed(t):
                for g, (a, b) in enumerate(CHUNKS):
                    act.wait_ge(tr_done, nth(t, g) + 1)
                    nc.scalar.activation(AT[:, a:b, t * P:(t + 1) * P],
                                         bank(3 + g, (b - a) * P).rearrange("p (j i) -> p j i", i=P),
                                         ACT.Copy).then_inc(tr_evac, 1)

            def rowsum(t):
                act.wait_ge(ld_a[t], 16)
                act.wait_ge(pads, 3)
                if t > 0:
                    act.wait_ge(rowsum_ready, t)
                nc.scalar.activation(JUNK[:, :], A[:, t, :], ACT.Copy,
                                     accum_out=st[:, ROWSUM, t:t + 1]).then_inc(rowsum_ready, 1)

            for t in range(0, 4):
                transposed(t)
            for t in range(4, 8):
                transposed(t)
                rowsum(t - 4)
            act.wait_ge(ld_w, 16 * N_WEIGHTS)
            act_agg(act, 0, 0, 0)
            act_bias(act, 0, 0, 0, 1)
            act_bias(act, 0, 0, 0, 2)
            for t in range(8, NT):
                transposed(t)
                rowsum(t - 4)
            act_agg(act, 0, 0, 1)
            act_bias(act, 0, 0, 1, 1)
            act_agg(act, 0, 0, 2)

            def fill(s):
                act.wait_ge(rowsum_ready, s + 7)
                nc.scalar.activation(JUNK[:, :].unsqueeze(1), A[:, bass.ds(s + 7, 1), :], ACT.Copy,
                                     accum_out=st[:, ROWSUM, bass.ds(s + 7, 1)]).then_inc(rowsum_ready, 1)
                act.wait_ge(rowsum_ready, s + 8)
                act_count(act, 2 * s)
                act_count(act, 2 * s + 1)

            with act.Fori(0, ROUNDS - 1) as r:
                act_rest(act, 2 * r, 0)
                fill(2 * r)
                act_stage(act, 2 * r + 1, 1)
                act_rest(act, 2 * r + 1, 1)
                fill(2 * r + 1)
                act_stage(act, 2 * r + 2, 0)
            act_rest(act, LAST_STAGE, 0)

            def squares(dst, src, ready, base, said):
                for t in range(NT):
                    if t in (0, 4, 8):
                        act.wait_ge(ready, base + t // 4 + 1)
                    last = nc.scalar.activation(JUNK[:, t * D:(t + 1) * D], src[:, t, :], ACT.Square,
                                                accum_out=st[:, dst, t:t + 1])
                last.then_inc(said, 1)

            def row_transposed(base, c):
                lo, hi = cols(c)
                act.wait_ge(rowT_done, base + c + 1)
                nc.scalar.activation(T2[:, lo:hi], bank(6 + c % 2, hi - lo), ACT.Copy).then_inc(rowT_evac, 1)

            act.wait_ge(rowsum_ready, NT)
            for c in range(NC):
                act_square(act, 1, c)
            squares(R2, H, h_ready, NC, rsq_ready)
            act.wait_ge(rsq_ready, 1)
            for t in range(NT):
                act.wait_ge(row_ready, t + 1)
                last = nc.scalar.activation(JUNK[:, t * D:(t + 1) * D], U[:, t, :], ACT.Square,
                                            accum_out=st[:, AN2, t:t + 1])
                if t in (5, 9):
                    row_transposed(0, (t - 5) // 4)
            last.then_inc(n2_ready, 1)
            row_transposed(0, 2)
            act.wait_ge(q_ready, 1)
            nc.scalar.activation(st[:, LNQ, :], st[:, QUO, :], ACT.Ln).then_inc(ln_ready, 1)
            act.wait_ge(n2_ready, 1)
            squares(YN2, U, y_ready, 0, yn2_ready)
            act.wait_ge(yn_ready, 1)
            nc.scalar.activation(st[:, TH, :], st[:, NS, :], ACT.Tanh).then_inc(tanh_ready, 1)

            act.wait_ge(yn2_ready, 1)
            for c in range(NC):
                act_square(act, 2, c)
            for t in range(NT):
                act.wait_ge(ragg_done, NT + t + 1)
                nc.scalar.activation(U[:, t, :], bank(t % 6, D), ACT.Copy,
                                     scale=st[:, DL, t:t + 1]).then_inc(ragg_evac, 1)
                if t in (1, 3, 7):
                    if t == 1:
                        act.wait_ge(ln_squared, NC * 3)
                    act_count(act, 8 + t // 3)
                if t in (5, 9):
                    row_transposed(NC, (t - 5) // 4)
            row_transposed(NC, 2)
            for c in range(NC):
                lo, hi = cols(c)
                act.wait_ge(z_done, c + 1)
                nc.scalar.activation(Z[:, lo:hi], bank(c, hi - lo), ACT.Identity, bias=bcol[:, 4:5]).then_inc(z_bias, 1)
            for c in range(NC):
                lo, hi = cols(c)
                act.wait_ge(z_ready, c + 1)
                nc.scalar.activation(T2[:, lo:hi], Z[:, lo:hi], ACT.Square).then_inc(zsq_ready, 1)
            for c in range(NC):
                lo, hi = cols(c)
                act.wait_ge(sqb_done, c + 1)
                nc.scalar.activation(SQ[:, lo:hi], bank(3 + c, hi - lo), ACT.Copy).then_inc(sqb_evac, 1)
            act.wait_ge(nsq_done, 1)
            nc.scalar.activation(st[:, NSQ, :], bank(6, NT), ACT.Copy).then_inc(nsq_evac, 1)
            for t in range(NT):
                act.wait_ge(d4_out, t + 1)
                nc.scalar.activation(S4[:, t, :], S4[:, t, :], ACT.Exp, scale=-0.5,
                                     accum_out=st[:, SSUM, t:t + 1]).then_inc(s4_ready, 1)
            for c in range(NC):
                row_transposed(2 * NC, c)

            for c in range(NC):
                act_square(act, 3, c)
            for c in range(NC):
                row_transposed(3 * NC, c)
            act.wait_ge(wl_done, 1)
            nc.scalar.activation(WLT[:, :, :].rearrange("p h d -> p (h d)"), bank(7), ACT.Copy).then_inc(wl_evac, 1)
            for t in range(NT):
                act.wait_ge(x1_done, t + 1)
                nc.scalar.activation(X1H[:, t, :], bank(t % 3), ACT.Copy).then_inc(x1_evac, 1)
            act.wait_ge(flag_ready, 1)
            sparse = act.value_load(flag[0:1, 0:1], min_val=0, max_val=1)
            with act.If(sparse > 0):
                for c, (a, b) in enumerate(CHUNKS):
                    act.wait_ge(oht_done, c + 1)
                    nc.scalar.activation(OHT[:, a:b, :].rearrange("p t n -> p (t n)"), bank(c, (b - a) * P),
                                         ACT.Copy).then_inc(oht_evac, 1)

                def blend(u):
                    T, g = unit(u)
                    act.wait_ge(ew_ready, u + 1)
                    for k in range(GS):
                        if GS * u + k >= 2:
                            act.wait_ge(eg_used, GS * u + k - 1)
                        for h in range(HEADS):
                            ins = nc.scalar.activation(EG[:, k % 2, h * D:(h + 1) * D], GB[u % 3][:, k, HD:HD + D],
                                                       ACT.Copy, scale=EW[:, T, g * GS + k, h:h + 1])
                        ins.then_inc(eg_ready, 1)

                for u in range(UNITS):
                    s2 = sc[:, u % 2, 2, :]
                    if u >= 1:
                        blend(u - 1)
                    act.wait_ge(score_ready, u + 1)
                    alink(nc.scalar.activation(s2, s2, ACT.Tanh, scale=0.125))
                    nc.scalar.activation(s2, s2, ACT.Exp, scale=8.0).then_inc(exp_ready, 1)
                blend(UNITS - 1)
            with act.Else():
                with act.Fori(0, NT * (NP // GS)) as n:
                    s2 = sc[:, 0, 2, :]
                    act.wait_ge(f_score, n + 1)
                    nc.scalar.activation(s2, s2, ACT.Tanh, scale=0.125).then_inc(f_tanh, 1)
                    act.wait_ge(f_tanh, n + 1)
                    nc.scalar.activation(s2, s2, ACT.Exp, scale=8.0).then_inc(f_exp, 1)
            for t in range(NT + 1):
                if t < NT:
                    act.wait_ge(numT_done, t + 1)
                    nc.scalar.activation(AGT[t % 2], bank(t % 2), ACT.Copy).then_inc(numT_evac, 1)
                if t >= 1:
                    act.wait_ge(lin_done, t)
                    nc.scalar.activation(LRS[(t - 1) % 2], bank(2 + (t - 1) % 2), ACT.Copy).then_inc(lin_copied, 1)

        @block.vector
        def _(dve):
            link = Link(dve, dve_self)
            nc.vector.memset(X[64:P, NT - 1, :], 0.0).then_inc(pads, 1)
            nc.vector.memset(A[64:P, NT - 1, 0:N], 0.0).then_inc(pads, 1)
            nc.vector.memset(A[:, :, N:NP], 0.0).then_inc(pads, 1)
            dve.wait_ge(ld_x, 32)
            dve_layernorm(dve, link, 0)
            for t in range(2):
                dve.wait_ge(ld_a[t], 16)
                dve_neighbours(link, t, SCR)
            dve.wait_ge(ld_w, 16 * N_WEIGHTS)
            for i in range(2):
                link(nc.vector.tensor_tensor(SCR[:, 0:HD], GW[:, i, :], aB[:, :], ALU.mult))
                link(nc.vector.reduce_sum(WPQ[:, i, :], SCR[:, 0:HD].rearrange("p (h d) -> p h d", d=D), AX.X))
            dve_neighbours(link, 2, SCR)
            dve_leaky(dve, 0, 0, 1)
            dve_neighbours(link, 3, SCR)
            dve_leaky(dve, 0, 0, 2)
            dve_neighbours(link, 4, SCR)
            dve_l3(dve, 0, 0, 0)
            dve_neighbours(link, 5, SCR)
            dve_leaky(dve, 0, 1, 1)
            for s in range(1, LAST_STAGE + 1):
                dve_rest(dve, s - 1, (s - 1) % 2)
                dve_neighbours(link, EARLY + s - 1, SCR)
                dve_stage(dve, s, s % 2)
            dve_rest(dve, LAST_STAGE, 0)

            def S(i, a=0, b=NT):
                return st[:, i, a:b]

            dve.wait_ge(rowsum_ready, NT)
            dve.wait_ge(consts, 3)
            nc.vector.tensor_scalar(S(DEG), S(ROWSUM), 1.0, None, ALU.add).then_inc(deg_ready, 1)
            nc.vector.tensor_tensor(S(RS2), S(ROWSUM), padone[:, :], ALU.add).then_inc(rs2_ready, 1)
            for c, (a, b) in enumerate(CHUNKS):
                dve.wait_ge(u_ready, nth(LAST_STAGE, c) + 1)
                link(nc.vector.tensor_tensor(X[:, a:b, :], X[:, a:b, :], U[:, a:b, :], ALU.add))
            dve_layernorm(dve, link, 1)
            dve.wait_ge(degi_ready, 1)
            for c, (a, b) in enumerate(CHUNKS):
                dve.wait_ge(h_ready, nth(1, c) + 1)
                for t in range(a, b):
                    nc.vector.tensor_scalar(XC[:, t, 0:D], H[:, t, :], S(DEGI, t, t + 1), None, ALU.mult)
                nc.vector.tensor_copy(XC[:, a:b, D:D + 1], S(DEGI, a, b).unsqueeze(2)).then_inc(ye_ready, 1)
            dve.wait_ge(rsq_ready, 1)
            link(nc.vector.tensor_scalar(S(T_A), S(R2), -1.0, 1.0, ALU.mult, ALU.add))
            link(nc.vector.reciprocal(S(T_B), S(T_A)))
            link(nc.vector.tensor_scalar(S(GAM), S(T_B), 2.0, GAMMA_MAX, ALU.mult, ALU.min))
            link(nc.vector.tensor_scalar(S(T_C), S(GAM), -1.0, None, ALU.add))
            link(nc.vector.tensor_tensor(S(GM), S(T_C), S(DEGI), ALU.mult))
            link(nc.vector.tensor_tensor(S(GD), S(GAM), S(DEGI), ALU.mult))
            dve.wait_ge(ye_ready, NC)
            for t in range(NT):
                dve.wait_ge(ragg_done, t + 1)
                nc.vector.tensor_tensor(NX[:, t, :], bank(t % 6, D + 1), XC[:, t, :], ALU.add).then_inc(ragg_evac, 1)
                dve.wait_ge(ragg_evac, t + 1)
                link(nc.vector.tensor_scalar(S(T_D, t, t + 1), NX[:, t, D:D + 1], S(GM, t, t + 1), None, ALU.mult))
                link(nc.vector.reciprocal(S(T_E, t, t + 1), S(T_D, t, t + 1)))
                nc.vector.tensor_scalar(U[:, t, :], NX[:, t, 0:D], S(T_E, t, t + 1), S(GD, t, t + 1),
                                        ALU.mult, ALU.mult).then_inc(row_ready, 1)
                if t == 1:
                    dve_neighbours(link, NT - 1, SCR)
            dve.wait_ge(pow_out, 1)
            link(nc.vector.tensor_scalar(S(NS), S(AN), EPS, ONE_EPS, ALU.max, ALU.min))
            link(nc.vector.tensor_scalar(S(T_A), S(NS), -1.0, 1.0, ALU.mult, ALU.add))
            link(nc.vector.tensor_scalar(S(T_B), S(NS), 1.0, None, ALU.add))
            nc.vector.tensor_tensor(S(T_C), S(T_A), S(T_B), ALU.mult).then_inc(pow_in, 1)
            dve.wait_ge(pow_out, 2)
            link(nc.vector.tensor_scalar(S(T_A), S(T_D), 1.0, None, ALU.add))
            link(nc.vector.reciprocal(S(T_B), S(T_A)))
            link(nc.vector.tensor_tensor(S(NN), S(AN), S(T_B), ALU.mult))
            link(nc.vector.tensor_scalar(S(NSB), S(NN), EPS, ONE_EPS, ALU.max, ALU.min))
            link(nc.vector.tensor_scalar(S(T_A), S(NSB), -1.0, 1.0, ALU.mult, ALU.add))
            link(nc.vector.reciprocal(S(T_C), S(T_A)))
            link(nc.vector.tensor_scalar(S(T_A), S(NSB), 1.0, None, ALU.add))
            nc.vector.tensor_tensor(S(QUO), S(T_A), S(T_C), ALU.mult).then_inc(q_ready, 1)
            dve.wait_ge(q_ready, 1)
            link(nc.vector.tensor_tensor(S(T_A), S(NSB), S(NSB), ALU.mult))
            link(nc.vector.tensor_scalar(S(SER), S(T_A), 1.0 / 17, None, ALU.mult))
            for k in (15, 13, 11, 9, 7, 5, 3):
                link(nc.vector.scalar_tensor_tensor(S(SER), S(SER), 1.0 / k, S(T_A), ALU.add, ALU.mult))
            link(nc.vector.tensor_scalar(S(SER), S(SER), 1.0, None, ALU.add))
            link(nc.vector.reciprocal(S(T_C), S(NSB)))
            link(nc.vector.tensor_scalar(mask[:, :], S(NSB), 0.25, None, ALU.is_lt))
            dve.wait_ge(ln_ready, 1)
            link(nc.vector.scalar_tensor_tensor(S(FAC), S(LNQ), 0.5, S(T_C), ALU.mult, ALU.mult))
            link(nc.vector.copy_predicated(S(FAC), mask[:, :], S(SER)))
            link(nc.vector.tensor_tensor(S(FAC), S(FAC), S(T_B), ALU.mult))
            for c, (a, b) in enumerate(CHUNKS):
                dve.wait_ge(prod_done, c + 1)
                for t in range(a, b):
                    ins = nc.vector.scalar_tensor_tensor(U[:, t, :], PS[:, c, (t - a) * D:(t - a + 1) * D],
                                                         S(FAC, t, t + 1), brow[:, 0, :], ALU.mult, ALU.add)
                link(ins)
                nc.vector.tensor_scalar(U[:, a:b, :], U[:, a:b, :], 0.0, None, ALU.max).then_inc(y_ready, 1)
            dve.wait_ge(pow_out, 3)
            nc.vector.tensor_scalar(S(NS), S(YN), EPS, None, ALU.max).then_inc(yn_ready, 1)
            dve.wait_ge(yn_ready, 1)
            link(nc.vector.reciprocal(S(T_A), S(NS)))
            dve.wait_ge(tanh_ready, 1)
            link(nc.vector.tensor_tensor(S(EF), S(TH), S(T_A), ALU.mult))
            for t in range(NT):
                ins = nc.vector.scalar_tensor_tensor(X[:, t, :], U[:, t, :], S(EF, t, t + 1), X[:, t, :],
                                                     ALU.mult, ALU.add)
            ins.then_inc(x_ready, 1)
            dve.wait_ge(x_ready, 1)

            dve_layernorm(dve, link, 2)
            dve.wait_ge(dl_ready, 1)
            for c, (a, b) in enumerate(CHUNKS):
                dve.wait_ge(h_ready, nth(2, c) + 1)
                for t in range(a, b):
                    ins = nc.vector.tensor_scalar(XC[:, t, 0:D], H[:, t, :], S(DL, t, t + 1), None, ALU.mult)
                ins.then_inc(ys_ready, 1)
            for c in range(NC):
                lo, hi = cols(c)
                dve.wait_ge(z_bias, c + 1)
                nc.vector.scalar_tensor_tensor(Z[:, lo:hi], Z[:, lo:hi], 0.1, Z[:, lo:hi],
                                               ALU.mult, ALU.max).then_inc(z_ready, 1)
                dve.wait_ge(z_ready, c + 1)
                nc.vector.tensor_scalar(T1[:, lo:hi], Z[:, lo:hi], 2.0, None, ALU.mult).then_inc(z2_ready, 1)

            for c in range(NC):
                lo, hi = cols(c)
                dve.wait_ge(sqb_evac, c + 1)
                nc.vector.tensor_tensor(SQ[TWO:TWO + 1, lo:hi], PS[TWO:TWO + 1, 3 + c, 0:hi - lo],
                                        SQ[TWO:TWO + 1, lo:hi].bitcast(F32), ALU.subtract).then_inc(sq_ready, 1)
            dve.wait_ge(nsq_evac, 1)
            for t in range(NT):
                key = PS[:, 3 * (t % 2):3 * (t % 2) + 3, :].rearrange("p b n -> p (b n)")[:, 0:N]
                dve.wait_ge(dist_done, t + 1)
                link(nc.vector.max(V8[:, t, :], key))
                nc.vector.max_index(I8[:, t, :], V8[:, t, :], key).then_inc(key_read, 1)
                link(nc.vector.tensor_scalar(S4[:, t, :], V8[:, t, 0:TOPK], S(NSQ, t, t + 1), 0.0, ALU.add, ALU.min))
                nc.vector.tensor_scalar(S4[:, t, :], S4[:, t, :], -1.0, 1e-10, ALU.mult, ALU.add).then_inc(d4_in, 1)
            dve.wait_ge(s4_ready, NT)
            nc.vector.tensor_tensor(S(DD2I), S(RS2), S(SSUM), ALU.add).then_inc(ssum_ready, 1)
            dve.wait_ge(dd_ready, 1)
            for c, (a, b) in enumerate(CHUNKS):
                for t in range(a, b):
                    ins = nc.vector.tensor_scalar(U[:, t, :], H[:, t, :], S(DD, t, t + 1), None, ALU.mult)
                ins.then_inc(yd_ready, 1)
            link(nc.vector.tensor_tensor(X[:, :, :], X[:, :, :], brow[:, 1:2, :].to_broadcast([P, NT, D]), ALU.add))
            for t in range(NT):
                dve.wait_ge(ragg_done, 2 * NT + t + 1)
                dve.wait_ge(near_here[t % 3], 16 * TOPK * (t // 3 + 1))
                nc.vector.scalar_tensor_tensor(XC[:, t, 0:D], G2[:, t % 3, 0, :], S4[:, t, 0:1], bank(t % 6, D),
                                               ALU.mult, ALU.add).then_inc(ragg_evac, 1)
                dve.wait_ge(ragg_evac, 2 * NT + t + 1)
                for k in range(1, TOPK):
                    ins = nc.vector.scalar_tensor_tensor(XC[:, t, 0:D], G2[:, t % 3, k, :], S4[:, t, k:k + 1],
                                                         XC[:, t, 0:D], ALU.mult, ALU.add)
                    if k < TOPK - 1:
                        link(ins)
                ins.then_inc(row_ready, 1)

            link(nc.vector.tensor_scalar(c16[:, :, :], WG[:, :, :], 0.0, None, ALU.is_gt))
            link(nc.vector.reduce_sum(S(T_A), c16[:, :, :], AX.X))
            dve.wait_ge(cnt_ready, NT)
            link(nc.vector.tensor_tensor(S(T_B), S(T_A), CNT[:, :], ALU.not_equal))
            link(nc.vector.reduce_sum(tally[:, 0:1], S(T_B), AX.X))
            link(nc.vector.tensor_copy(S(OVF).unsqueeze(2), c16[:, :, MAIN:MAIN + 1]))
            link(nc.vector.reduce_sum(tally[:, 1:2], S(OVF), AX.X))
            link(nc.vector.memset(S(CUM, 0, 1), 0.0))
            for t in range(NT - 1):
                link(nc.vector.tensor_tensor(S(CUM, t + 1, t + 2), S(CUM, t, t + 1), S(OVF, t, t + 1), ALU.add))
            nc.vector.tensor_copy(IGF[:, :, :], IG[:, :, :]).then_inc(plan_ready, 1)
            dve.wait_ge(plan_ready, 1)
            link(nc.vector.tensor_scalar(away[:, :, :], c16[:, :, 0:MAIN], -float(FAR), float(FAR), ALU.mult, ALU.add))
            link(nc.vector.tensor_tensor(away[:, :, :], away[:, :, :], IGF[:, :, 0:MAIN], ALU.add))
            link(nc.vector.tensor_copy(IGU[:, 0:NT, :], away[:, :, :]))
            dve.wait_ge(plan_done, 1)
            link(nc.vector.tensor_scalar(within[:, 0:1], PS[0:1, 7, 0:1], 0.5, None, ALU.is_lt))
            link(nc.vector.tensor_scalar(within[:, 1:2], PS[0:1, 7, 1:2], P + 0.5, None, ALU.is_lt))
            nc.vector.tensor_tensor(flag[:, :], within[:, 0:1], within[:, 1:2], ALU.mult).then_inc(flag_ready, 1)
            link(nc.vector.tensor_copy(S(POS), PS[:, 7, 16:16 + NT]))
            for t in range(NT):
                ins = nc.vector.tensor_scalar(OH[:, t, :], iota[:, :], S(POS, t, t + 1), S(OVF, t, t + 1),
                                              ALU.is_equal, ALU.mult)
            ins.then_inc(oh_ready, 1)
            for c, (a, b) in enumerate(CHUNKS):
                dve.wait_ge(prod_done, NC + c + 1)
                for t in range(a, b):
                    ins = nc.vector.scalar_tensor_tensor(X[:, t, :], PS[:, c, (t - a) * D:(t - a + 1) * D],
                                                         S(DD, t, t + 1), X[:, t, :], ALU.mult, ALU.add)
            ins.then_inc(x_ready, 1)
            dve.wait_ge(x_ready, 2)

            dve.wait_ge(over_done, 1)
            link(nc.vector.tensor_copy(WGO[:, 0:NBR], PS[:, 7, 64:64 + NBR]))
            link(nc.vector.tensor_scalar(away[:, 0, :], WGO[:, 0:MAIN], 0.0, float(FAR), ALU.is_le, ALU.mult))
            link(nc.vector.tensor_tensor(away[:, 0, :], away[:, 0, :], WGO[:, MAIN:NBR], ALU.add))
            nc.vector.tensor_copy(IGU[:, NT, :], away[:, 0, :]).then_inc(idx_ready, 1)
            dve_layernorm(dve, link, 3)
            dve.wait_ge(h_ready, NC * 4)
            for t in range(NT):
                row = JUNK[:, (t % 2) * TW:(t % 2 + 1) * TW]
                if t >= 2:
                    dve.wait_ge(tab3_written[t % 2], 16 * (t // 2))
                nc.vector.tensor_copy(row[:, HD:HD + D], H[:, t, :])
                dve.wait_ge(x2_done, t + 1)
                nc.vector.tensor_copy(row[:, 0:HD], bank(3 + t % 3)).then_inc(x2_evac, 1)
                nc.vector.tensor_copy(row[:, HD + D:TW], PS[:, 6, 8 * t + HEADS:8 * t + 2 * HEADS])
                nc.vector.tensor_copy(PQ[:, t, :], PS[:, 6, 8 * t:8 * t + HEADS]).then_inc(row3_ready, 1)
            dve.wait_ge(row3_ready, NT)
            dve.wait_ge(x1_evac, NT)
            sparse = dve.value_load(flag[0:1, 0:1], min_val=0, max_val=1)
            with dve.If(sparse > 0):
                dve.wait_ge(xo_done, 1)
                dve.wait_ge(oht_done, NC)
                link(nc.vector.tensor_copy(XO[:, :], bank(7)))
                link(nc.vector.tensor_copy(PO[:, :], PS[:, 6, 128:128 + HEADS]))

                def weigh(u):
                    T, g = unit(u)
                    w = WG[:, T, g * GS:(g + 1) * GS] if T < NT else WGO[:, g * GS:(g + 1) * GS]
                    dve.wait_ge(exp_ready, u + 1)
                    nc.vector.tensor_tensor(EW[:, T, g * GS:(g + 1) * GS, :],
                                            sc[:, u % 2, 2, :].rearrange("p (k h) -> p k h", h=HEADS),
                                            w.unsqueeze(2).to_broadcast([P, GS, HEADS]), ALU.mult).then_inc(ew_ready, 1)

                def finish(T):
                    link(nc.vector.reduce_sum(DEN[:, T, :], EW[:, T, :, :].rearrange("p k h -> p h k"), AX.X))
                    dve.wait_ge(num_done, T + 1)
                    link(nc.vector.tensor_tensor(DEN[:, T, :], DEN[:, T, :],
                                                 PS[:, 6 + T % 2, 256:256 + HEADS], ALU.add))
                    if T == NT - 1:
                        link(nc.vector.tensor_scalar(DEN[:, T, :], DEN[:, T, :], padone[:, T:T + 1], None, ALU.add))
                    link(nc.vector.reciprocal(DEN[:, T, :], DEN[:, T, :]))
                    nc.vector.tensor_tensor(NUM[:, T, :].rearrange("p (h d) -> p h d", d=D),
                                            bank(4 + T % 2).rearrange("p (h d) -> p h d", d=D),
                                            DEN[:, T, :].unsqueeze(2).to_broadcast([P, HEADS, D]),
                                            ALU.mult).then_inc(num_ready, 1)

                for u in range(UNITS):
                    T, g = unit(u)
                    G = GB[u % 3]
                    x1, p1 = (X1H[:, T, :], PQ[:, T, :]) if T < NT else (XO, PO[:, :])
                    s0, s1, s2 = (sc[:, u % 2, i, :].rearrange("p (k h) -> p k h", h=HEADS) for i in range(3))
                    dve.wait_ge(g_here[u % 3], 16 * GS * (u // 3 + 1))
                    nc.vector.tensor_tensor(s1, G[:, :, HD + D:TW], p1.unsqueeze(1).to_broadcast([P, GS, HEADS]), ALU.add)
                    link(nc.vector.tensor_tensor(TT[:, :, :], G[:, :, 0:HD],
                                                 x1.unsqueeze(1).to_broadcast([P, GS, HD]), ALU.add))
                    if u >= 1:
                        weigh(u - 1)
                    link(nc.vector.scalar_tensor_tensor(TT[:, :, :], TT[:, :, :], 0.0,
                                                        aB[:, :].unsqueeze(1).to_broadcast([P, GS, HD]),
                                                        ALU.max, ALU.mult))
                    link(nc.vector.reduce_sum(s0, TT[:, :, :].rearrange("p k (h d) -> p k h d", d=D), AX.X))
                    link(nc.vector.tensor_scalar(s0, s0, 1.0 - SLOPE, None, ALU.mult))
                    nc.vector.scalar_tensor_tensor(s2, s1, SLOPE, s0, ALU.mult, ALU.add).then_inc(score_ready, 1)
                    if u == 2:
                        dve.wait_ge(ew_ready, 2)
                        dve.wait_ge(tab3_written[0], 16 * ((NT + 1) // 2))
                        nc.vector.reduce_sum(DEN[:, NT, :], EW[:, NT, :, :].rearrange("p k h -> p h k"), AX.X)
                        dve.wait_ge(eg_used, 2 * GS)
                        nc.vector.tensor_copy(NO, bank(3)).then_inc(no_ready, 1)
                    if u >= 4 and u % 2 == 0:
                        dve.wait_ge(ew_ready, u - 1)
                        finish((u - 4) // 2)
                weigh(UNITS - 1)
                dve.wait_ge(ew_ready, UNITS)
                finish(NT - 1)
            with dve.Else():
                K = 6 + GS * HEADS

                def chain(ins, n, i):
                    ins.then_inc(f_self, 1)
                    dve.wait_ge(f_self, n * K + 2 + i)

                nc.vector.memset(NUM[:, :, :], 0.0).then_inc(f_self, 1)
                nc.vector.memset(DEN[:, :, :], 0.0).then_inc(f_self, 1)
                dve.wait_ge(f_self, 2)
                nc.vector.tensor_scalar(DEN[:, NT - 1, :], DEN[:, NT - 1, :], padone[:, NT - 1:NT], None, ALU.add)
                nc.vector.memset(EWF[:, :, :], 0.0).then_inc(f_used, 1)
                dve.wait_ge(f_used, 1)
                with dve.Fori(0, NT) as t:
                    with dve.Fori(0, NP // GS) as g:
                        n = t * (NP // GS) + g
                        s0, s1, s2 = (sc[:, 0, i, :].rearrange("p (k h) -> p k h", h=HEADS) for i in range(3))
                        dve.wait_ge(f_here, n * 16 + 16)
                        nc.vector.tensor_tensor(s1, Ga[:, :, HD + D:TW],
                                                PQ[:, bass.ds(t, 1), :].to_broadcast([P, GS, HEADS]), ALU.add)
                        chain(nc.vector.tensor_tensor(TT[:, :, :], Ga[:, :, 0:HD],
                                                      X1H[:, bass.ds(t, 1), :].to_broadcast([P, GS, HD]), ALU.add), n, 1)
                        chain(nc.vector.scalar_tensor_tensor(TT[:, :, :], TT[:, :, :], 0.0,
                                                             aB[:, :].unsqueeze(1).to_broadcast([P, GS, HD]),
                                                             ALU.max, ALU.mult), n, 2)
                        chain(nc.vector.reduce_sum(s0, TT[:, :, :].rearrange("p k (h d) -> p k h d", d=D), AX.X), n, 3)
                        chain(nc.vector.tensor_scalar(s0, s0, 1.0 - SLOPE, None, ALU.mult), n, 4)
                        nc.vector.scalar_tensor_tensor(s2, s1, SLOPE, s0, ALU.mult, ALU.add).then_inc(f_score, 1)
                        dve.wait_ge(f_exp, n + 1)
                        chain(nc.vector.tensor_tensor(EWF[:, :, :], s2,
                                                      A[:, bass.ds(t, 1), bass.ds(g * GS, GS)].rearrange("p o k -> p k o")
                                                      .to_broadcast([P, GS, HEADS]), ALU.mult), n, 5)
                        for k in range(GS):
                            for h in range(HEADS):
                                acc = NUM[:, bass.ds(t, 1), h * D:(h + 1) * D]
                                chain(nc.vector.scalar_tensor_tensor(acc, Ga[:, k:k + 1, HD:HD + D], EWF[:, k, h:h + 1],
                                                                     acc, ALU.mult, ALU.add), n, 6 + k * HEADS + h)
                        chain(nc.vector.reduce_sum(DENF[:, :], EWF[:, :, :].rearrange("p k h -> p h k"), AX.X), n, K)
                        nc.vector.tensor_tensor(DEN[:, bass.ds(t, 1), :], DEN[:, bass.ds(t, 1), :],
                                                DENF[:, :].unsqueeze(1), ALU.add).then_inc(f_used, 1)
                        dve.wait_ge(f_used, n + 2)
                nc.vector.reciprocal(DEN[:, 0:NT, :], DEN[:, 0:NT, :]).then_inc(f_used, 1)
                dve.wait_ge(f_used, NT * (NP // GS) + 2)
                for t in range(NT):
                    nc.vector.tensor_tensor(NUM[:, t, :].rearrange("p (h d) -> p h d", d=D),
                                            NUM[:, t, :].rearrange("p (h d) -> p h d", d=D),
                                            DEN[:, t, :].unsqueeze(2).to_broadcast([P, HEADS, D]),
                                            ALU.mult).then_inc(num_ready, 1)
            for t in range(NT):
                LR = LRS[t % 2]
                dve.wait_ge(lin_copied, t + 1)
                nc.vector.scalar_tensor_tensor(LR, LR, SLOPE, LR, ALU.mult, ALU.max).then_inc(lin_ready, 1)
                if t >= 1:
                    dve.wait_ge(fin_done, t)
                    nc.vector.tensor_tensor(X[:, t - 1, :], X[:, t - 1, :], bank(4 + (t - 1) % 2, D), ALU.add)\
                        .then_inc(out_ready, 1)
            dve.wait_ge(fin_done, NT)
            nc.vector.tensor_tensor(X[:, NT - 1, :], X[:, NT - 1, :], bank(4 + (NT - 1) % 2, D), ALU.add)\
                .then_inc(out_ready, 1)

        @block.gpsimd
        def _(pool):
            plink = Link(pool, pool_self)
            pool.memset(mhalf[:, :], -0.5).then_inc(consts, 1)
            plink(pool.memset(ident[:, :], 0.0))
            pool.affine_select(out=ident[:, :], in_=ident[:, :], compare_op=ALU.not_equal, fill=1.0,
                               base=0, pattern=[[-1, P]], channel_multiplier=1).then_inc(consts, 1)
            pool.wait_ge(consts, 2)
            for c in range(NC):
                pool_rstd(pool, 0, c)
            plink(pool.memset(phalf[:, :], 0.5))
            plink(pool.memset(negs[:, :], -1.0))
            plink(pool.memset(ones[:, :], 1.0))
            plink(pool.memset(iota[:, :], 0.0))
            plink(pool.memset(iota[0:1, :], 1.0))
            plink(pool.memset(iota[TWO:TWO + 1, :], 1.0))
            plink(pool.tensor_copy(OW[:, :], iota[:, :]))
            plink(pool.affine_select(out=ltri[:, :], in_=ones[:, :], compare_op=ALU.is_gt, fill=0.0,
                                     base=0, pattern=[[1, P]], channel_multiplier=-1))
            plink(pool.memset(padone[:, :], 0.0))
            plink(pool.affine_select(out=padone[:, :], in_=padone[:, :], compare_op=ALU.is_ge, fill=1.0,
                                     base=N - 1, pattern=[[-P, NT]], channel_multiplier=-1))
            pool.iota(iota[:, :], pattern=[[1, P]], base=0, channel_multiplier=0,
                      allow_small_or_imprecise_dtypes=True).then_inc(consts, 1)

            def power(dst, src, exponent, ready, value, said, n=NT):
                pool.wait_ge(ready, value)
                pool.tensor_tensor(dst, src, exponent[:, 0:n], ALU.pow).then_inc(said, 1)

            power(st[:, DEGI, :], st[:, DEG, :], mhalf, deg_ready, 1, degi_ready)
            power(st[:, DL, :], st[:, RS2, :], mhalf, rs2_ready, 1, dl_ready)
            for c in range(NC):
                pool_rstd(pool, 1, c)
            power(st[:, AN, :], st[:, AN2, :], phalf, n2_ready, 1, pow_out)
            power(st[:, T_D, :], st[:, T_C, :], phalf, pow_in, 1, pow_out)
            power(st[:, YN, :], st[:, YN2, :], phalf, yn2_ready, 1, pow_out)

            for c in range(NC):
                pool_rstd(pool, 2, c)
            for t in range(NT):
                power(S4[:, t, :], S4[:, t, :], phalf, d4_in, t + 1, d4_out, TOPK)
            power(st[:, DD, :], st[:, DD2I, :], mhalf, ssum_ready, 1, dd_ready)
            pool.wait_ge(tab2_written, 16 * NC)
            for t in range(NT):
                if t >= 3:
                    pool.wait_ge(row_ready, NT + t - 2)
                for k in range(TOPK):
                    pool.indirect_dma_start(G2[:, t % 3, k, :], None, TAB2[:, :],
                                            bass.IndirectOffsetOnAxis(ap=I8[:, t, k:k + 1], axis=0))\
                        .then_inc(near_here[t % 3], 16)

            for c in range(NC):
                pool_rstd(pool, 3, c)
            pool.wait_ge(flag_ready, 1)
            sparse = pool.value_load(flag[0:1, 0:1], min_val=0, max_val=1)
            with pool.If(sparse > 0):
                pool.wait_ge(x2_evac, NT)
                pool.wait_ge(x1_evac, NT)
                for G in GB:
                    pool.memset(G, 0.0).then_inc(g_clear, 1)
                pool.wait_ge(g_clear, 3)
                pool.wait_ge(idx_ready, 1)
                pool.wait_ge(tab3_written[0], 16 * ((NT + 1) // 2))
                pool.wait_ge(tab3_written[1], 16 * (NT // 2))
                for u in range(UNITS):
                    T, g = unit(u)
                    if u >= 3:
                        pool.wait_ge(eg_ready, GS * (u - 2))
                    for k in range(GS):
                        at = g * GS + k
                        pool.indirect_dma_start(GB[u % 3][:, k, :], None, TAB3[:, :],
                                                bass.IndirectOffsetOnAxis(ap=IGU[:, T, at:at + 1], axis=0),
                                                bounds_check=NP - 1, oob_is_err=False).then_inc(g_here[u % 3], 16)

        @block.tensor
        def _(pe):
            def transpose_tile(t):
                pe.wait_ge(ld_a[t], 16)
                for g, (a, b) in enumerate(CHUNKS):
                    if t > 0:
                        pe.wait_ge(tr_evac, nth(t - 1, g) + 1)
                    for j in range(a, b):
                        last = nc.tensor.transpose(PS[:, 3 + g, (j - a) * P:(j - a + 1) * P],
                                                   A[:, t, j * P:(j + 1) * P], ident[:, :])
                    last.then_inc(tr_done, 1)

            pe.wait_ge(consts, 2)
            pe.wait_ge(pads, 3)
            for t in range(0, 4):
                transpose_tile(t)
            pe.wait_ge(h_ready, NC)
            pe.wait_ge(tr_evac, 4 * NC)
            pe_agg(pe, 0, 0, 0, 0, NT, H)
            for t in range(4, 8):
                transpose_tile(t)
            pe.wait_ge(ld_w, 16 * N_WEIGHTS)
            pe_l1(pe, 0, 0, 0)
            pe.wait_ge(tr_evac, 8 * NC)
            pe_agg(pe, 0, 0, 1, 0, 5, H)
            pe_l2(pe, 0, 0, 0)
            pe_agg(pe, 0, 0, 1, 5, 8, H)
            for t in range(8, NT):
                transpose_tile(t)
            pe_l3(pe, 0, 0, 0)
            pe_agg(pe, 0, 0, 1, 8, NT, H)
            pe.wait_ge(tr_evac, NT * NC)
            pe_agg(pe, 0, 0, 2, 0, 5, H)
            pe_l1(pe, 0, 0, 1)
            pe_agg(pe, 0, 0, 2, 5, NT, H)
            with pe.Fori(0, ROUNDS - 1) as r:
                pe_stage(pe, 2 * r + 1, 1)
                pe_stage(pe, 2 * r + 2, 0)
            pe_rest(pe, LAST_STAGE, 0)

            def row_transpose(src, t, base):
                c = t // 4
                if t % 4 == 0 and base + c >= 2:
                    pe.wait_ge(rowT_evac, base + c - 1)
                ins = nc.tensor.transpose(PS[:, 6 + c % 2, (t % 4) * P:(t % 4 + 1) * P], src[:, t, :], ident[:, :])
                if t + 1 == CHUNKS[c][1]:
                    ins.then_inc(rowT_done, 1)

            def row_aggregate(src, n, base, t, ready, rbase):
                if base + t >= 6:
                    pe.wait_ge(ragg_evac, base + t - 5)
                for j in range(NT):
                    if t == 0 and j in (0, 4, 8):
                        pe.wait_ge(ready, rbase + j // 4 + 1)
                    last = nc.tensor.matmul(bank(t % 6, n), AT[:, j, t * P:(t + 1) * P], src[:, j, 0:n],
                                            start=(j == 0), stop=(j == NT - 1))
                last.then_inc(ragg_done, 1)

            def row_product(w, c, done):
                a, b = CHUNKS[c]
                for t in range(a, b):
                    last = nc.tensor.matmul(PS[:, c, (t - a) * D:(t - a + 1) * D], T2[:, t * P:(t + 1) * P],
                                            W12[:, w, :], start=True, stop=True)
                last.then_inc(done, 1)

            for t in range(NT + 2):
                if t < NT:
                    row_aggregate(XC, D + 1, 0, t, ye_ready, 0)
                if t >= 2:
                    if t == 2:
                        pe.wait_ge(l3_sum, nth(LAST_STAGE, 2) + 1)
                    pe.wait_ge(row_ready, t - 1)
                    row_transpose(U, t - 2, 0)
            pe.wait_ge(ragg_evac, NT)
            for c in range(NC):
                pe.wait_ge(rowT_evac, c + 1)
                row_product(0, c, prod_done)

            for t in range(NT + 2):
                if t < NT:
                    row_aggregate(XC, D, NT, t, ys_ready, 0)
                if t >= 2:
                    pe.wait_ge(ragg_evac, NT + t - 1)
                    row_transpose(U, t - 2, NC)
            for c in range(NC):
                lo, hi = cols(c)
                pe.wait_ge(rowT_evac, NC + c + 1)
                nc.tensor.matmul(bank(c, hi - lo), W12[:, 1, :], T2[:, lo:hi], start=True, stop=True).then_inc(z_done, 1)
            for c in range(NC):
                lo, hi = cols(c)
                pe.wait_ge(zsq_ready, c + 1)
                nc.tensor.matmul(bank(3 + c, hi - lo), negs[:, :], T2[:, lo:hi], start=True, stop=True).then_inc(sqb_done, 1)
            for t in range(NT):
                ins = nc.tensor.matmul(PS[:, 6, t:t + 1], T2[:, t * P:(t + 1) * P], negs[:, 0:1], start=True, stop=True)
            ins.then_inc(nsq_done, 1)
            pe.wait_ge(z2_ready, NC)
            for t in range(NT):
                if t == 0:
                    pe.wait_ge(z_bias, NC)
                    pe.wait_ge(sq_ready, NC)
                elif t >= 2:
                    pe.wait_ge(key_read, t - 1)
                for c in range(NC):
                    lo, hi = cols(c)
                    hi = min(hi, N)
                    b = bank(3 * (t % 2) + c, hi - lo)
                    nc.tensor.matmul(b, Z[:, t * P:(t + 1) * P], T1[:, lo:hi], start=True, stop=False)
                    ins = nc.tensor.matmul(b, OW[0:TWO + 1, :], SQ[0:TWO + 1, lo:hi], start=False, stop=True)
                ins.then_inc(dist_done, 1)
            pe.wait_ge(key_read, NT)
            for t in range(NT + 2):
                if t < NT:
                    row_aggregate(U, D, 2 * NT, t, yd_ready, 0)
                if t >= 2:
                    pe.wait_ge(row_ready, NT + t - 1)
                    row_transpose(XC[:, :, 0:D], t - 2, 2 * NC)
            pe.wait_ge(ragg_evac, 3 * NT)
            pe.wait_ge(rowT_evac, 2 * NC + 2)
            pe.wait_ge(plan_ready, 1)
            nc.tensor.matmul(PS[:, 7, 0:2], ones[:, :], tally[:, :], start=True, stop=True)
            nc.tensor.matmul(PS[:, 7, 16:16 + NT], ltri[:, :], st[:, OVF, :], start=True, stop=False)
            nc.tensor.matmul(PS[:, 7, 16:16 + NT], ones[:, :], st[:, CUM, :], start=False, stop=True)\
                .then_inc(plan_done, 1)
            for c in range(NC):
                pe.wait_ge(rowT_evac, 2 * NC + c + 1)
                row_product(2, c, prod_done)
            pe.wait_ge(oh_ready, 1)
            for o, src in ((64, WG), (64 + MAIN, IGF)):
                for t in range(NT):
                    ins = nc.tensor.matmul(PS[:, 7, o:o + MAIN], OH[:, t, :], src[:, t, MAIN:NBR],
                                           start=(t == 0), stop=(t == NT - 1))
            ins.then_inc(over_done, 1)

            for t in range(NT):
                if t in (0, 4, 8):
                    pe.wait_ge(h_ready, nth(3, t // 4) + 1)
                if t == 4:
                    pe.wait_ge(idx_ready, 1)
                row_transpose(H, t, 3 * NC)
            pe.wait_ge(rowT_evac, 4 * NC)
            for h in range(HEADS):
                ins = nc.tensor.transpose(PS[:, 7, h * D:(h + 1) * D], WL[:, h, :], ident[:, :])
            ins.then_inc(wl_done, 1)
            for t in range(NT):
                nc.tensor.matmul(PS[:, 6, 8 * t:8 * t + 8], T2[:, t * P:(t + 1) * P],
                                 WPQ[:, :, :].rearrange("p i h -> p (i h)"), start=True, stop=True)
            pe.wait_ge(x_ready, 2)
            for t in range(NT):
                if t >= 3:
                    pe.wait_ge(x1_evac, t - 2)
                nc.tensor.matmul(bank(t % 3), T2[:, t * P:(t + 1) * P], GW[:, 0, :], start=True, stop=True).then_inc(x1_done, 1)
                if t >= 3:
                    pe.wait_ge(x2_evac, t - 2)
                nc.tensor.matmul(bank(3 + t % 3), T2[:, t * P:(t + 1) * P], GW[:, 1, :], start=True, stop=True).then_inc(x2_done, 1)
            pe.wait_ge(x1_evac, NT)
            pe.wait_ge(row3_ready, NT)
            pe.wait_ge(wl_evac, 1)
            sparse = pe.value_load(flag[0:1, 0:1], min_val=0, max_val=1)
            with pe.If(sparse > 0):
                for t in range(NT):
                    nc.tensor.matmul(bank(7), OH[:, t, :], X1H[:, t, :], start=(t == 0), stop=(t == NT - 1))
                for t in range(NT):
                    ins = nc.tensor.matmul(PS[:, 6, 128:128 + HEADS], OH[:, t, :], PQ[:, t, :],
                                           start=(t == 0), stop=(t == NT - 1))
                ins.then_inc(xo_done, 1)
                for c, (a, b) in enumerate(CHUNKS):
                    for t in range(a, b):
                        ins = nc.tensor.transpose(PS[:, c, (t - a) * P:(t - a + 1) * P], OH[:, t, :], ident[:, :])
                    ins.then_inc(oht_done, 1)
                for u in range(UNITS):
                    T, g = unit(u)
                    b = 3 if T == NT else 4 + T % 2
                    if T < NT and g == 0 and T >= 2:
                        pe.wait_ge(num_ready, T - 1)
                    for k in range(GS):
                        pe.wait_ge(eg_ready, GS * u + k + 1)
                        ins = nc.tensor.matmul(bank(b), ident[:, :], EG[:, k % 2, :], start=(g == 0 and k == 0),
                                               stop=(T == NT and g == 1 and k == GS - 1))
                        ins.then_inc(eg_used, 1)
                    if T < NT and g == 1:
                        if T == 0:
                            pe.wait_ge(no_ready, 1)
                            pe.wait_ge(oht_evac, NC)
                        nc.tensor.matmul(bank(b), OHT[:, T, :], NO, start=False, stop=True)
                        nc.tensor.matmul(PS[:, 6 + T % 2, 256:256 + HEADS], OHT[:, T, :], DEN[:, NT, :],
                                         start=True, stop=True).then_inc(num_done, 1)
            for t in range(NT + 2):
                if t < NT:
                    pe.wait_ge(num_ready, t + 1)
                    if t >= 2:
                        pe.wait_ge(numT_evac, t - 1)
                    for h in range(HEADS):
                        ins = nc.tensor.transpose(PS[:, t % 2, h * P:(h + 1) * P], NUM[:, t, h * D:(h + 1) * D], ident[:, :])
                    ins.then_inc(numT_done, 1)
                if 1 <= t <= NT:
                    i = t - 1
                    pe.wait_ge(numT_evac, i + 1)
                    if i >= 2:
                        pe.wait_ge(lin_copied, i - 1)
                    for h in range(HEADS):
                        ins = nc.tensor.matmul(PS[:, 2 + i % 2, h * P:(h + 1) * P], WLT[:, h, :],
                                               AGT[i % 2][:, h * P:(h + 1) * P], start=True, stop=True)
                    ins.then_inc(lin_done, 1)
                if t >= 2:
                    i = t - 2
                    pe.wait_ge(lin_ready, i + 1)
                    if i == 0:
                        pe.wait_ge(num_ready, NT)
                    if i >= 2:
                        pe.wait_ge(out_ready, i - 1)
                    for h in range(HEADS):
                        ins = nc.tensor.matmul(bank(4 + i % 2, D), LRS[i % 2][:, h * P:(h + 1) * P], WO[:, h, :],
                                               start=(h == 0), stop=(h == HEADS - 1))
                    ins.then_inc(fin_done, 1)


_INS = ['x', 'adj', 'L0_gnn_v_node_feats', 'L0_gnn_uv_W1', 'L0_gnn_uv_b1', 'L0_gnn_uv_W2', 'L0_gnn_uv_b2',
        'L0_gnn_uv_W3', 'L0_gnn_uv_b3', 'L0_gnn_vu_W1', 'L0_gnn_vu_b1', 'L0_gnn_vu_W2', 'L0_gnn_vu_b2',
        'L0_gnn_vu_W3', 'L0_gnn_vu_b3', 'L1_gnn_W', 'L1_gnn_b', 'L2_gnn_W1', 'L2_gnn_b1', 'L2_gnn_W2',
        'L2_gnn_b2', 'L3_gnn_w1', 'L3_gnn_w2', 'L3_gnn_a', 'L3_gnn_Wlin', 'L3_gnn_w']


def kernel(**inputs):
    import numpy as _np
    import concourse.bacc as _bacc
    from concourse import mybir as _mybir
    from concourse.bass_utils import run_bass_kernel_spmd as _run

    nc = _bacc.Bacc("TRN2", target_bir_lowering=False, num_devices=1)
    arrays, args = {}, []
    for name in _INS:
        a = _np.ascontiguousarray(inputs[name])
        arrays[f"in_{name}"] = a
        args.append(nc.dram_tensor(f"in_{name}", a.shape, _mybir.dt.from_np(a.dtype), kind="ExternalInput").ap())
    args.append(nc.dram_tensor("out_0", (N, D), _mybir.dt.float32, kind="ExternalOutput").ap())
    build(nc, *args)
    r = _run(nc, [arrays], core_ids=[0])
    return r.results[0]["out_0"]
```

```python
import concourse.bass as bass
from concourse import mybir
from contextlib import ExitStack

F32 = mybir.dt.float32
F32R = mybir.dt.float32r
I32 = mybir.dt.int32
U32 = mybir.dt.uint32
ALU = mybir.AluOpType
ACT = mybir.ActivationFunctionType
AX = mybir.AxisListType

N = 1354
D = 128
P = 128
NT = -(-N // P)
NP = NT * P
LAST = N - (NT - 1) * P
ROUNDS = 3
HEADS = 4
HD = HEADS * D
CHUNKS = [(0, 4), (4, 8), (8, NT)]
NC = len(CHUNKS)
TWO = 32
MAIN = 8
NBR = 2 * MAIN
TOPK = 4
GS = 4
ROWS = 8
NG = 5
NE = 4
TW = HD + D + HEADS
LAST_STAGE = 2 * ROUNDS - 2
N_WEIGHTS = 23
(MEAN, SSQ, VAR, RSTD, ROWSUM, DEG, DEGI, RS2, DL, R2, GAM, GM, GD, AN2, AN, NS, T_A, T_B, T_C, T_D, NN, NSB, SER,
 FAC, QUO, LNQ, YN2, YN, TH, EF, NSQ, SSUM, DD2I, DD, FB, OVF, CUM, POS, T_E) = range(39)
FAR = 1 << 20


EARLY = 6
SLOPE = 0.01
UNITS = 2 * (NT + 1)
EPS = 1e-7
ONE_EPS = 1.0 - 2.0 ** -23
GAMMA_MAX = 1e7


def on_pe(u):
    return 2 if u % 2 == 0 else 1


def sum_banks(u):
    return slice(0, on_pe(u)) if u % 2 == 0 else slice(2, 3)


class Link:

    def __init__(self, eng, sem):
        self.eng, self.sem, self.n = eng, sem, 0

    def mark(self, ins):
        self.n += 1
        ins.then_inc(self.sem, 1)
        return self.n

    def after(self, n):
        self.eng.wait_ge(self.sem, n)

    def __call__(self, ins):
        self.after(self.mark(ins))


def unit(u):
    return (NT if u < 2 else u // 2 - 1), u % 2


def wait_table(eng, written):
    for i in range(ROWS):
        eng.wait_ge(written[i], 16 * len(range(i, NT, ROWS)))


def cols(c):
    return CHUNKS[c][0] * P, CHUNKS[c][1] * P


def build(nc, x, adj, v_unused, uW1, ub1, uW2, ub2, uW3, ub3, vW1, vb1, vW2, vb2, vW3, vb3,
          hW, hb, lW1, lb1, lW2, lb2, gw1, gw2, ga, gWlin, gw, out):
    with ExitStack() as ctx:
        def sb(name, shape, dt=F32):
            return ctx.enter_context(nc.sbuf_tensor(name, shape, dt))

        def sem(name):
            return ctx.enter_context(nc.semaphore(name))

        A = sb("A", [P, NT, NP])
        AT = sb("AT", [P, NT, NP])
        X = sb("X", [P, NT, D])
        UH = sb("UH", [P, 2 * NT * D])
        U = UH[:, 0:NT * D].rearrange("p (t d) -> p t d", d=D)
        H = UH[:, NT * D:2 * NT * D].rearrange("p (t d) -> p t d", d=D)
        R = sb("R", [P, 3 * NP])
        Z = R[:, 0:NP]
        T1 = R[:, NP:2 * NP]
        T2 = R[:, 2 * NP:3 * NP]
        NX = R[:, 0:NT * (D + 1)].rearrange("p (t n) -> p t n", n=D + 1)
        XG = sb("XG", [P, NT * (D + 1) + 1 + 3 * TOPK * D])
        XC = XG[:, 0:NT * (D + 1)].rearrange("p (t n) -> p t n", n=D + 1)
        JUNK = sb("JUNK", [P, NP])
        SQ = sb("SQ", [P, NP], F32R)
        OW = sb("OW", [P, P], F32R)
        ident = sb("ident", [P, P])
        ones = sb("ones", [P, P])
        negs = sb("negs", [P, P])
        ltri = sb("ltri", [P, P])
        iota = sb("iota", [P, P])
        padone = sb("padone", [P, NT])
        mhalf = sb("mhalf", [P, NT * TOPK])
        phalf = sb("phalf", [P, NT * TOPK])
        W0 = sb("W0", [P, 6, D])
        bcol = sb("bcol", [P, 4 + 1])
        b3 = sb("b3", [P, 2, D])
        brow = sb("brow", [P, 2, D])
        W12 = sb("W12", [P, 3, D])
        GW = sb("GW", [P, 2, HD])
        aB = sb("aB", [P, HD])
        WPQ = sb("WPQ", [P, 2, HEADS])
        WL = sb("WL", [P, HEADS, D])
        WLT = sb("WLT", [P, HEADS, D])
        WO = sb("WO", [P, HEADS, D])
        WG = sb("WG", [P, NT, NBR])
        IG = sb("IG", [P, NT, NBR], U32)
        IGF = sb("IGF", [P, NT, NBR])
        IGU = sb("IGU", [P, NT + 1, MAIN], U32)
        WGO = sb("WGO", [P, NBR])
        CNT = sb("CNT", [P, NT])
        c16 = sb("c16", [P, NT, NBR])
        st = sb("st", [P, 48, NT])
        V8 = sb("V8", [P, NT, 8])
        I8 = sb("I8", [P, NT, 8], U32)
        S4 = sb("S4", [P, NT, TOPK])
        OH = JUNK[:, :].rearrange("p (t n) -> p t n", n=P)
        tally = sb("tally", [P, 2])
        within = sb("within", [1, 2])
        away = sb("away", [P, NT, MAIN])
        flag = sb("flag", [1, 1], I32)
        mask = sb("mask", [P, NT], I32)
        SCR = XG[:, NT * (D + 1) + 1:NT * (D + 1) + 1 + N]
        G2 = XG[:, NT * (D + 1) + 1:].rearrange("p (a k d) -> p a k d", a=3, d=D)
        flatAT = AT[:, :, :].rearrange("p t n -> p (t n)")
        o = 0
        X1H = flatAT[:, o:o + NT * HD].rearrange("p (t n) -> p t n", n=HD); o += NT * HD
        NUM = flatAT[:, o:o + NT * HD].rearrange("p (t n) -> p t n", n=HD); o += NT * HD
        Ga = flatAT[:, o:o + GS * TW].rearrange("p (k n) -> p k n", n=TW); o += GS * TW
        OHT = flatAT[:, o:o + NT * P].rearrange("p (t n) -> p t n", n=P); o += NT * P
        assert o <= NT * NP
        flatA = A[:, :, :].rearrange("p t n -> p (t n)")
        GB = [flatA[:, i * GS * TW:(i + 1) * GS * TW].rearrange("p (k n) -> p k n", n=TW) for i in range(NG)]
        EG = flatA[:, NG * GS * TW:NG * GS * TW + NE * HD].rearrange("p (k n) -> p k n", n=HD)
        TT = UH[:, 0:GS * HD].rearrange("p (k n) -> p k n", n=HD)
        XO = UH[:, GS * HD:GS * HD + HD]
        AGT = [UH[:, 0:HD], UH[:, HD:2 * HD]]
        LRS = [UH[:, 2 * HD:3 * HD], UH[:, 3 * HD:4 * HD]]
        ROW = flatAT[:, NT * HD:NT * HD + ROWS * TW].rearrange("p (k n) -> p k n", n=TW)
        HO = T1[:, 0:P]
        NO = JUNK[:, 0:HD]
        PQ = sb("PQ", [P, NT, HEADS])
        PO = sb("PO", [P, HEADS])
        DEN = sb("DEN", [P, NT + 1, HEADS])
        sc = sb("sc", [P, 2, 3, GS * HEADS])
        EW = sb("EW", [P, NT + 1, MAIN, HEADS])
        EWF = sb("EWF", [P, GS, HEADS])
        DENF = sb("DENF", [P, HEADS])

        TAB2 = nc.dram_tensor("tab2", [NP, D], F32, kind="Internal").ap()
        TAB3 = nc.dram_tensor("tab3", [NP, TW], F32, kind="Internal").ap()

        PS = ctx.enter_context(nc.psum_tensor("PS", [P, 8, 512], F32))

        def bank(b, n=512):
            return PS[:, b, 0:n]

        ld_x, ld_w, ld_a = sem("ld_x"), sem("ld_w"), [sem(f"ld_a{t}") for t in range(NT)]
        pads, consts = sem("pads"), sem("consts")
        dve_self, act_self, pool_self = sem("dve_self"), sem("act_self"), sem("pool_self")
        st_out = sem("st_out")
        tr_done, tr_evac = sem("tr_done"), sem("tr_evac")
        u_ready = sem("u_ready")
        agg_done, agg_evac = sem("agg_done"), sem("agg_evac")
        l1_done, l1_bias, l1_act = sem("l1_done"), sem("l1_bias"), sem("l1_act")
        l2_done, l2_bias, l2_act = sem("l2_done"), sem("l2_bias"), sem("l2_act")
        l3_done, l3_sum = sem("l3_done"), sem("l3_sum")
        rowsum_ready = sem("rowsum_ready")
        ln_centred, ln_squared, ln_var, ln_rstd, h_ready = (sem("ln_centred"), sem("ln_squared"), sem("ln_var"),
                                                            sem("ln_rstd"), sem("h_ready"))
        deg_ready, degi_ready, dl_ready = sem("deg_ready"), sem("degi_ready"), sem("dl_ready")
        rsq_ready, ye_ready = sem("rsq_ready"), sem("ye_ready")
        ragg_done, ragg_evac = sem("ragg_done"), sem("ragg_evac")
        row_ready, rowT_done, rowT_evac = sem("row_ready"), sem("rowT_done"), sem("rowT_evac")
        n2_ready, pow_in, pow_out = sem("n2_ready"), sem("pow_in"), sem("pow_out")
        q_ready, ln_ready, prod_done = sem("q_ready"), sem("ln_ready"), sem("prod_done")
        y_ready, yn2_ready, yn_ready, tanh_ready = sem("y_ready"), sem("yn2_ready"), sem("yn_ready"), sem("tanh_ready")
        x_ready = sem("x_ready")
        rs2_ready, ys_ready = sem("rs2_ready"), sem("ys_ready")
        z_done, z_bias, z_ready, z2_ready, zsq_ready = (sem("z_done"), sem("z_bias"), sem("z_ready"), sem("z2_ready"),
                                                        sem("zsq_ready"))
        sqb_done, sqb_evac, nsq_done, nsq_evac = sem("sqb_done"), sem("sqb_evac"), sem("nsq_done"), sem("nsq_evac")
        sq_ready, dist_done, key_read = sem("sq_ready"), sem("dist_done"), sem("key_read")
        d4_in, d4_out, s4_ready, ssum_ready, dd_ready = (sem("d4_in"), sem("d4_out"), sem("s4_ready"),
                                                         sem("ssum_ready"), sem("dd_ready"))
        yd_ready, tab2_written, cnt_ready = sem("yd_ready"), sem("tab2_written"), sem("cnt_ready")
        cnt_sign = sem("cnt_sign")
        near_here = [sem(f"near_here{i}") for i in range(3)]
        plan_ready, plan_done, flag_ready, oh_ready, over_done = (sem("plan_ready"), sem("plan_done"),
                                                                  sem("flag_ready"), sem("oh_ready"), sem("over_done"))
        idx_ready = sem("idx_ready")
        wl_done, wl_evac = sem("wl_done"), sem("wl_evac")
        x1_done, x1_evac, x2_done, x2_evac, row3_ready = (sem("x1_done"), sem("x1_evac"), sem("x2_done"),
                                                          sem("x2_evac"), sem("row3_ready"))
        tab3_written = [sem(f"tab3_written{i}") for i in range(ROWS)]
        oht_done, oht_evac, xo_done = sem("oht_done"), sem("oht_evac"), sem("xo_done")
        ho_done, ho_evac = sem("ho_done"), sem("ho_evac")
        sums_ready, sums_used, xo_read = sem("sums_ready"), sem("sums_used"), sem("xo_read")
        g_here = [sem(f"g_here{i}") for i in range(NG)]
        score_ready, exp_ready, ew_ready = sem("score_ready"), sem("exp_ready"), sem("ew_ready")
        eg_ready, eg_used = sem("eg_ready"), sem("eg_used")
        no_ready, num_done = sem("no_ready"), sem("num_done")
        f_used, f_here, f_self, f_score, f_tanh, f_exp = (sem("f_used"), sem("f_here"), sem("f_self"), sem("f_score"),
                                                          sem("f_tanh"), sem("f_exp"))
        num_ready = sem("num_ready")
        numT_done, numT_evac, lin_done, lin_copied, lin_ready, fin_done, out_ready = (
            sem("numT_done"), sem("numT_evac"), sem("lin_done"), sem("lin_copied"), sem("lin_ready"), sem("fin_done"),
            sem("out_ready"))
        block = ctx.enter_context(nc.Block())

        def nth(s, c):
            return NC * s + c

        def pe_agg(pe, s, kind, c, j0, j1, src):
            lo, hi = cols(c)
            for j in range(j0, j1):
                if src is U and j in (0, 4, 8):
                    pe.wait_ge(u_ready, nth(s - 1, j // 4) + 1)
                last = nc.tensor.matmul(bank(3 * kind + c, hi - lo), src[:, j, :], AT[:, j, lo:hi],
                                        start=(j == 0), stop=(j == NT - 1))
            if j1 == NT:
                last.then_inc(agg_done, 1)

        def pe_l1(pe, s, kind, c):
            lo, hi = cols(c)
            pe.wait_ge(agg_evac, nth(s, c) + 1)
            if not (isinstance(s, int) and s == 0 and c == 0):
                pe.wait_ge(l1_bias, nth(s, c))
            nc.tensor.matmul(bank(6, hi - lo), W0[:, 3 * kind, :], Z[:, lo:hi],
                             start=True, stop=True).then_inc(l1_done, 1)

        def pe_l2(pe, s, kind, c):
            lo, hi = cols(c)
            pe.wait_ge(l1_act, nth(s, c) + 1)
            if not (isinstance(s, int) and s == 0 and c == 0):
                pe.wait_ge(l2_bias, nth(s, c))
            nc.tensor.matmul(bank(7, hi - lo), W0[:, 3 * kind + 1, :], T1[:, lo:hi],
                             start=True, stop=True).then_inc(l2_done, 1)

        def pe_l3(pe, s, kind, c):
            pe.wait_ge(l2_act, nth(s, c) + 1)
            a, b = CHUNKS[c]
            for t in range(a, b):
                last = nc.tensor.matmul(PS[:, 3 * kind + c, (t - a) * D:(t - a + 1) * D],
                                        T2[:, t * P:(t + 1) * P], W0[:, 3 * kind + 2, :],
                                        start=True, stop=True)
            last.then_inc(l3_done, 1)

        def act_agg(act, s, kind, c):
            lo, hi = cols(c)
            act.wait_ge(agg_done, nth(s, c) + 1)
            nc.scalar.activation(Z[:, lo:hi], bank(3 * kind + c, hi - lo), ACT.Copy).then_inc(agg_evac, 1)

        def act_bias(act, s, kind, c, layer):
            lo, hi = cols(c)
            done, said, dst = (l1_done, l1_bias, T1) if layer == 1 else (l2_done, l2_bias, T2)
            act.wait_ge(done, nth(s, c) + 1)
            nc.scalar.activation(dst[:, lo:hi], bank(5 + layer, hi - lo), ACT.Identity,
                                 bias=bcol[:, 2 * kind + layer - 1:2 * kind + layer]).then_inc(said, 1)

        def dve_leaky(dve, s, c, layer):
            lo, hi = cols(c)
            given, said, dst = (l1_bias, l1_act, T1) if layer == 1 else (l2_bias, l2_act, T2)
            dve.wait_ge(given, nth(s, c) + 1)
            nc.vector.scalar_tensor_tensor(dst[:, lo:hi], dst[:, lo:hi], 0.01, dst[:, lo:hi],
                                           ALU.mult, ALU.max).then_inc(said, 1)

        def dve_l3(dve, s, kind, c):
            a, b = CHUNKS[c]
            dve.wait_ge(l3_done, nth(s, c) + 1)
            nc.vector.tensor_tensor(XC[:, a:b, 0:D],
                                    bank(3 * kind + c, (b - a) * D).rearrange("p (t d) -> p t d", d=D),
                                    b3[:, kind:kind + 1, :].to_broadcast([P, b - a, D]),
                                    ALU.add).then_inc(l3_sum, 1)
            dve.wait_ge(l3_sum, nth(s, c) + 1)
            nc.vector.scalar_tensor_tensor(U[:, a:b, :], XC[:, a:b, 0:D], 0.01, XC[:, a:b, 0:D],
                                           ALU.mult, ALU.max).then_inc(u_ready, 1)

        def pe_stage(pe, s, kind):
            k = 1 - kind
            pe_agg(pe, s, kind, 0, 0, 1, U)
            pe_l2(pe, s - 1, k, 1)
            pe_agg(pe, s, kind, 0, 1, 2, U)
            pe_l1(pe, s - 1, k, 2)
            pe_agg(pe, s, kind, 0, 2, 3, U)
            pe_l3(pe, s - 1, k, 1)
            pe_agg(pe, s, kind, 0, 3, 4, U)
            pe_l2(pe, s - 1, k, 2)
            pe_agg(pe, s, kind, 1, 0, 3, U)
            pe_l3(pe, s - 1, k, 2)
            pe_agg(pe, s, kind, 1, 3, 4, U)
            pe_agg(pe, s, kind, 0, 4, 8, U)
            pe_agg(pe, s, kind, 1, 4, 8, U)
            pe_agg(pe, s, kind, 0, 8, NT, U)
            pe_agg(pe, s, kind, 2, 0, 4, U)
            pe_l1(pe, s, kind, 0)
            pe_agg(pe, s, kind, 2, 4, 8, U)
            pe_l2(pe, s, kind, 0)
            pe_agg(pe, s, kind, 1, 8, NT, U)
            pe_l3(pe, s, kind, 0)
            pe_agg(pe, s, kind, 2, 8, NT, U)
            pe_l1(pe, s, kind, 1)

        def pe_rest(pe, s, kind):
            pe_l2(pe, s, kind, 1)
            pe_l1(pe, s, kind, 2)
            pe_l3(pe, s, kind, 1)
            pe_l2(pe, s, kind, 2)
            pe_l3(pe, s, kind, 2)

        def act_rest(act, s, kind):
            act_bias(act, s, kind, 1, 2)
            act_bias(act, s, kind, 2, 1)
            act_bias(act, s, kind, 2, 2)

        def act_stage(act, s, kind):
            act_agg(act, s, kind, 0)
            act_bias(act, s, kind, 0, 1)
            act_bias(act, s, kind, 0, 2)
            act_agg(act, s, kind, 1)
            act_agg(act, s, kind, 2)
            act_bias(act, s, kind, 1, 1)

        def dve_rest(dve, s, kind):
            dve_leaky(dve, s, 1, 2)
            dve_leaky(dve, s, 2, 1)
            dve_l3(dve, s, kind, 1)
            dve_leaky(dve, s, 2, 2)
            dve_l3(dve, s, kind, 2)

        def dve_stage(dve, s, kind):
            dve_leaky(dve, s, 0, 1)
            dve_leaky(dve, s, 0, 2)
            dve_l3(dve, s, kind, 0)
            dve_leaky(dve, s, 1, 1)

        def dve_center(link, l, c):
            a, b = CHUNKS[c]
            link(nc.vector.reduce_sum(st[:, MEAN, a:b], X[:, a:b, :], AX.X))
            link(nc.vector.tensor_scalar(st[:, MEAN, a:b], st[:, MEAN, a:b], 1.0 / D, None, ALU.mult))
            nc.vector.tensor_tensor(XC[:, a:b, 0:D], X[:, a:b, :],
                                    st[:, MEAN, a:b].unsqueeze(2).to_broadcast([P, b - a, D]),
                                    ALU.subtract).then_inc(ln_centred, 1)

        def act_square(act, l, c):
            a, b = CHUNKS[c]
            act.wait_ge(ln_centred, nth(l, c) + 1)
            for t in range(a, b):
                last = nc.scalar.activation((Z if l == 3 else JUNK)[:, t * D:(t + 1) * D], XC[:, t, 0:D], ACT.Square,
                                            accum_out=st[:, SSQ, t:t + 1])
            last.then_inc(ln_squared, 1)

        def dve_var(dve, l, c):
            a, b = CHUNKS[c]
            dve.wait_ge(ln_squared, nth(l, c) + 1)
            nc.vector.tensor_scalar(st[:, VAR, a:b], st[:, SSQ, a:b], 1.0 / D, 1e-5, ALU.mult,
                                    ALU.add).then_inc(ln_var, 1)

        def pool_rstd(pool, l, c):
            a, b = CHUNKS[c]
            pool.wait_ge(ln_var, nth(l, c) + 1)
            pool.tensor_tensor(st[:, RSTD, a:b], st[:, VAR, a:b], mhalf[:, a:b], ALU.pow).then_inc(ln_rstd, 1)

        def dve_norm(dve, l, c):
            a, b = CHUNKS[c]
            dve.wait_ge(ln_rstd, nth(l, c) + 1)
            for t in range(a, b):
                last = nc.vector.tensor_scalar(H[:, t, :], XC[:, t, 0:D], st[:, RSTD, t:t + 1], 0.0,
                                               ALU.mult, ALU.max)
            last.then_inc(h_ready, 1)

        def dve_layernorm(dve, link, l, before=None, after=None):
            def begin(c):
                if before:
                    before(c)
                dve_center(link, l, c)

            def end(c):
                dve_norm(dve, l, c)
                if after:
                    after(c)

            begin(0)
            begin(1)
            dve_var(dve, l, 0)
            begin(2)
            dve_var(dve, l, 1)
            end(0)
            dve_var(dve, l, 2)
            end(1)
            end(2)

        def dve_neighbours(link, t, scratch):
            link(nc.vector.max(WG[:, t, 0:8], A[:, t, 0:N]))
            link(nc.vector.max_index(IG[:, t, 0:8], WG[:, t, 0:8], A[:, t, 0:N]))
            link(nc.vector.match_replace(scratch, WG[:, t, 0:8], A[:, t, 0:N], 0.0))
            link(nc.vector.max(WG[:, t, 8:16], scratch))
            link(nc.vector.max_index(IG[:, t, 8:16], WG[:, t, 8:16], scratch))

        def act_count(act, t):
            at = slice(t, t + 1) if isinstance(t, int) else bass.ds(t, 1)
            nc.scalar.activation(JUNK[:, :].unsqueeze(1), A[:, at, :], ACT.Sign).then_inc(cnt_sign, 1)
            act.wait_ge(cnt_sign, t + 1)
            nc.scalar.activation(JUNK[:, :], JUNK[:, :], ACT.Square,
                                 accum_out=CNT[:, at]).then_inc(cnt_ready, 1)
            act.wait_ge(cnt_ready, t + 1)

        @block.sync
        def _(sp):
            def rows(t):
                return P if t < NT - 1 else LAST

            full = NT - 1
            sp.dma_start(X[:, 0:full, :], x[0:full * P, :].rearrange("(t p) d -> p t d", p=P)).then_inc(ld_x, 16)
            sp.wait_ge(pads, 2)
            sp.dma_start(X[0:LAST, full, :], x[full * P:N, :]).then_inc(ld_x, 16)
            def load_tiles(a, b):
                for t in range(a, b):
                    sp.dma_start(A[0:rows(t), t, 0:N], adj[t * P:t * P + rows(t), :]).then_inc(ld_a[t], 16)

            load_tiles(0, 4)
            for i, w in enumerate((uW1, uW2, uW3, vW1, vW2, vW3)):
                sp.dma_start(W0[:, i, :], w).then_inc(ld_w, 16)
            for i, b in enumerate((ub1, ub2, vb1, vb2, lb1)):
                sp.dma_start(bcol[:, i:i + 1], b.rearrange("(p o) -> p o", o=1)).then_inc(ld_w, 16)
            for i, b in enumerate((ub3, vb3)):
                sp.dma_start(b3[:, i, :], b.rearrange("(o d) -> o d", o=1).to_broadcast([P, D])).then_inc(ld_w, 16)
            load_tiles(4, NT)
            for i, b in enumerate((hb, lb2)):
                sp.dma_start(brow[:, i, :], b.rearrange("(o d) -> o d", o=1).to_broadcast([P, D])).then_inc(ld_w, 16)
            for i, w in enumerate((hW, lW1, lW2)):
                sp.dma_start(W12[:, i, :], w).then_inc(ld_w, 16)
            for i, w in enumerate((gw1, gw2)):
                sp.dma_start(GW[:, i, :].rearrange("p (h d) -> p h d", d=D),
                              w.rearrange("h p d -> p h d")).then_inc(ld_w, 16)
            sp.dma_start(aB[:, :], ga.rearrange("(o h) d -> o (h d)", o=1).to_broadcast([P, HD])).then_inc(ld_w, 16)
            sp.dma_start(WL[:, :, :], gWlin.rearrange("h p d -> p h d")).then_inc(ld_w, 16)
            sp.dma_start(WO[:, :, :], gw.rearrange("(h p) d -> p h d", p=P)).then_inc(ld_w, 16)
            for c, (a, b) in enumerate(CHUNKS):
                sp.wait_ge(yd_ready, c + 1)
                sp.dma_start(TAB2[a * P:b * P, :].rearrange("(t p) d -> p t d", p=P), U[:, a:b, :])\
                  .then_inc(tab2_written, 16)
            for t in range(NT):
                sp.wait_ge(row3_ready, t + 1)
                sp.dma_start(TAB3[t * P:(t + 1) * P, :], ROW[:, t % ROWS, :]).then_inc(tab3_written[t % ROWS], 16)
            sp.wait_ge(flag_ready, 1)
            sparse = sp.value_load(flag[0:1, 0:1], min_val=0, max_val=1)
            with sp.If(sparse < 1):
                wait_table(sp, tab3_written)
                with sp.Fori(0, NT) as t:
                    with sp.Fori(0, NP // GS) as g:
                        sp.wait_ge(f_used, t * (NP // GS) + g + 1)
                        sp.dma_start(Ga[:, :, :],
                                     TAB3[bass.ds(g * GS, GS), :].rearrange("(o k) n -> o k n", o=1)
                                     .to_broadcast([P, GS, TW])).then_inc(f_here, 16)
            for t in range(NT):
                n = P if t < NT - 1 else LAST
                sp.wait_ge(out_ready, t + 1)
                sp.dma_start(out[t * P:t * P + n, :], X[0:n, t, :]).then_inc(st_out, 16)
            sp.wait_ge(st_out, 16 * NT)

        @block.scalar
        def _(act):
            alink = Link(act, act_self)
            for c in range(NC):
                act_square(act, 0, c)

            def transposed(t):
                for g, (a, b) in enumerate(CHUNKS):
                    act.wait_ge(tr_done, nth(t, g) + 1)
                    nc.scalar.activation(AT[:, a:b, t * P:(t + 1) * P],
                                         bank(3 + g, (b - a) * P).rearrange("p (j i) -> p j i", i=P),
                                         ACT.Copy).then_inc(tr_evac, 1)

            def rowsum(t):
                act.wait_ge(ld_a[t], 16)
                act.wait_ge(pads, 3)
                if t > 0:
                    act.wait_ge(rowsum_ready, t)
                nc.scalar.activation(JUNK[:, :], A[:, t, :], ACT.Copy,
                                     accum_out=st[:, ROWSUM, t:t + 1]).then_inc(rowsum_ready, 1)

            for t in range(0, 4):
                transposed(t)
            for t in range(4, 8):
                transposed(t)
                rowsum(t - 4)
            act.wait_ge(ld_w, 16 * N_WEIGHTS)
            act_agg(act, 0, 0, 0)
            act_bias(act, 0, 0, 0, 1)
            act_bias(act, 0, 0, 0, 2)
            for t in range(8, NT):
                transposed(t)
                rowsum(t - 4)
            act_agg(act, 0, 0, 1)
            act_bias(act, 0, 0, 1, 1)
            act_agg(act, 0, 0, 2)

            def fill(s):
                act.wait_ge(rowsum_ready, s + 7)
                nc.scalar.activation(JUNK[:, :].unsqueeze(1), A[:, bass.ds(s + 7, 1), :], ACT.Copy,
                                     accum_out=st[:, ROWSUM, bass.ds(s + 7, 1)]).then_inc(rowsum_ready, 1)
                act.wait_ge(rowsum_ready, s + 8)
                act_count(act, 2 * s)
                act_count(act, 2 * s + 1)

            with act.Fori(0, ROUNDS - 1) as r:
                act_rest(act, 2 * r, 0)
                fill(2 * r)
                act_stage(act, 2 * r + 1, 1)
                act_rest(act, 2 * r + 1, 1)
                fill(2 * r + 1)
                act_stage(act, 2 * r + 2, 0)
            act_rest(act, LAST_STAGE, 0)

            def squares(dst, src, ready, base, said):
                for t in range(NT):
                    if t in (0, 4, 8):
                        act.wait_ge(ready, base + t // 4 + 1)
                    ins = nc.scalar.activation(JUNK[:, t * D:(t + 1) * D], src[:, t, :], ACT.Square,
                                               accum_out=st[:, dst, t:t + 1])
                    if t in (3, 7, NT - 1):
                        ins.then_inc(said, 1)

            def row_transposed(base, c):
                lo, hi = cols(c)
                act.wait_ge(rowT_done, base + c + 1)
                nc.scalar.activation(T2[:, lo:hi], bank(6 + c % 2, hi - lo), ACT.Copy).then_inc(rowT_evac, 1)

            act.wait_ge(wl_done, 1)
            nc.scalar.activation(WLT[:, :, :].rearrange("p h d -> p (h d)"), bank(7), ACT.Copy).then_inc(wl_evac, 1)
            act.wait_ge(rowsum_ready, NT)
            for c in range(NC):
                act_square(act, 1, c)
            squares(R2, H, h_ready, NC, rsq_ready)
            act.wait_ge(rsq_ready, NC)
            for t in range(NT):
                act.wait_ge(row_ready, t + 1)
                last = nc.scalar.activation(JUNK[:, t * D:(t + 1) * D], U[:, t, :], ACT.Square,
                                            accum_out=st[:, AN2, t:t + 1])
                if t in (3, 7, NT - 1):
                    last.then_inc(n2_ready, 1)
                if t in (1, 5, 9):
                    last.then_inc(act_self, 1)
                    alink.n += 1
                    act.wait_ge(act_self, alink.n)
                    act_count(act, 8 + t // 4)
                if t in (5, 9):
                    row_transposed(0, (t - 5) // 4)
            row_transposed(0, 2)
            act.wait_ge(q_ready, 1)
            nc.scalar.activation(st[:, LNQ, :], st[:, QUO, :], ACT.Ln).then_inc(ln_ready, 1)
            act.wait_ge(n2_ready, NC)
            squares(YN2, U, y_ready, 0, yn2_ready)
            act.wait_ge(yn_ready, 1)
            nc.scalar.activation(st[:, TH, :], st[:, NS, :], ACT.Tanh).then_inc(tanh_ready, 1)

            act.wait_ge(yn2_ready, NC)
            for c in range(NC):
                act_square(act, 2, c)
            for t in range(NT):
                act.wait_ge(ragg_done, NT + t + 1)
                nc.scalar.activation(U[:, t, :], bank(t % 6, D), ACT.Copy,
                                     scale=st[:, DL, t:t + 1]).then_inc(ragg_evac, 1)
                if t in (5, 9):
                    row_transposed(NC, (t - 5) // 4)
            row_transposed(NC, 2)
            for c in range(NC):
                lo, hi = cols(c)
                act.wait_ge(z_done, c + 1)
                nc.scalar.activation(Z[:, lo:hi], bank(c, hi - lo), ACT.Identity, bias=bcol[:, 4:5]).then_inc(z_bias, 1)
            for c in range(NC):
                lo, hi = cols(c)
                act.wait_ge(z_ready, c + 1)
                nc.scalar.activation(T2[:, lo:hi], Z[:, lo:hi], ACT.Square).then_inc(zsq_ready, 1)
            for c in range(NC):
                lo, hi = cols(c)
                act.wait_ge(sqb_done, c + 1)
                nc.scalar.activation(SQ[:, lo:hi], bank(3 + c, hi - lo), ACT.Copy).then_inc(sqb_evac, 1)
            act.wait_ge(nsq_done, 1)
            nc.scalar.activation(st[:, NSQ, :], bank(6, NT), ACT.Copy).then_inc(nsq_evac, 1)
            for t in range(NT):
                act.wait_ge(d4_out, t + 1)
                nc.scalar.activation(S4[:, t, :], S4[:, t, :], ACT.Exp, scale=-0.5,
                                     accum_out=st[:, SSUM, t:t + 1]).then_inc(s4_ready, 1)
            for c in range(NC):
                row_transposed(2 * NC, c)
                if c < NC - 1:
                    act_square(act, 3, c)

            for c, (a, b) in enumerate(CHUNKS):
                act.wait_ge(oht_done, c + 1)
                nc.scalar.activation(OHT[:, a:b, :].rearrange("p t n -> p (t n)"), bank(3 + c, (b - a) * P),
                                     ACT.Copy).then_inc(oht_evac, 1)
            act_square(act, 3, NC - 1)
            for c in range(NC):
                row_transposed(3 * NC, c)
            act.wait_ge(ho_done, 1)
            nc.scalar.activation(HO, bank(7, P), ACT.Copy).then_inc(ho_evac, 1)
            for t in range(NT):
                act.wait_ge(x1_done, t + 1)
                nc.scalar.activation(X1H[:, t, :], bank(t % 3), ACT.Copy).then_inc(x1_evac, 1)
            act.wait_ge(flag_ready, 1)
            sparse = act.value_load(flag[0:1, 0:1], min_val=0, max_val=1)
            with act.If(sparse > 0):
                def blend(u):
                    T, g = unit(u)
                    act.wait_ge(ew_ready, u + 1)
                    for k in range(GS):
                        if GS * u + k >= NE:
                            act.wait_ge(eg_used, GS * u + k - NE + 1)
                        for h in range(HEADS):
                            ins = nc.scalar.activation(EG[:, k % NE, h * D:(h + 1) * D], GB[u % NG][:, k, HD:HD + D],
                                                       ACT.Copy, scale=EW[:, T, g * GS + k, h:h + 1])
                        ins.then_inc(eg_ready, 1)

                for u in range(UNITS):
                    s2 = sc[:, u % 2, 2, :]
                    if u >= 1:
                        blend(u - 1)
                    act.wait_ge(score_ready, u + 1)
                    alink(nc.scalar.activation(s2, s2, ACT.Tanh, scale=0.125))
                    nc.scalar.activation(s2, s2, ACT.Exp, scale=8.0).then_inc(exp_ready, 1)
                blend(UNITS - 1)
            with act.Else():
                with act.Fori(0, NT * (NP // GS)) as n:
                    s2 = sc[:, 0, 2, :]
                    act.wait_ge(f_score, n + 1)
                    nc.scalar.activation(s2, s2, ACT.Tanh, scale=0.125).then_inc(f_tanh, 1)
                    act.wait_ge(f_tanh, n + 1)
                    nc.scalar.activation(s2, s2, ACT.Exp, scale=8.0).then_inc(f_exp, 1)
            for t in range(NT + 1):
                if t < NT:
                    act.wait_ge(numT_done, t + 1)
                    nc.scalar.activation(AGT[t % 2], bank(t % 2), ACT.Copy).then_inc(numT_evac, 1)
                if t >= 1:
                    act.wait_ge(lin_done, t)
                    nc.scalar.activation(LRS[(t - 1) % 2], bank(2 + (t - 1) % 2), ACT.Copy).then_inc(lin_copied, 1)

        @block.vector
        def _(dve):
            link = Link(dve, dve_self)
            nc.vector.memset(X[64:P, NT - 1, :], 0.0).then_inc(pads, 1)
            nc.vector.memset(A[64:P, NT - 1, 0:N], 0.0).then_inc(pads, 1)
            nc.vector.memset(A[:, :, N:NP], 0.0).then_inc(pads, 1)
            dve.wait_ge(ld_x, 32)
            dve_layernorm(dve, link, 0)
            for t in range(2):
                dve.wait_ge(ld_a[t], 16)
                dve_neighbours(link, t, SCR)
            dve.wait_ge(ld_w, 16 * N_WEIGHTS)
            for i in range(2):
                link(nc.vector.tensor_tensor(SCR[:, 0:HD], GW[:, i, :], aB[:, :], ALU.mult))
                link(nc.vector.reduce_sum(WPQ[:, i, :], SCR[:, 0:HD].rearrange("p (h d) -> p h d", d=D), AX.X))
            dve_neighbours(link, 2, SCR)
            dve_leaky(dve, 0, 0, 1)
            dve_neighbours(link, 3, SCR)
            dve_leaky(dve, 0, 0, 2)
            dve_neighbours(link, 4, SCR)
            dve_l3(dve, 0, 0, 0)
            dve_neighbours(link, 5, SCR)
            dve_leaky(dve, 0, 1, 1)
            for s in range(1, LAST_STAGE + 1):
                dve_rest(dve, s - 1, (s - 1) % 2)
                dve_neighbours(link, EARLY + s - 1, SCR)
                dve_stage(dve, s, s % 2)
            dve_rest(dve, LAST_STAGE, 0)

            def S(i, a=0, b=NT):
                return st[:, i, a:b]

            dve.wait_ge(rowsum_ready, NT)
            dve.wait_ge(consts, 3)
            nc.vector.tensor_scalar(S(DEG), S(ROWSUM), 1.0, None, ALU.add).then_inc(deg_ready, 1)
            nc.vector.tensor_tensor(S(RS2), S(ROWSUM), padone[:, :], ALU.add).then_inc(rs2_ready, 1)

            def add_layer0(c):
                a, b = CHUNKS[c]
                dve.wait_ge(u_ready, nth(LAST_STAGE, c) + 1)
                link(nc.vector.tensor_tensor(X[:, a:b, :], X[:, a:b, :], U[:, a:b, :], ALU.add))

            def by_degree(c):
                a, b = CHUNKS[c]
                if c == 0:
                    dve.wait_ge(degi_ready, 1)
                dve.wait_ge(h_ready, nth(1, c) + 1)
                for t in range(a, b):
                    nc.vector.tensor_scalar(XC[:, t, 0:D], H[:, t, :], S(DEGI, t, t + 1), None, ALU.mult)
                nc.vector.tensor_copy(XC[:, a:b, D:D + 1], S(DEGI, a, b).unsqueeze(2)).then_inc(ye_ready, 1)

            dve_layernorm(dve, link, 1, add_layer0, by_degree)
            dve.wait_ge(rsq_ready, NC)
            link(nc.vector.tensor_scalar(S(T_A), S(R2), -1.0, 1.0, ALU.mult, ALU.add))
            link(nc.vector.reciprocal(S(T_B), S(T_A)))
            link(nc.vector.tensor_scalar(S(GAM), S(T_B), 2.0, GAMMA_MAX, ALU.mult, ALU.min))
            link(nc.vector.tensor_scalar(S(T_C), S(GAM), -1.0, None, ALU.add))
            link(nc.vector.tensor_tensor(S(GM), S(T_C), S(DEGI), ALU.mult))
            link(nc.vector.tensor_tensor(S(GD), S(GAM), S(DEGI), ALU.mult))
            dve.wait_ge(ye_ready, NC)
            for t in range(NT):
                dve.wait_ge(ragg_done, t + 1)
                nc.vector.tensor_tensor(NX[:, t, :], bank(t % 6, D + 1), XC[:, t, :], ALU.add).then_inc(ragg_evac, 1)
                dve.wait_ge(ragg_evac, t + 1)
                link(nc.vector.tensor_scalar(S(T_D, t, t + 1), NX[:, t, D:D + 1], S(GM, t, t + 1), None, ALU.mult))
                link(nc.vector.reciprocal(S(T_E, t, t + 1), S(T_D, t, t + 1)))
                nc.vector.tensor_scalar(U[:, t, :], NX[:, t, 0:D], S(T_E, t, t + 1), S(GD, t, t + 1),
                                        ALU.mult, ALU.mult).then_inc(row_ready, 1)
                if t == 1:
                    dve_neighbours(link, NT - 1, SCR)
            dve.wait_ge(pow_out, NC)
            link(nc.vector.tensor_scalar(S(NS), S(AN), EPS, ONE_EPS, ALU.max, ALU.min))
            link(nc.vector.tensor_scalar(S(T_A), S(NS), -1.0, 1.0, ALU.mult, ALU.add))
            link(nc.vector.tensor_scalar(S(T_B), S(NS), 1.0, None, ALU.add))
            nc.vector.tensor_tensor(S(T_C), S(T_A), S(T_B), ALU.mult).then_inc(pow_in, 1)
            dve.wait_ge(pow_out, NC + 1)
            link(nc.vector.tensor_scalar(S(T_A), S(T_D), 1.0, None, ALU.add))
            link(nc.vector.reciprocal(S(T_B), S(T_A)))
            link(nc.vector.tensor_tensor(S(NN), S(AN), S(T_B), ALU.mult))
            link(nc.vector.tensor_scalar(S(NSB), S(NN), EPS, ONE_EPS, ALU.max, ALU.min))
            link(nc.vector.tensor_scalar(S(T_A), S(NSB), -1.0, 1.0, ALU.mult, ALU.add))
            link(nc.vector.reciprocal(S(T_C), S(T_A)))
            link(nc.vector.tensor_scalar(S(T_A), S(NSB), 1.0, None, ALU.add))
            nc.vector.tensor_tensor(S(QUO), S(T_A), S(T_C), ALU.mult).then_inc(q_ready, 1)
            dve.wait_ge(q_ready, 1)
            link(nc.vector.tensor_tensor(S(T_A), S(NSB), S(NSB), ALU.mult))
            link(nc.vector.tensor_scalar(S(SER), S(T_A), 1.0 / 17, None, ALU.mult))
            for k in (15, 13, 11, 9, 7, 5, 3):
                link(nc.vector.scalar_tensor_tensor(S(SER), S(SER), 1.0 / k, S(T_A), ALU.add, ALU.mult))
            link(nc.vector.tensor_scalar(S(SER), S(SER), 1.0, None, ALU.add))
            link(nc.vector.reciprocal(S(T_C), S(NSB)))
            link(nc.vector.tensor_scalar(mask[:, :], S(NSB), 0.25, None, ALU.is_lt))
            dve.wait_ge(ln_ready, 1)
            link(nc.vector.scalar_tensor_tensor(S(FAC), S(LNQ), 0.5, S(T_C), ALU.mult, ALU.mult))
            link(nc.vector.copy_predicated(S(FAC), mask[:, :], S(SER)))
            link(nc.vector.tensor_tensor(S(FAC), S(FAC), S(T_B), ALU.mult))
            for c, (a, b) in enumerate(CHUNKS):
                dve.wait_ge(prod_done, c + 1)
                for t in range(a, b):
                    ins = nc.vector.scalar_tensor_tensor(U[:, t, :], PS[:, c, (t - a) * D:(t - a + 1) * D],
                                                         S(FAC, t, t + 1), brow[:, 0, :], ALU.mult, ALU.add)
                link(ins)
                nc.vector.tensor_scalar(U[:, a:b, :], U[:, a:b, :], 0.0, None, ALU.max).then_inc(y_ready, 1)
            dve.wait_ge(pow_out, 2 * NC + 1)
            nc.vector.tensor_scalar(S(NS), S(YN), EPS, None, ALU.max).then_inc(yn_ready, 1)
            dve.wait_ge(yn_ready, 1)
            link(nc.vector.reciprocal(S(T_A), S(NS)))
            dve.wait_ge(tanh_ready, 1)
            link(nc.vector.tensor_tensor(S(EF), S(TH), S(T_A), ALU.mult))

            def add_layer1(c):
                a, b = CHUNKS[c]
                for t in range(a, b):
                    ins = nc.vector.scalar_tensor_tensor(X[:, t, :], U[:, t, :], S(EF, t, t + 1), X[:, t, :],
                                                         ALU.mult, ALU.add)
                ins.then_inc(x_ready, 1)
                dve.wait_ge(x_ready, c + 1)


            def by_root(c):
                a, b = CHUNKS[c]
                if c == 0:
                    dve.wait_ge(dl_ready, 1)
                dve.wait_ge(h_ready, nth(2, c) + 1)
                for t in range(a, b):
                    ins = nc.vector.tensor_scalar(XC[:, t, 0:D], H[:, t, :], S(DL, t, t + 1), None, ALU.mult)
                ins.then_inc(ys_ready, 1)

            dve_layernorm(dve, link, 2, add_layer1, by_root)
            link(nc.vector.tensor_scalar(c16[:, :, :], WG[:, :, :], 0.0, None, ALU.is_gt))
            link(nc.vector.reduce_sum(S(T_A), c16[:, :, :], AX.X))
            dve.wait_ge(cnt_ready, NT)
            link(nc.vector.tensor_tensor(S(T_B), S(T_A), CNT[:, :], ALU.not_equal))
            link(nc.vector.reduce_sum(tally[:, 0:1], S(T_B), AX.X))
            link(nc.vector.tensor_copy(S(OVF).unsqueeze(2), c16[:, :, MAIN:MAIN + 1]))
            link(nc.vector.reduce_sum(tally[:, 1:2], S(OVF), AX.X))
            link(nc.vector.memset(S(CUM, 0, 1), 0.0))
            for t in range(NT - 1):
                link(nc.vector.tensor_tensor(S(CUM, t + 1, t + 2), S(CUM, t, t + 1), S(OVF, t, t + 1), ALU.add))
            nc.vector.tensor_copy(IGF[:, :, :], IG[:, :, :]).then_inc(plan_ready, 1)
            dve.wait_ge(plan_ready, 1)
            link(nc.vector.tensor_scalar(away[:, :, :], c16[:, :, 0:MAIN], -float(FAR), float(FAR), ALU.mult, ALU.add))
            link(nc.vector.tensor_tensor(away[:, :, :], away[:, :, :], IGF[:, :, 0:MAIN], ALU.add))
            link(nc.vector.tensor_copy(IGU[:, 0:NT, :], away[:, :, :]))
            for c in range(NC):
                lo, hi = cols(c)
                dve.wait_ge(z_bias, c + 1)
                nc.vector.scalar_tensor_tensor(Z[:, lo:hi], Z[:, lo:hi], 0.1, Z[:, lo:hi],
                                               ALU.mult, ALU.max).then_inc(z_ready, 1)
                dve.wait_ge(z_ready, c + 1)
                nc.vector.tensor_scalar(T1[:, lo:hi], Z[:, lo:hi], 2.0, None, ALU.mult).then_inc(z2_ready, 1)

            for c in range(NC):
                lo, hi = cols(c)
                dve.wait_ge(sqb_evac, c + 1)
                nc.vector.tensor_tensor(SQ[TWO:TWO + 1, lo:hi], PS[TWO:TWO + 1, 3 + c, 0:hi - lo],
                                        SQ[TWO:TWO + 1, lo:hi].bitcast(F32), ALU.subtract).then_inc(sq_ready, 1)
            dve.wait_ge(nsq_evac, 1)
            for t in range(NT):
                key = PS[:, 3 * (t % 2):3 * (t % 2) + 3, :].rearrange("p b n -> p (b n)")[:, 0:N]
                dve.wait_ge(dist_done, t + 1)
                link(nc.vector.max(V8[:, t, :], key))
                nc.vector.max_index(I8[:, t, :], V8[:, t, :], key).then_inc(key_read, 1)
                link(nc.vector.tensor_scalar(S4[:, t, :], V8[:, t, 0:TOPK], S(NSQ, t, t + 1), 0.0, ALU.add, ALU.min))
                nc.vector.tensor_scalar(S4[:, t, :], S4[:, t, :], -1.0, 1e-10, ALU.mult, ALU.add).then_inc(d4_in, 1)
            dve.wait_ge(s4_ready, NT)
            nc.vector.tensor_tensor(S(DD2I), S(RS2), S(SSUM), ALU.add).then_inc(ssum_ready, 1)
            dve.wait_ge(dd_ready, 1)
            for c, (a, b) in enumerate(CHUNKS):
                for t in range(a, b):
                    ins = nc.vector.tensor_scalar(U[:, t, :], H[:, t, :], S(DD, t, t + 1), None, ALU.mult)
                ins.then_inc(yd_ready, 1)
            dve.wait_ge(plan_done, 1)
            link(nc.vector.tensor_scalar(within[:, 0:1], PS[0:1, 7, 0:1], 0.5, None, ALU.is_lt))
            link(nc.vector.tensor_scalar(within[:, 1:2], PS[0:1, 7, 1:2], P + 0.5, None, ALU.is_lt))
            nc.vector.tensor_tensor(flag[:, :], within[:, 0:1], within[:, 1:2], ALU.mult).then_inc(flag_ready, 1)
            link(nc.vector.tensor_copy(S(POS), PS[:, 7, 16:16 + NT]))
            for t in range(NT):
                ins = nc.vector.tensor_scalar(OH[:, t, :], iota[:, :], S(POS, t, t + 1), S(OVF, t, t + 1),
                                              ALU.is_equal, ALU.mult)
            ins.then_inc(oh_ready, 1)

            def residual(c):
                a, b = CHUNKS[c]
                dve.wait_ge(prod_done, NC + c + 1)
                for t in range(a, b):
                    ins = nc.vector.scalar_tensor_tensor(X[:, t, :], PS[:, c, (t - a) * D:(t - a + 1) * D],
                                                         S(DD, t, t + 1), X[:, t, :], ALU.mult, ALU.add)
                ins.then_inc(x_ready, 1)
                dve.wait_ge(x_ready, NC + c + 1)

            link(nc.vector.tensor_tensor(X[:, :, :], X[:, :, :], brow[:, 1:2, :].to_broadcast([P, NT, D]), ALU.add))
            for t in range(NT):
                dve.wait_ge(ragg_done, 2 * NT + t + 1)
                dve.wait_ge(near_here[t % 3], 16 * TOPK * (t // 3 + 1))
                nc.vector.scalar_tensor_tensor(XC[:, t, 0:D], G2[:, t % 3, 0, :], S4[:, t, 0:1], bank(3 + t % 3, D),
                                               ALU.mult, ALU.add).then_inc(ragg_evac, 1)
                dve.wait_ge(ragg_evac, 2 * NT + t + 1)
                for k in range(1, TOPK):
                    ins = nc.vector.scalar_tensor_tensor(XC[:, t, 0:D], G2[:, t % 3, k, :], S4[:, t, k:k + 1],
                                                         XC[:, t, 0:D], ALU.mult, ALU.add)
                    if k < TOPK - 1:
                        link(ins)
                ins.then_inc(row_ready, 1)
                if t == 3:
                    dve.wait_ge(over_done, 1)
                    link(nc.vector.tensor_copy(WGO[:, 0:NBR], PS[:, 7, 64:64 + NBR]))
                    link(nc.vector.tensor_scalar(away[:, 0, :], WGO[:, 0:MAIN], 0.0, float(FAR), ALU.is_le, ALU.mult))
                    link(nc.vector.tensor_tensor(away[:, 0, :], away[:, 0, :], WGO[:, MAIN:NBR], ALU.add))
                    nc.vector.tensor_copy(IGU[:, NT, :], away[:, 0, :]).then_inc(idx_ready, 1)
                if t in (5, 9):
                    residual((t - 5) // 4)
                    dve_center(link, 3, (t - 5) // 4)
                if t == 8:
                    dve_var(dve, 3, 0)
            dve_var(dve, 3, 1)
            for c in range(NC - 1):
                dve_norm(dve, 3, c)
            residual(NC - 1)
            dve_center(link, 3, NC - 1)
            dve_var(dve, 3, NC - 1)
            dve_norm(dve, 3, NC - 1)


            dve.wait_ge(h_ready, NC * 4)
            for t in range(NT):
                row = ROW[:, t % ROWS, :]
                if t >= ROWS:
                    dve.wait_ge(tab3_written[t % ROWS], 16 * (t // ROWS))
                nc.vector.tensor_copy(row[:, HD:HD + D], H[:, t, :])
                dve.wait_ge(x2_done, t + 1)
                nc.vector.tensor_copy(row[:, 0:HD], bank(3 + t % 3)).then_inc(x2_evac, 1)
                nc.vector.tensor_copy(row[:, HD + D:TW], PS[:, 6, 8 * t + HEADS:8 * t + 2 * HEADS])
                nc.vector.tensor_copy(PQ[:, t, :], PS[:, 6, 8 * t:8 * t + HEADS]).then_inc(row3_ready, 1)
            dve.wait_ge(row3_ready, NT)
            sparse = dve.value_load(flag[0:1, 0:1], min_val=0, max_val=1)
            with dve.If(sparse > 0):
                dve.wait_ge(xo_done, 1)
                link(nc.vector.tensor_copy(XO[:, :], bank(7)))
                nc.vector.tensor_copy(PO[:, :], PS[:, 6, 128:128 + HEADS]).then_inc(xo_read, 1)
                dve.wait_ge(xo_read, 1)

                def weigh(u):
                    T, g = unit(u)
                    w = WG[:, T, g * GS:(g + 1) * GS] if T < NT else WGO[:, g * GS:(g + 1) * GS]
                    dve.wait_ge(exp_ready, u + 1)
                    nc.vector.tensor_tensor(EW[:, T, g * GS:(g + 1) * GS, :],
                                            sc[:, u % 2, 2, :].rearrange("p (k h) -> p k h", h=HEADS),
                                            w.unsqueeze(2).to_broadcast([P, GS, HEADS]), ALU.mult).then_inc(ew_ready, 1)

                def den_sum(T):
                    dve.wait_ge(ew_ready, 2 * T + 4 if T < NT else 2)
                    return link.mark(nc.vector.reduce_sum(DEN[:, T, :], EW[:, T, :, :].rearrange("p k h -> p h k"), AX.X))

                def den_total(T, summed):
                    dve.wait_ge(num_done, T + 1)
                    link.after(summed)
                    n = link.mark(nc.vector.tensor_tensor(DEN[:, T, :], DEN[:, T, :],
                                                          PS[:, 6 + T % 2, 256:256 + HEADS], ALU.add))
                    if T == NT - 1:
                        link.after(n)
                        n = link.mark(nc.vector.tensor_scalar(DEN[:, T, :], DEN[:, T, :], padone[:, T:T + 1], None,
                                                              ALU.add))
                    return n

                def den_inverse(T, total):
                    link.after(total)
                    return link.mark(nc.vector.reciprocal(DEN[:, T, :], DEN[:, T, :]))

                def divide(T, inverse):
                    link.after(inverse)
                    nc.vector.tensor_tensor(NUM[:, T, :].rearrange("p (h d) -> p h d", d=D),
                                            bank(4 + T % 2).rearrange("p (h d) -> p h d", d=D),
                                            DEN[:, T, :].unsqueeze(2).to_broadcast([P, HEADS, D]),
                                            ALU.mult).then_inc(num_ready, 1)

                def relu_a(dst, src, n):
                    return nc.vector.scalar_tensor_tensor(dst, src, 0.0, aB[:, :].unsqueeze(1).to_broadcast([P, n, HD]),
                                                          ALU.max, ALU.mult)

                def total(u, a, b):
                    s0 = sc[:, u % 2, 0, a * HEADS:b * HEADS].rearrange("p (k h) -> p k h", h=HEADS)
                    return link.mark(nc.vector.reduce_sum(s0, TT[:, a:b, :].rearrange("p k (h d) -> p k h d", d=D), AX.X))

                link(nc.vector.tensor_scalar(aB[:, :], aB[:, :], 1.0 - SLOPE, None, ALU.mult))
                rest = summed = low = 0
                for u in range(UNITS):
                    T, g = unit(u)
                    n = on_pe(u)
                    G = GB[u % NG]
                    x1, p1 = (X1H[:, T, :], PQ[:, T, :]) if T < NT else (XO, PO[:, :])
                    s1, s2 = (sc[:, u % 2, i, :].rearrange("p (k h) -> p k h", h=HEADS) for i in (1, 2))
                    if u == 2:
                        dve.wait_ge(x1_evac, NT)
                    dve.wait_ge(g_here[u % NG], 16 * GS * (u // NG + 1))
                    link.mark(nc.vector.tensor_tensor(s1, G[:, :, HD + D:TW],
                                                      p1.unsqueeze(1).to_broadcast([P, GS, HEADS]), ALU.add))
                    if u >= 1:
                        link.after(rest)
                    rest = link.mark(nc.vector.tensor_tensor(TT[:, n:GS, :], G[:, n:GS, 0:HD],
                                                             x1.unsqueeze(1).to_broadcast([P, GS - n, HD]), ALU.add))
                    if u >= 6 and u % 2 == 0:
                        divide((u - 6) // 2, low)
                    dve.wait_ge(sums_ready, u + 1)
                    relu_a(TT[:, 0:n, :], PS[:, sum_banks(u), :], n).then_inc(sums_used, 1)
                    if u >= 1:
                        weigh(u - 1)
                    link.after(rest)
                    rest = link.mark(relu_a(TT[:, n:GS, :], TT[:, n:GS, :], GS - n))
                    if u >= 5 and u % 2 == 1:
                        summed = den_sum((u - 5) // 2)
                    dve.wait_ge(sums_used, u + 1)
                    total(u, 0, n)
                    link.after(rest)
                    rest = total(u, n, GS)
                    if u >= 5 and u % 2 == 1:
                        summed = den_total((u - 5) // 2, summed)
                    link.after(rest)
                    nc.vector.scalar_tensor_tensor(s2, s1, SLOPE, sc[:, u % 2, 0, :].rearrange("p (k h) -> p k h", h=HEADS),
                                                   ALU.mult, ALU.add).then_inc(score_ready, 1)
                    if u >= 5 and u % 2 == 1:
                        low = den_inverse((u - 5) // 2, summed)
                    if u == 3:
                        den_sum(NT)
                        dve.wait_ge(eg_used, 2 * GS)
                        nc.vector.tensor_copy(NO, bank(3)).then_inc(no_ready, 1)
                divide(NT - 2, low)
                weigh(UNITS - 1)
                summed = den_total(NT - 1, den_sum(NT - 1))
                divide(NT - 1, den_inverse(NT - 1, summed))
            with dve.Else():
                dve.wait_ge(x1_evac, NT)
                K = 6 + GS * HEADS

                def chain(ins, n, i):
                    ins.then_inc(f_self, 1)
                    dve.wait_ge(f_self, n * K + 2 + i)

                wait_table(dve, tab3_written)
                nc.vector.memset(NUM[:, :, :], 0.0).then_inc(f_self, 1)
                nc.vector.memset(DEN[:, :, :], 0.0).then_inc(f_self, 1)
                dve.wait_ge(f_self, 2)
                nc.vector.tensor_scalar(DEN[:, NT - 1, :], DEN[:, NT - 1, :], padone[:, NT - 1:NT], None, ALU.add)
                nc.vector.memset(EWF[:, :, :], 0.0).then_inc(f_used, 1)
                dve.wait_ge(f_used, 1)
                with dve.Fori(0, NT) as t:
                    with dve.Fori(0, NP // GS) as g:
                        n = t * (NP // GS) + g
                        s0, s1, s2 = (sc[:, 0, i, :].rearrange("p (k h) -> p k h", h=HEADS) for i in range(3))
                        dve.wait_ge(f_here, n * 16 + 16)
                        nc.vector.tensor_tensor(s1, Ga[:, :, HD + D:TW],
                                                PQ[:, bass.ds(t, 1), :].to_broadcast([P, GS, HEADS]), ALU.add)
                        chain(nc.vector.tensor_tensor(TT[:, :, :], Ga[:, :, 0:HD],
                                                      X1H[:, bass.ds(t, 1), :].to_broadcast([P, GS, HD]), ALU.add), n, 1)
                        chain(nc.vector.scalar_tensor_tensor(TT[:, :, :], TT[:, :, :], 0.0,
                                                             aB[:, :].unsqueeze(1).to_broadcast([P, GS, HD]),
                                                             ALU.max, ALU.mult), n, 2)
                        chain(nc.vector.reduce_sum(s0, TT[:, :, :].rearrange("p k (h d) -> p k h d", d=D), AX.X), n, 3)
                        chain(nc.vector.tensor_scalar(s0, s0, 1.0 - SLOPE, None, ALU.mult), n, 4)
                        nc.vector.scalar_tensor_tensor(s2, s1, SLOPE, s0, ALU.mult, ALU.add).then_inc(f_score, 1)
                        dve.wait_ge(f_exp, n + 1)
                        chain(nc.vector.tensor_tensor(EWF[:, :, :], s2,
                                                      A[:, bass.ds(t, 1), bass.ds(g * GS, GS)].rearrange("p o k -> p k o")
                                                      .to_broadcast([P, GS, HEADS]), ALU.mult), n, 5)
                        for k in range(GS):
                            for h in range(HEADS):
                                acc = NUM[:, bass.ds(t, 1), h * D:(h + 1) * D]
                                chain(nc.vector.scalar_tensor_tensor(acc, Ga[:, k:k + 1, HD:HD + D], EWF[:, k, h:h + 1],
                                                                     acc, ALU.mult, ALU.add), n, 6 + k * HEADS + h)
                        chain(nc.vector.reduce_sum(DENF[:, :], EWF[:, :, :].rearrange("p k h -> p h k"), AX.X), n, K)
                        nc.vector.tensor_tensor(DEN[:, bass.ds(t, 1), :], DEN[:, bass.ds(t, 1), :],
                                                DENF[:, :].unsqueeze(1), ALU.add).then_inc(f_used, 1)
                        dve.wait_ge(f_used, n + 2)
                nc.vector.reciprocal(DEN[:, 0:NT, :], DEN[:, 0:NT, :]).then_inc(f_used, 1)
                dve.wait_ge(f_used, NT * (NP // GS) + 2)
                for t in range(NT):
                    nc.vector.tensor_tensor(NUM[:, t, :].rearrange("p (h d) -> p h d", d=D),
                                            NUM[:, t, :].rearrange("p (h d) -> p h d", d=D),
                                            DEN[:, t, :].unsqueeze(2).to_broadcast([P, HEADS, D]),
                                            ALU.mult).then_inc(num_ready, 1)
            for t in range(NT):
                LR = LRS[t % 2]
                dve.wait_ge(lin_copied, t + 1)
                nc.vector.scalar_tensor_tensor(LR, LR, SLOPE, LR, ALU.mult, ALU.max).then_inc(lin_ready, 1)
                if t >= 1:
                    dve.wait_ge(fin_done, t)
                    nc.vector.tensor_tensor(X[:, t - 1, :], X[:, t - 1, :], bank(4 + (t - 1) % 2, D), ALU.add)\
                        .then_inc(out_ready, 1)
            dve.wait_ge(fin_done, NT)
            nc.vector.tensor_tensor(X[:, NT - 1, :], X[:, NT - 1, :], bank(4 + (NT - 1) % 2, D), ALU.add)\
                .then_inc(out_ready, 1)

        @block.gpsimd
        def _(pool):
            plink = Link(pool, pool_self)
            pool.memset(mhalf[:, :], -0.5).then_inc(consts, 1)
            plink(pool.memset(ident[:, :], 0.0))
            pool.affine_select(out=ident[:, :], in_=ident[:, :], compare_op=ALU.not_equal, fill=1.0,
                               base=0, pattern=[[-1, P]], channel_multiplier=1).then_inc(consts, 1)
            pool.wait_ge(consts, 2)
            for c in range(NC):
                pool_rstd(pool, 0, c)
            plink(pool.memset(phalf[:, :], 0.5))
            plink(pool.memset(negs[:, :], -1.0))
            plink(pool.memset(ones[:, :], 1.0))
            plink(pool.memset(iota[:, :], 0.0))
            plink(pool.memset(iota[0:1, :], 1.0))
            plink(pool.memset(iota[TWO:TWO + 1, :], 1.0))
            plink(pool.tensor_copy(OW[:, :], iota[:, :]))
            plink(pool.affine_select(out=ltri[:, :], in_=ones[:, :], compare_op=ALU.is_gt, fill=0.0,
                                     base=0, pattern=[[1, P]], channel_multiplier=-1))
            plink(pool.memset(padone[:, :], 0.0))
            plink(pool.affine_select(out=padone[:, :], in_=padone[:, :], compare_op=ALU.is_ge, fill=1.0,
                                     base=N - 1, pattern=[[-P, NT]], channel_multiplier=-1))
            pool.iota(iota[:, :], pattern=[[1, P]], base=0, channel_multiplier=0,
                      allow_small_or_imprecise_dtypes=True).then_inc(consts, 1)

            def power(dst, src, exponent, ready, value, said, n=NT):
                pool.wait_ge(ready, value)
                pool.tensor_tensor(dst, src, exponent[:, 0:n], ALU.pow).then_inc(said, 1)

            power(st[:, DEGI, :], st[:, DEG, :], mhalf, deg_ready, 1, degi_ready)
            power(st[:, DL, :], st[:, RS2, :], mhalf, rs2_ready, 1, dl_ready)
            for c in range(NC):
                pool_rstd(pool, 1, c)
            for c, (a, b) in enumerate(CHUNKS):
                power(st[:, AN, a:b], st[:, AN2, a:b], phalf, n2_ready, c + 1, pow_out, b - a)
            power(st[:, T_D, :], st[:, T_C, :], phalf, pow_in, 1, pow_out)
            for c, (a, b) in enumerate(CHUNKS):
                power(st[:, YN, a:b], st[:, YN2, a:b], phalf, yn2_ready, c + 1, pow_out, b - a)

            for c in range(NC):
                pool_rstd(pool, 2, c)
            for t in range(NT):
                power(S4[:, t, :], S4[:, t, :], phalf, d4_in, t + 1, d4_out, TOPK)
            power(st[:, DD, :], st[:, DD2I, :], mhalf, ssum_ready, 1, dd_ready)
            pool.wait_ge(tab2_written, 16 * NC)
            for t in range(NT):
                if t >= 3:
                    pool.wait_ge(row_ready, NT + t - 2)
                for k in range(TOPK):
                    pool.indirect_dma_start(G2[:, t % 3, k, :], None, TAB2[:, :],
                                            bass.IndirectOffsetOnAxis(ap=I8[:, t, k:k + 1], axis=0))\
                        .then_inc(near_here[t % 3], 16)

            for c in range(NC):
                pool_rstd(pool, 3, c)
            pool.wait_ge(flag_ready, 1)
            sparse = pool.value_load(flag[0:1, 0:1], min_val=0, max_val=1)
            with pool.If(sparse > 0):
                pool.wait_ge(idx_ready, 1)
                wait_table(pool, tab3_written)
                for u in range(UNITS):
                    T, g = unit(u)
                    if u >= NG:
                        pool.wait_ge(eg_ready, GS * (u - NG + 1))
                    for k in range(GS):
                        at = g * GS + k
                        pool.indirect_dma_start(GB[u % NG][:, k, :], None, TAB3[:, :],
                                                bass.IndirectOffsetOnAxis(ap=IGU[:, T, at:at + 1], axis=0),
                                                bounds_check=NP - 1, oob_is_err=False).then_inc(g_here[u % NG], 16)

        @block.tensor
        def _(pe):
            def transpose_tile(t):
                pe.wait_ge(ld_a[t], 16)
                for g, (a, b) in enumerate(CHUNKS):
                    if t > 0:
                        pe.wait_ge(tr_evac, nth(t - 1, g) + 1)
                    for j in range(a, b):
                        last = nc.tensor.transpose(PS[:, 3 + g, (j - a) * P:(j - a + 1) * P],
                                                   A[:, t, j * P:(j + 1) * P], ident[:, :])
                    last.then_inc(tr_done, 1)

            pe.wait_ge(consts, 2)
            pe.wait_ge(pads, 3)
            for t in range(0, 4):
                transpose_tile(t)
            pe.wait_ge(h_ready, NC)
            pe.wait_ge(tr_evac, 4 * NC)
            pe_agg(pe, 0, 0, 0, 0, NT, H)
            for t in range(4, 8):
                transpose_tile(t)
            pe.wait_ge(ld_w, 16 * N_WEIGHTS)
            pe_l1(pe, 0, 0, 0)
            pe.wait_ge(tr_evac, 8 * NC)
            pe_agg(pe, 0, 0, 1, 0, 5, H)
            pe_l2(pe, 0, 0, 0)
            pe_agg(pe, 0, 0, 1, 5, 8, H)
            for t in range(8, NT):
                transpose_tile(t)
            pe_l3(pe, 0, 0, 0)
            pe_agg(pe, 0, 0, 1, 8, NT, H)
            pe.wait_ge(tr_evac, NT * NC)
            pe_agg(pe, 0, 0, 2, 0, 5, H)
            pe_l1(pe, 0, 0, 1)
            pe_agg(pe, 0, 0, 2, 5, NT, H)
            with pe.Fori(0, ROUNDS - 1) as r:
                pe_stage(pe, 2 * r + 1, 1)
                pe_stage(pe, 2 * r + 2, 0)
            pe_rest(pe, LAST_STAGE, 0)

            def row_transpose(src, t, base):
                c = t // 4
                if t % 4 == 0 and base + c >= 2:
                    pe.wait_ge(rowT_evac, base + c - 1)
                ins = nc.tensor.transpose(PS[:, 6 + c % 2, (t % 4) * P:(t % 4 + 1) * P], src[:, t, :], ident[:, :])
                if t + 1 == CHUNKS[c][1]:
                    ins.then_inc(rowT_done, 1)

            def row_aggregate(src, n, base, t, ready, rbase):
                if base + t >= 6:
                    pe.wait_ge(ragg_evac, base + t - 5)
                for j in range(NT):
                    if t == 0 and j in (0, 4, 8):
                        pe.wait_ge(ready, rbase + j // 4 + 1)
                    last = nc.tensor.matmul(bank(t % 6, n), AT[:, j, t * P:(t + 1) * P], src[:, j, 0:n],
                                            start=(j == 0), stop=(j == NT - 1))
                last.then_inc(ragg_done, 1)

            def row_product(w, c, done):
                a, b = CHUNKS[c]
                for t in range(a, b):
                    last = nc.tensor.matmul(PS[:, c, (t - a) * D:(t - a + 1) * D], T2[:, t * P:(t + 1) * P],
                                            W12[:, w, :], start=True, stop=True)
                last.then_inc(done, 1)

            pe.wait_ge(l2_bias, nth(LAST_STAGE, 2) + 1)
            for h in range(HEADS):
                ins = nc.tensor.transpose(PS[:, 7, h * D:(h + 1) * D], WL[:, h, :], ident[:, :])
            ins.then_inc(wl_done, 1)
            for t in range(NT + 2):
                if t < NT:
                    row_aggregate(XC, D + 1, 0, t, ye_ready, 0)
                if t >= 2:
                    if t == 2:
                        pe.wait_ge(l3_sum, nth(LAST_STAGE, 2) + 1)
                    if t == 6:
                        pe.wait_ge(wl_evac, 1)
                    pe.wait_ge(row_ready, t - 1)
                    row_transpose(U, t - 2, 0)
            pe.wait_ge(ragg_evac, NT)
            for c in range(NC):
                pe.wait_ge(rowT_evac, c + 1)
                row_product(0, c, prod_done)

            for t in range(NT + 2):
                if t < NT:
                    row_aggregate(XC, D, NT, t, ys_ready, 0)
                if t >= 2:
                    pe.wait_ge(ragg_evac, NT + t - 1)
                    row_transpose(U, t - 2, NC)
            for c in range(NC):
                lo, hi = cols(c)
                pe.wait_ge(rowT_evac, NC + c + 1)
                nc.tensor.matmul(bank(c, hi - lo), W12[:, 1, :], T2[:, lo:hi], start=True, stop=True).then_inc(z_done, 1)
            for c in range(NC):
                lo, hi = cols(c)
                pe.wait_ge(zsq_ready, c + 1)
                nc.tensor.matmul(bank(3 + c, hi - lo), negs[:, :], T2[:, lo:hi], start=True, stop=True).then_inc(sqb_done, 1)
            for t in range(NT):
                ins = nc.tensor.matmul(PS[:, 6, t:t + 1], T2[:, t * P:(t + 1) * P], negs[:, 0:1], start=True, stop=True)
            ins.then_inc(nsq_done, 1)
            pe.wait_ge(rowT_evac, NC + 2)
            pe.wait_ge(plan_ready, 1)
            nc.tensor.matmul(PS[:, 7, 0:2], ones[:, :], tally[:, :], start=True, stop=True)
            nc.tensor.matmul(PS[:, 7, 16:16 + NT], ltri[:, :], st[:, OVF, :], start=True, stop=False)
            nc.tensor.matmul(PS[:, 7, 16:16 + NT], ones[:, :], st[:, CUM, :], start=False, stop=True)\
                .then_inc(plan_done, 1)
            pe.wait_ge(z2_ready, NC)
            for t in range(NT):
                if t == 0:
                    pe.wait_ge(z_bias, NC)
                    pe.wait_ge(sq_ready, NC)
                elif t >= 2:
                    pe.wait_ge(key_read, t - 1)
                for c in range(NC):
                    lo, hi = cols(c)
                    hi = min(hi, N)
                    b = bank(3 * (t % 2) + c, hi - lo)
                    nc.tensor.matmul(b, Z[:, t * P:(t + 1) * P], T1[:, lo:hi], start=True, stop=False)
                    ins = nc.tensor.matmul(b, OW[0:TWO + 1, :], SQ[0:TWO + 1, lo:hi], start=False, stop=True)
                ins.then_inc(dist_done, 1)
            pe.wait_ge(key_read, NT)
            for t in range(NT + 2):
                if t < NT:
                    if t >= 3:
                        pe.wait_ge(ragg_evac, 2 * NT + t - 2)
                    for j in range(NT):
                        if t == 0 and j in (0, 4, 8):
                            pe.wait_ge(yd_ready, j // 4 + 1)
                        ins = nc.tensor.matmul(bank(3 + t % 3, D), AT[:, j, t * P:(t + 1) * P], U[:, j, :],
                                               start=(j == 0), stop=(j == NT - 1))
                    ins.then_inc(ragg_done, 1)
                if t == 2:
                    pe.wait_ge(oh_ready, 1)
                    for o, src in ((64, WG), (64 + MAIN, IGF)):
                        for j in range(NT):
                            ins = nc.tensor.matmul(PS[:, 7, o:o + MAIN], OH[:, j, :], src[:, j, MAIN:NBR],
                                                   start=(j == 0), stop=(j == NT - 1))
                    ins.then_inc(over_done, 1)
                if t >= 2:
                    if t == 6:
                        pe.wait_ge(idx_ready, 1)
                    pe.wait_ge(row_ready, NT + t - 1)
                    row_transpose(XC[:, :, 0:D], t - 2, 2 * NC)
                if t in (6, 10):
                    c = (t - 6) // 4
                    pe.wait_ge(rowT_evac, 2 * NC + c + 1)
                    row_product(2, c, prod_done)
            pe.wait_ge(ragg_evac, 3 * NT)
            for c, (a, b) in enumerate(CHUNKS):
                for t in range(a, b):
                    ins = nc.tensor.transpose(PS[:, 3 + c, (t - a) * P:(t - a + 1) * P], OH[:, t, :], ident[:, :])
                ins.then_inc(oht_done, 1)
            pe.wait_ge(rowT_evac, 3 * NC)
            row_product(2, NC - 1, prod_done)

            for t in range(NT):
                if t in (0, 4, 8):
                    pe.wait_ge(h_ready, nth(3, t // 4) + 1)
                row_transpose(H, t, 3 * NC)
            pe.wait_ge(rowT_evac, 3 * NC + 2)
            for t in range(NT):
                ins = nc.tensor.matmul(bank(7, P), H[:, t, :], OH[:, t, :], start=(t == 0), stop=(t == NT - 1))
            ins.then_inc(ho_done, 1)
            pe.wait_ge(rowT_evac, 4 * NC)
            for t in range(NT):
                nc.tensor.matmul(PS[:, 6, 8 * t:8 * t + 8], T2[:, t * P:(t + 1) * P],
                                 WPQ[:, :, :].rearrange("p i h -> p (i h)"), start=True, stop=True)
            pe.wait_ge(ho_evac, 1)
            nc.tensor.matmul(PS[:, 6, 128:128 + HEADS], HO, WPQ[:, 0, :], start=True, stop=True)
            pe.wait_ge(oht_evac, NC)
            for t in range(NT):
                if t >= 3:
                    pe.wait_ge(x2_evac, t - 2)
                nc.tensor.matmul(bank(3 + t % 3), T2[:, t * P:(t + 1) * P], GW[:, 1, :],
                                 start=True, stop=True).then_inc(x2_done, 1)
            nc.tensor.matmul(bank(7), HO, GW[:, 0, :], start=True, stop=True).then_inc(xo_done, 1)
            pe.wait_ge(x_ready, 2 * NC)
            for t in range(NT):
                if t >= 3:
                    pe.wait_ge(x1_evac, t - 2)
                nc.tensor.matmul(bank(t % 3), T2[:, t * P:(t + 1) * P], GW[:, 0, :],
                                 start=True, stop=True).then_inc(x1_done, 1)
            pe.wait_ge(x1_evac, NT)
            pe.wait_ge(row3_ready, NT)
            sparse = pe.value_load(flag[0:1, 0:1], min_val=0, max_val=1)
            with pe.If(sparse > 0):
                def sums(u):
                    T, g = unit(u)
                    x1 = X1H[:, T, :] if T < NT else XO
                    pe.wait_ge(g_here[u % NG], 16 * GS * (u // NG + 1))
                    if u == 0:
                        pe.wait_ge(xo_read, 1)
                    if u >= 2:
                        pe.wait_ge(sums_used, u - 1)
                    for k in range(on_pe(u)):
                        b = bank(sum_banks(u).start + k)
                        nc.tensor.matmul(b, ident[:, :], x1, start=True, stop=False)
                        ins = nc.tensor.matmul(b, ident[:, :], GB[u % NG][:, k, 0:HD], start=False, stop=True)
                    ins.then_inc(sums_ready, 1)

                def numerators(u):
                    T, g = unit(u)
                    b = 3 if T == NT else 4 + T % 2
                    if T < NT and g == 0 and T >= 2:
                        pe.wait_ge(num_ready, T - 1)
                    for k in range(GS):
                        pe.wait_ge(eg_ready, GS * u + k + 1)
                        nc.tensor.matmul(bank(b), ident[:, :], EG[:, k % NE, :], start=(g == 0 and k == 0),
                                         stop=(T == NT and g == 1 and k == GS - 1)).then_inc(eg_used, 1)
                    if T < NT and g == 1:
                        if T == 0:
                            pe.wait_ge(no_ready, 1)
                        nc.tensor.matmul(bank(b), OHT[:, T, :], NO, start=False, stop=True)
                        nc.tensor.matmul(PS[:, 6 + T % 2, 256:256 + HEADS], OHT[:, T, :], DEN[:, NT, :],
                                         start=True, stop=True).then_inc(num_done, 1)

                for u in range(UNITS + 2):
                    if u < UNITS:
                        sums(u)
                    if u >= 2:
                        numerators(u - 2)
            for t in range(NT + 2):
                if t < NT:
                    pe.wait_ge(num_ready, t + 1)
                    if t >= 2:
                        pe.wait_ge(numT_evac, t - 1)
                    for h in range(HEADS):
                        ins = nc.tensor.transpose(PS[:, t % 2, h * P:(h + 1) * P], NUM[:, t, h * D:(h + 1) * D], ident[:, :])
                    ins.then_inc(numT_done, 1)
                if 1 <= t <= NT:
                    i = t - 1
                    pe.wait_ge(numT_evac, i + 1)
                    if i >= 2:
                        pe.wait_ge(lin_copied, i - 1)
                    for h in range(HEADS):
                        ins = nc.tensor.matmul(PS[:, 2 + i % 2, h * P:(h + 1) * P], WLT[:, h, :],
                                               AGT[i % 2][:, h * P:(h + 1) * P], start=True, stop=True)
                    ins.then_inc(lin_done, 1)
                if t >= 2:
                    i = t - 2
                    pe.wait_ge(lin_ready, i + 1)
                    if i == 0:
                        pe.wait_ge(num_ready, NT)
                    if i >= 2:
                        pe.wait_ge(out_ready, i - 1)
                    for h in range(HEADS):
                        ins = nc.tensor.matmul(bank(4 + i % 2, D), LRS[i % 2][:, h * P:(h + 1) * P], WO[:, h, :],
                                               start=(h == 0), stop=(h == HEADS - 1))
                    ins.then_inc(fin_done, 1)


_INS = ['x', 'adj', 'L0_gnn_v_node_feats', 'L0_gnn_uv_W1', 'L0_gnn_uv_b1', 'L0_gnn_uv_W2', 'L0_gnn_uv_b2',
        'L0_gnn_uv_W3', 'L0_gnn_uv_b3', 'L0_gnn_vu_W1', 'L0_gnn_vu_b1', 'L0_gnn_vu_W2', 'L0_gnn_vu_b2',
        'L0_gnn_vu_W3', 'L0_gnn_vu_b3', 'L1_gnn_W', 'L1_gnn_b', 'L2_gnn_W1', 'L2_gnn_b1', 'L2_gnn_W2',
        'L2_gnn_b2', 'L3_gnn_w1', 'L3_gnn_w2', 'L3_gnn_a', 'L3_gnn_Wlin', 'L3_gnn_w']


def kernel(**inputs):
    import numpy as _np
    import concourse.bacc as _bacc
    from concourse import mybir as _mybir
    from concourse.bass_utils import run_bass_kernel_spmd as _run

    nc = _bacc.Bacc("TRN2", target_bir_lowering=False, num_devices=1)
    arrays, args = {}, []
    for name in _INS:
        a = _np.ascontiguousarray(inputs[name])
        arrays[f"in_{name}"] = a
        args.append(nc.dram_tensor(f"in_{name}", a.shape, _mybir.dt.from_np(a.dtype), kind="ExternalInput").ap())
    args.append(nc.dram_tensor("out_0", (N, D), _mybir.dt.float32, kind="ExternalOutput").ap())
    build(nc, *args)
    r = _run(nc, [arrays], core_ids=[0])
    return r.results[0]["out_0"]
```

```python
import concourse.bass as bass
from concourse import mybir
from contextlib import ExitStack

F32 = mybir.dt.float32
F32R = mybir.dt.float32r
I32 = mybir.dt.int32
U32 = mybir.dt.uint32
ALU = mybir.AluOpType
ACT = mybir.ActivationFunctionType
AX = mybir.AxisListType

N = 1354
D = 128
P = 128
NT = -(-N // P)
NP = NT * P
LAST = N - (NT - 1) * P
ROUNDS = 3
HEADS = 4
HD = HEADS * D
CHUNKS = [(0, 4), (4, 8), (8, NT)]
NC = len(CHUNKS)
TWO = 32
MAIN = 8
NBR = 2 * MAIN
TOPK = 4
NEAR = 4
GS = 4
ROWS = 8
NG = 5
NE = 4
TW = HD + D + HEADS
LAST_STAGE = 2 * ROUNDS - 2
N_WEIGHTS = 23
(MEAN, SSQ, VAR, RSTD, ROWSUM, DEG, DEGI, RS2, DL, R2, GAM, GM, GD, AN2, AN, NS, T_A, T_B, T_C, T_D, NN, NSB, SER,
 FAC, QUO, LNQ, YN2, YN, TH, EF, NSQ, SSUM, DD2I, DD, OVF, CUM, POS, T_E, T_F) = range(39)
FAR = 1 << 20


EARLY = 6
SLOPE = 0.01
UNITS = 2 * (NT + 1)
TRANSPOSE, LINEAR, FINAL = 7, 8, 9
DRAINED = 2 * (NT - 1) + FINAL + 1
EPS = 1e-7
ONE_EPS = 1.0 - 2.0 ** -23
GAMMA_MAX = 1e7


def on_pe(u):
    return 0 if u % 3 == 2 else 1


def sums_before(u):
    return sum(on_pe(v) for v in range(u))


def sum_bank(u):
    return 2 * (u % 2)


class Link:

    def __init__(self, eng, sem):
        self.eng, self.sem, self.n = eng, sem, 0

    def mark(self, ins):
        self.n += 1
        ins.then_inc(self.sem, 1)
        return self.n

    def after(self, n):
        self.eng.wait_ge(self.sem, n)

    def __call__(self, ins):
        self.after(self.mark(ins))


def unit(u):
    return (NT if u < 2 else u // 2 - 1), u % 2


def ended(u, lag):
    t = (u - lag) // 2
    return t if (u - lag) % 2 == 0 and 0 <= t < NT else None


def lin_bank(t):
    return 6 if t < NT - 1 else 0


def wait_table(eng, written):
    for i in range(ROWS):
        eng.wait_ge(written[i], 16 * len(range(i, NT, ROWS)))


def cols(c):
    return CHUNKS[c][0] * P, CHUNKS[c][1] * P


def build(nc, x, adj, v_unused, uW1, ub1, uW2, ub2, uW3, ub3, vW1, vb1, vW2, vb2, vW3, vb3,
          hW, hb, lW1, lb1, lW2, lb2, gw1, gw2, ga, gWlin, gw, out):
    with ExitStack() as ctx:
        def sb(name, shape, dt=F32):
            return ctx.enter_context(nc.sbuf_tensor(name, shape, dt))

        def sem(name):
            return ctx.enter_context(nc.semaphore(name))

        A = sb("A", [P, NT, NP])
        AT = sb("AT", [P, NT, NP])
        X = sb("X", [P, NT, D])
        UH = sb("UH", [P, 2 * NT * D])
        U = UH[:, 0:NT * D].rearrange("p (t d) -> p t d", d=D)
        H = UH[:, NT * D:2 * NT * D].rearrange("p (t d) -> p t d", d=D)
        R = sb("R", [P, 3 * NP])
        Z = R[:, 0:NP]
        T1 = R[:, NP:2 * NP]
        T2 = R[:, 2 * NP:3 * NP]
        NX = R[:, 0:NT * (D + 1)].rearrange("p (t n) -> p t n", n=D + 1)
        XG = sb("XG", [P, NT * (D + 1) + 1 + NEAR * (TOPK - 1) * D])
        XC = XG[:, 0:NT * (D + 1)].rearrange("p (t n) -> p t n", n=D + 1)
        JUNK = sb("JUNK", [P, NP])
        SQ = sb("SQ", [P, NP], F32R)
        OW = sb("OW", [P, P], F32R)
        ident = sb("ident", [P, P])
        ones = sb("ones", [P, P])
        negs = sb("negs", [P, P])
        ltri = sb("ltri", [P, P])
        iota = sb("iota", [P, P])
        padone = sb("padone", [P, NT])
        mhalf = sb("mhalf", [P, NT * TOPK])
        phalf = sb("phalf", [P, NT * TOPK])
        W0 = sb("W0", [P, 6, D])
        bcol = sb("bcol", [P, 4 + 1])
        b3 = sb("b3", [P, 2, D])
        brow = sb("brow", [P, 2, D])
        W12 = sb("W12", [P, 3, D])
        GW = sb("GW", [P, 2, HD])
        aB = sb("aB", [P, HD])
        WPQ = sb("WPQ", [P, 2, HEADS])
        WL = sb("WL", [P, HEADS, D])
        WLT = sb("WLT", [P, HEADS, D])
        WO = sb("WO", [P, HEADS, D])
        WG = sb("WG", [P, NT, NBR])
        IG = sb("IG", [P, NT, NBR], U32)
        IGF = sb("IGF", [P, NT, NBR])
        IGU = sb("IGU", [P, NT + 1, MAIN], U32)
        WGO = sb("WGO", [P, NBR])
        CNT = sb("CNT", [P, NT])
        c16 = sb("c16", [P, NT, NBR])
        st = sb("st", [P, 48, NT])
        V8 = sb("V8", [P, NT, 8])
        I8 = sb("I8", [P, NT, 8], U32)
        S4 = sb("S4", [P, NT, TOPK])
        OH = JUNK[:, :].rearrange("p (t n) -> p t n", n=P)
        tally = sb("tally", [P, 2])
        within = sb("within", [1, 2])
        away = sb("away", [P, NT, MAIN])
        flag = sb("flag", [1, 1], I32)
        own = sb("own", [P, NT])
        others = sb("others", [P, 1])
        selfs = sb("selfs", [1, 1], I32)
        spare = sb("spare", [1, 1])
        mask = sb("mask", [P, NT], I32)
        SCR = XG[:, NT * (D + 1) + 1:NT * (D + 1) + 1 + N]
        SELF = T1.rearrange("p (t d) -> p t d", d=D)
        G2 = XG[:, NT * (D + 1) + 1:].rearrange("p (a k d) -> p a k d", a=NEAR, d=D)
        flatAT = AT[:, :, :].rearrange("p t n -> p (t n)")
        o = 0
        X1H = flatAT[:, o:o + NT * HD].rearrange("p (t n) -> p t n", n=HD); o += NT * HD
        NUM = flatAT[:, o:o + NT * HD].rearrange("p (t n) -> p t n", n=HD); o += NT * HD
        Ga = flatAT[:, o:o + GS * TW].rearrange("p (k n) -> p k n", n=TW); o += GS * TW
        OHT = flatAT[:, o:o + NT * P].rearrange("p (t n) -> p t n", n=P); o += NT * P
        assert o <= NT * NP
        flatA = A[:, :, :].rearrange("p t n -> p (t n)")
        GB = [flatA[:, i * GS * TW:(i + 1) * GS * TW].rearrange("p (k n) -> p k n", n=TW) for i in range(NG)]
        EG = flatA[:, NG * GS * TW:NG * GS * TW + NE * HD].rearrange("p (k n) -> p k n", n=HD)
        TT = UH[:, 0:GS * HD].rearrange("p (k n) -> p k n", n=HD)
        XO = UH[:, GS * HD:GS * HD + HD]
        AGT = [R[:, 0:HD], R[:, HD:2 * HD]]
        LRS = [T2[:, 0:HD], T2[:, HD:2 * HD]]
        ROW = flatAT[:, NT * HD:NT * HD + ROWS * TW].rearrange("p (k n) -> p k n", n=TW)
        HO = T1[:, 0:P]
        NO = JUNK[:, 0:HD]
        PQ = sb("PQ", [P, NT, HEADS])
        PO = sb("PO", [P, HEADS])
        DEN = sb("DEN", [P, NT + 1, HEADS])
        sc = sb("sc", [P, 2, 3, GS * HEADS])
        EW = sb("EW", [P, NT + 1, MAIN, HEADS])
        EWF = sb("EWF", [P, GS, HEADS])
        DENF = sb("DENF", [P, HEADS])

        TAB2 = nc.dram_tensor("tab2", [NP, D], F32, kind="Internal").ap()
        TAB3 = nc.dram_tensor("tab3", [NP, TW], F32, kind="Internal").ap()

        PS = ctx.enter_context(nc.psum_tensor("PS", [P, 8, 512], F32))

        def bank(b, n=512):
            return PS[:, b, 0:n]

        ld_x, ld_w, ld_a = sem("ld_x"), sem("ld_w"), [sem(f"ld_a{t}") for t in range(NT)]
        pads, consts = sem("pads"), sem("consts")
        dve_self, act_self, pool_self = sem("dve_self"), sem("act_self"), sem("pool_self")
        st_out = sem("st_out")
        tr_done, tr_evac = sem("tr_done"), sem("tr_evac")
        u_ready = sem("u_ready")
        agg_done, agg_evac = sem("agg_done"), sem("agg_evac")
        l1_done, l1_bias, l1_act = sem("l1_done"), sem("l1_bias"), sem("l1_act")
        l2_done, l2_bias, l2_act = sem("l2_done"), sem("l2_bias"), sem("l2_act")
        l3_done, l3_sum = sem("l3_done"), sem("l3_sum")
        rowsum_ready = sem("rowsum_ready")
        ln_centred, ln_squared, ln_var, ln_rstd, h_ready = (sem("ln_centred"), sem("ln_squared"), sem("ln_var"),
                                                            sem("ln_rstd"), sem("h_ready"))
        deg_ready, degi_ready, dl_ready = sem("deg_ready"), sem("degi_ready"), sem("dl_ready")
        rsq_ready, ye_ready = sem("rsq_ready"), sem("ye_ready")
        ragg_done, ragg_evac = sem("ragg_done"), sem("ragg_evac")
        row_ready, rowT_done, rowT_evac = sem("row_ready"), sem("rowT_done"), sem("rowT_evac")
        n2_ready, pow_in, pow_out = sem("n2_ready"), sem("pow_in"), sem("pow_out")
        q_ready, ln_ready, prod_done = sem("q_ready"), sem("ln_ready"), sem("prod_done")
        y_ready, yn2_ready, yn_ready, tanh_ready = sem("y_ready"), sem("yn2_ready"), sem("yn_ready"), sem("tanh_ready")
        x_ready = sem("x_ready")
        rs2_ready, ys_ready = sem("rs2_ready"), sem("ys_ready")
        z_done, z_bias, z_ready, z2_ready, zsq_ready = (sem("z_done"), sem("z_bias"), sem("z_ready"), sem("z2_ready"),
                                                        sem("zsq_ready"))
        sqb_done, sqb_evac, nsq_done, nsq_evac = sem("sqb_done"), sem("sqb_evac"), sem("nsq_done"), sem("nsq_evac")
        sq_ready, dist_done, key_read = sem("sq_ready"), sem("dist_done"), sem("key_read")
        d4_in, d4_out, s4_ready, ssum_ready, dd_ready = (sem("d4_in"), sem("d4_out"), sem("s4_ready"),
                                                         sem("ssum_ready"), sem("dd_ready"))
        yd_ready, tab2_written, cnt_ready = sem("yd_ready"), sem("tab2_written"), sem("cnt_ready")
        cnt_sign = sem("cnt_sign")
        near_here = [sem(f"near_here{i}") for i in range(NEAR)]
        others_ready, others_done, selfs_ready, self_copied, self_here, self_ready = (
            sem("others_ready"), sem("others_done"), sem("selfs_ready"), sem("self_copied"), sem("self_here"),
            sem("self_ready"))
        plan_ready, plan_done, flag_ready, oh_ready, over_done = (sem("plan_ready"), sem("plan_done"),
                                                                  sem("flag_ready"), sem("oh_ready"), sem("over_done"))
        idx_ready = sem("idx_ready")
        wl_done, wl_evac = sem("wl_done"), sem("wl_evac")
        x1_done, x1_evac, x2_done, x2_evac, row3_ready = (sem("x1_done"), sem("x1_evac"), sem("x2_done"),
                                                          sem("x2_evac"), sem("row3_ready"))
        tab3_written = [sem(f"tab3_written{i}") for i in range(ROWS)]
        oht_done, oht_evac, xo_done = sem("oht_done"), sem("oht_evac"), sem("xo_done")
        ho_done, ho_evac = sem("ho_done"), sem("ho_evac")
        sums_ready, sums_used, xo_read = sem("sums_ready"), sem("sums_used"), sem("xo_read")
        g_here = [sem(f"g_here{i}") for i in range(NG)]
        score_ready, exp_ready, ew_ready = sem("score_ready"), sem("exp_ready"), sem("ew_ready")
        eg_ready, eg_used = sem("eg_ready"), sem("eg_used")
        no_ready, num_done = sem("no_ready"), sem("num_done")
        f_used, f_here, f_self, f_score, f_tanh, f_exp = (sem("f_used"), sem("f_here"), sem("f_self"), sem("f_score"),
                                                          sem("f_tanh"), sem("f_exp"))
        num_ready = sem("num_ready")
        numT_done, numT_evac, lin_done, lin_copied, lin_ready, fin_done, out_ready = (
            sem("numT_done"), sem("numT_evac"), sem("lin_done"), sem("lin_copied"), sem("lin_ready"), sem("fin_done"),
            sem("out_ready"))
        block = ctx.enter_context(nc.Block())

        def nth(s, c):
            return NC * s + c

        def pe_agg(pe, s, kind, c, j0, j1, src):
            lo, hi = cols(c)
            for j in range(j0, j1):
                if src is U and j in (0, 4, 8):
                    pe.wait_ge(u_ready, nth(s - 1, j // 4) + 1)
                last = nc.tensor.matmul(bank(3 * kind + c, hi - lo), src[:, j, :], AT[:, j, lo:hi],
                                        start=(j == 0), stop=(j == NT - 1))
            if j1 == NT:
                last.then_inc(agg_done, 1)

        def pe_l1(pe, s, kind, c):
            lo, hi = cols(c)
            pe.wait_ge(agg_evac, nth(s, c) + 1)
            if not (isinstance(s, int) and s == 0 and c == 0):
                pe.wait_ge(l1_bias, nth(s, c))
            nc.tensor.matmul(bank(6, hi - lo), W0[:, 3 * kind, :], Z[:, lo:hi],
                             start=True, stop=True).then_inc(l1_done, 1)

        def pe_l2(pe, s, kind, c):
            lo, hi = cols(c)
            pe.wait_ge(l1_act, nth(s, c) + 1)
            if not (isinstance(s, int) and s == 0 and c == 0):
                pe.wait_ge(l2_bias, nth(s, c))
            nc.tensor.matmul(bank(7, hi - lo), W0[:, 3 * kind + 1, :], T1[:, lo:hi],
                             start=True, stop=True).then_inc(l2_done, 1)

        def pe_l3(pe, s, kind, c):
            pe.wait_ge(l2_act, nth(s, c) + 1)
            a, b = CHUNKS[c]
            for t in range(a, b):
                last = nc.tensor.matmul(PS[:, 3 * kind + c, (t - a) * D:(t - a + 1) * D],
                                        T2[:, t * P:(t + 1) * P], W0[:, 3 * kind + 2, :],
                                        start=True, stop=True)
            last.then_inc(l3_done, 1)

        def act_agg(act, s, kind, c):
            lo, hi = cols(c)
            act.wait_ge(agg_done, nth(s, c) + 1)
            nc.scalar.activation(Z[:, lo:hi], bank(3 * kind + c, hi - lo), ACT.Copy).then_inc(agg_evac, 1)

        def act_bias(act, s, kind, c, layer):
            lo, hi = cols(c)
            done, said, dst = (l1_done, l1_bias, T1) if layer == 1 else (l2_done, l2_bias, T2)
            act.wait_ge(done, nth(s, c) + 1)
            nc.scalar.activation(dst[:, lo:hi], bank(5 + layer, hi - lo), ACT.Identity,
                                 bias=bcol[:, 2 * kind + layer - 1:2 * kind + layer]).then_inc(said, 1)

        def dve_leaky(dve, s, c, layer):
            lo, hi = cols(c)
            given, said, dst = (l1_bias, l1_act, T1) if layer == 1 else (l2_bias, l2_act, T2)
            dve.wait_ge(given, nth(s, c) + 1)
            nc.vector.scalar_tensor_tensor(dst[:, lo:hi], dst[:, lo:hi], 0.01, dst[:, lo:hi],
                                           ALU.mult, ALU.max).then_inc(said, 1)

        def dve_l3(dve, s, kind, c):
            a, b = CHUNKS[c]
            dve.wait_ge(l3_done, nth(s, c) + 1)
            nc.vector.tensor_tensor(XC[:, a:b, 0:D],
                                    bank(3 * kind + c, (b - a) * D).rearrange("p (t d) -> p t d", d=D),
                                    b3[:, kind:kind + 1, :].to_broadcast([P, b - a, D]),
                                    ALU.add).then_inc(l3_sum, 1)
            dve.wait_ge(l3_sum, nth(s, c) + 1)
            nc.vector.scalar_tensor_tensor(U[:, a:b, :], XC[:, a:b, 0:D], 0.01, XC[:, a:b, 0:D],
                                           ALU.mult, ALU.max).then_inc(u_ready, 1)

        def pe_stage(pe, s, kind):
            k = 1 - kind
            pe_agg(pe, s, kind, 0, 0, 1, U)
            pe_l2(pe, s - 1, k, 1)
            pe_agg(pe, s, kind, 0, 1, 2, U)
            pe_l1(pe, s - 1, k, 2)
            pe_agg(pe, s, kind, 0, 2, 3, U)
            pe_l3(pe, s - 1, k, 1)
            pe_agg(pe, s, kind, 0, 3, 4, U)
            pe_l2(pe, s - 1, k, 2)
            pe_agg(pe, s, kind, 1, 0, 3, U)
            pe_l3(pe, s - 1, k, 2)
            pe_agg(pe, s, kind, 1, 3, 4, U)
            pe_agg(pe, s, kind, 0, 4, 8, U)
            pe_agg(pe, s, kind, 1, 4, 8, U)
            pe_agg(pe, s, kind, 0, 8, NT, U)
            pe_agg(pe, s, kind, 2, 0, 4, U)
            pe_l1(pe, s, kind, 0)
            pe_agg(pe, s, kind, 2, 4, 8, U)
            pe_l2(pe, s, kind, 0)
            pe_agg(pe, s, kind, 1, 8, NT, U)
            pe_l3(pe, s, kind, 0)
            pe_agg(pe, s, kind, 2, 8, NT, U)
            pe_l1(pe, s, kind, 1)

        def pe_rest(pe, s, kind):
            pe_l2(pe, s, kind, 1)
            pe_l1(pe, s, kind, 2)
            pe_l3(pe, s, kind, 1)
            pe_l2(pe, s, kind, 2)
            pe_l3(pe, s, kind, 2)

        def act_rest(act, s, kind):
            act_bias(act, s, kind, 1, 2)
            act_bias(act, s, kind, 2, 1)
            act_bias(act, s, kind, 2, 2)

        def act_stage(act, s, kind):
            act_agg(act, s, kind, 0)
            act_bias(act, s, kind, 0, 1)
            act_bias(act, s, kind, 0, 2)
            act_agg(act, s, kind, 1)
            act_agg(act, s, kind, 2)
            act_bias(act, s, kind, 1, 1)

        def dve_rest(dve, s, kind):
            dve_leaky(dve, s, 1, 2)
            dve_leaky(dve, s, 2, 1)
            dve_l3(dve, s, kind, 1)
            dve_leaky(dve, s, 2, 2)
            dve_l3(dve, s, kind, 2)

        def dve_stage(dve, s, kind):
            dve_leaky(dve, s, 0, 1)
            dve_leaky(dve, s, 0, 2)
            dve_l3(dve, s, kind, 0)
            dve_leaky(dve, s, 1, 1)

        def dve_center(link, l, c):
            a, b = CHUNKS[c]
            link(nc.vector.reduce_sum(st[:, MEAN, a:b], X[:, a:b, :], AX.X))
            link(nc.vector.tensor_scalar(st[:, MEAN, a:b], st[:, MEAN, a:b], 1.0 / D, None, ALU.mult))
            nc.vector.tensor_tensor(XC[:, a:b, 0:D], X[:, a:b, :],
                                    st[:, MEAN, a:b].unsqueeze(2).to_broadcast([P, b - a, D]),
                                    ALU.subtract).then_inc(ln_centred, 1)

        def act_square(act, l, c):
            a, b = CHUNKS[c]
            act.wait_ge(ln_centred, nth(l, c) + 1)
            for t in range(a, b):
                last = nc.scalar.activation((Z if l == 3 else JUNK)[:, t * D:(t + 1) * D], XC[:, t, 0:D], ACT.Square,
                                            accum_out=st[:, SSQ, t:t + 1])
            last.then_inc(ln_squared, 1)

        def dve_var(dve, l, c):
            a, b = CHUNKS[c]
            dve.wait_ge(ln_squared, nth(l, c) + 1)
            nc.vector.tensor_scalar(st[:, VAR, a:b], st[:, SSQ, a:b], 1.0 / D, 1e-5, ALU.mult,
                                    ALU.add).then_inc(ln_var, 1)

        def pool_rstd(pool, l, c):
            a, b = CHUNKS[c]
            pool.wait_ge(ln_var, nth(l, c) + 1)
            pool.tensor_tensor(st[:, RSTD, a:b], st[:, VAR, a:b], mhalf[:, a:b], ALU.pow).then_inc(ln_rstd, 1)

        def dve_norm(dve, l, c):
            a, b = CHUNKS[c]
            dve.wait_ge(ln_rstd, nth(l, c) + 1)
            for t in range(a, b):
                last = nc.vector.tensor_scalar(H[:, t, :], XC[:, t, 0:D], st[:, RSTD, t:t + 1], 0.0,
                                               ALU.mult, ALU.max)
            last.then_inc(h_ready, 1)

        def dve_layernorm(dve, link, l, before=None, after=None):
            def begin(c):
                if before:
                    before(c)
                dve_center(link, l, c)

            def end(c):
                dve_norm(dve, l, c)
                if after:
                    after(c)

            begin(0)
            begin(1)
            dve_var(dve, l, 0)
            begin(2)
            dve_var(dve, l, 1)
            end(0)
            dve_var(dve, l, 2)
            end(1)
            end(2)

        def dve_neighbours(link, t, scratch):
            link(nc.vector.max(WG[:, t, 0:8], A[:, t, 0:N]))
            link(nc.vector.max_index(IG[:, t, 0:8], WG[:, t, 0:8], A[:, t, 0:N]))
            link(nc.vector.match_replace(scratch, WG[:, t, 0:8], A[:, t, 0:N], 0.0))
            link(nc.vector.max(WG[:, t, 8:16], scratch))
            link(nc.vector.max_index(IG[:, t, 8:16], WG[:, t, 8:16], scratch))

        def act_count(act, t):
            at = slice(t, t + 1) if isinstance(t, int) else bass.ds(t, 1)
            nc.scalar.activation(JUNK[:, :].unsqueeze(1), A[:, at, :], ACT.Sign).then_inc(cnt_sign, 1)
            act.wait_ge(cnt_sign, t + 1)
            nc.scalar.activation(JUNK[:, :], JUNK[:, :], ACT.Square,
                                 accum_out=CNT[:, at]).then_inc(cnt_ready, 1)
            act.wait_ge(cnt_ready, t + 1)

        @block.sync
        def _(sp):
            def rows(t):
                return P if t < NT - 1 else LAST

            full = NT - 1
            sp.dma_start(X[:, 0:full, :], x[0:full * P, :].rearrange("(t p) d -> p t d", p=P)).then_inc(ld_x, 16)
            sp.wait_ge(pads, 2)
            sp.dma_start(X[0:LAST, full, :], x[full * P:N, :]).then_inc(ld_x, 16)
            def load_tiles(a, b):
                for t in range(a, b):
                    sp.dma_start(A[0:rows(t), t, 0:N], adj[t * P:t * P + rows(t), :]).then_inc(ld_a[t], 16)

            load_tiles(0, 4)
            for i, w in enumerate((uW1, uW2, uW3, vW1, vW2, vW3)):
                sp.dma_start(W0[:, i, :], w).then_inc(ld_w, 16)
            for i, b in enumerate((ub1, ub2, vb1, vb2, lb1)):
                sp.dma_start(bcol[:, i:i + 1], b.rearrange("(p o) -> p o", o=1)).then_inc(ld_w, 16)
            for i, b in enumerate((ub3, vb3)):
                sp.dma_start(b3[:, i, :], b.rearrange("(o d) -> o d", o=1).to_broadcast([P, D])).then_inc(ld_w, 16)
            load_tiles(4, NT)
            for i, b in enumerate((hb, lb2)):
                sp.dma_start(brow[:, i, :], b.rearrange("(o d) -> o d", o=1).to_broadcast([P, D])).then_inc(ld_w, 16)
            for i, w in enumerate((hW, lW1, lW2)):
                sp.dma_start(W12[:, i, :], w).then_inc(ld_w, 16)
            for i, w in enumerate((gw1, gw2)):
                sp.dma_start(GW[:, i, :].rearrange("p (h d) -> p h d", d=D),
                              w.rearrange("h p d -> p h d")).then_inc(ld_w, 16)
            sp.dma_start(aB[:, :], ga.rearrange("(o h) d -> o (h d)", o=1).to_broadcast([P, HD])).then_inc(ld_w, 16)
            sp.dma_start(WL[:, :, :], gWlin.rearrange("h p d -> p h d")).then_inc(ld_w, 16)
            sp.dma_start(WO[:, :, :], gw.rearrange("(h p) d -> p h d", p=P)).then_inc(ld_w, 16)
            for c, (a, b) in enumerate(CHUNKS):
                sp.wait_ge(yd_ready, c + 1)
                sp.dma_start(TAB2[a * P:b * P, :].rearrange("(t p) d -> p t d", p=P), U[:, a:b, :])\
                  .then_inc(tab2_written, 16)
            for t in range(NT):
                sp.wait_ge(row3_ready, t + 1)
                sp.dma_start(TAB3[t * P:(t + 1) * P, :], ROW[:, t % ROWS, :]).then_inc(tab3_written[t % ROWS], 16)
            sp.wait_ge(flag_ready, 1)
            sparse = sp.value_load(flag[0:1, 0:1], min_val=0, max_val=1)
            with sp.If(sparse < 1):
                wait_table(sp, tab3_written)
                with sp.Fori(0, NT) as t:
                    with sp.Fori(0, NP // GS) as g:
                        sp.wait_ge(f_used, t * (NP // GS) + g + 1)
                        sp.dma_start(Ga[:, :, :],
                                     TAB3[bass.ds(g * GS, GS), :].rearrange("(o k) n -> o k n", o=1)
                                     .to_broadcast([P, GS, TW])).then_inc(f_here, 16)
            for t in range(NT):
                n = P if t < NT - 1 else LAST
                sp.wait_ge(out_ready, t + 1)
                sp.dma_start(out[t * P:t * P + n, :], X[0:n, t, :]).then_inc(st_out, 16)
            sp.wait_ge(st_out, 16 * NT)

        @block.scalar
        def _(act):
            alink = Link(act, act_self)
            for c in range(NC):
                act_square(act, 0, c)

            def transposed(t):
                for g, (a, b) in enumerate(CHUNKS):
                    act.wait_ge(tr_done, nth(t, g) + 1)
                    nc.scalar.activation(AT[:, a:b, t * P:(t + 1) * P],
                                         bank(3 + g, (b - a) * P).rearrange("p (j i) -> p j i", i=P),
                                         ACT.Copy).then_inc(tr_evac, 1)

            def rowsum(t):
                act.wait_ge(ld_a[t], 16)
                act.wait_ge(pads, 3)
                if t > 0:
                    act.wait_ge(rowsum_ready, t)
                nc.scalar.activation(JUNK[:, :], A[:, t, :], ACT.Copy,
                                     accum_out=st[:, ROWSUM, t:t + 1]).then_inc(rowsum_ready, 1)

            for t in range(0, 4):
                transposed(t)
            for t in range(4, 8):
                transposed(t)
            act.wait_ge(ld_w, 16 * N_WEIGHTS)
            act_agg(act, 0, 0, 0)
            act_bias(act, 0, 0, 0, 1)
            act_bias(act, 0, 0, 0, 2)
            for t in range(8, NT):
                transposed(t)
            act_agg(act, 0, 0, 1)
            act_bias(act, 0, 0, 1, 1)
            for t in range(3):
                rowsum(t)
            act_agg(act, 0, 0, 2)

            def fill(s):
                for t in (2 * s + 3, 2 * s + 4):
                    act.wait_ge(rowsum_ready, t)
                    nc.scalar.activation(JUNK[:, :].unsqueeze(1), A[:, bass.ds(t, 1), :], ACT.Copy,
                                         accum_out=st[:, ROWSUM, bass.ds(t, 1)]).then_inc(rowsum_ready, 1)
                act.wait_ge(rowsum_ready, 2 * s + 5)
                act_count(act, 2 * s)
                act_count(act, 2 * s + 1)

            with act.Fori(0, ROUNDS - 1) as r:
                act_rest(act, 2 * r, 0)
                fill(2 * r)
                act_stage(act, 2 * r + 1, 1)
                act_rest(act, 2 * r + 1, 1)
                fill(2 * r + 1)
                act_stage(act, 2 * r + 2, 0)
            act_rest(act, LAST_STAGE, 0)

            def squares(dst, src, ready, base, said):
                for t in range(NT):
                    if t in (0, 4, 8):
                        act.wait_ge(ready, base + t // 4 + 1)
                    ins = nc.scalar.activation(JUNK[:, t * D:(t + 1) * D], src[:, t, :], ACT.Square,
                                               accum_out=st[:, dst, t:t + 1])
                    if t in (3, 7, NT - 1):
                        ins.then_inc(said, 1)

            def row_transposed(base, c):
                lo, hi = cols(c)
                act.wait_ge(rowT_done, base + c + 1)
                nc.scalar.activation(T2[:, lo:hi], bank(6 + c % 2, hi - lo), ACT.Copy).then_inc(rowT_evac, 1)

            act.wait_ge(wl_done, 1)
            nc.scalar.activation(WLT[:, :, :].rearrange("p h d -> p (h d)"), bank(7), ACT.Copy).then_inc(wl_evac, 1)
            act.wait_ge(rowsum_ready, NT)
            for c in range(NC):
                act_square(act, 1, c)
            squares(R2, H, h_ready, NC, rsq_ready)
            act.wait_ge(rsq_ready, NC)
            for t in range(NT):
                act.wait_ge(row_ready, t + 1)
                last = nc.scalar.activation(JUNK[:, t * D:(t + 1) * D], U[:, t, :], ACT.Square,
                                            accum_out=st[:, AN2, t:t + 1])
                if t in (3, 7, NT - 1):
                    last.then_inc(n2_ready, 1)
                if t in (1, 5, 9):
                    last.then_inc(act_self, 1)
                    alink.n += 1
                    act.wait_ge(act_self, alink.n)
                    act_count(act, 8 + t // 4)
                if t in (5, 9):
                    row_transposed(0, (t - 5) // 4)
            row_transposed(0, 2)
            act.wait_ge(q_ready, 1)
            nc.scalar.activation(st[:, LNQ, :], st[:, QUO, :], ACT.Ln).then_inc(ln_ready, 1)
            act.wait_ge(n2_ready, NC)
            squares(YN2, U, y_ready, 0, yn2_ready)
            act.wait_ge(yn_ready, 1)
            nc.scalar.activation(st[:, TH, :], st[:, NS, :], ACT.Tanh).then_inc(tanh_ready, 1)

            act.wait_ge(yn2_ready, NC)
            for c in range(NC):
                act_square(act, 2, c)
            for t in range(NT):
                act.wait_ge(ragg_done, NT + t + 1)
                nc.scalar.activation(U[:, t, :], bank(t % 6, D), ACT.Copy,
                                     scale=st[:, DL, t:t + 1]).then_inc(ragg_evac, 1)
                if t in (5, 9):
                    row_transposed(NC, (t - 5) // 4)
            row_transposed(NC, 2)
            for c in range(NC):
                lo, hi = cols(c)
                act.wait_ge(z_done, c + 1)
                nc.scalar.activation(Z[:, lo:hi], bank(c, hi - lo), ACT.Identity, bias=bcol[:, 4:5]).then_inc(z_bias, 1)
            for c in range(NC):
                lo, hi = cols(c)
                act.wait_ge(z_ready, c + 1)
                nc.scalar.activation(T2[:, lo:hi], Z[:, lo:hi], ACT.Square).then_inc(zsq_ready, 1)
            for c in range(NC):
                lo, hi = cols(c)
                act.wait_ge(sqb_done, c + 1)
                nc.scalar.activation(SQ[:, lo:hi], bank(3 + c, hi - lo), ACT.Copy).then_inc(sqb_evac, 1)
            act.wait_ge(nsq_done, 1)
            nc.scalar.activation(st[:, NSQ, :], bank(6, NT), ACT.Copy).then_inc(nsq_evac, 1)
            for t in range(NT):
                act.wait_ge(d4_out, t + 1)
                nc.scalar.activation(S4[:, t, :], S4[:, t, :], ACT.Exp, scale=-0.5,
                                     accum_out=st[:, SSUM, t:t + 1]).then_inc(s4_ready, 1)
            act.wait_ge(dist_done, NT)
            for c, (a, b) in enumerate(CHUNKS):
                act.wait_ge(yd_ready, c + 1)
                nc.scalar.activation(SELF[:, a:b, :], U[:, a:b, :], ACT.Copy).then_inc(self_copied, 1)
            for c in range(NC):
                row_transposed(2 * NC, c)
                if c < NC - 1:
                    act_square(act, 3, c)

            for c, (a, b) in enumerate(CHUNKS):
                act.wait_ge(oht_done, c + 1)
                nc.scalar.activation(OHT[:, a:b, :].rearrange("p t n -> p (t n)"), bank(3 + c, (b - a) * P),
                                     ACT.Copy).then_inc(oht_evac, 1)
            act_square(act, 3, NC - 1)
            for c in range(NC):
                row_transposed(3 * NC, c)
            for t in range(NT):
                act.wait_ge(x1_done, t + 1)
                nc.scalar.activation(X1H[:, t, :], bank(t % 3), ACT.Copy).then_inc(x1_evac, 1)
                if t == 2:
                    act.wait_ge(ho_done, 1)
                    nc.scalar.activation(HO, bank(7, P), ACT.Copy).then_inc(ho_evac, 1)

            def act_transposed(t):
                act.wait_ge(numT_done, t + 1)
                nc.scalar.activation(AGT[t % 2], bank(3), ACT.Copy).then_inc(numT_evac, 1)

            def act_linear(t):
                act.wait_ge(lin_done, t + 1)
                nc.scalar.activation(LRS[t % 2], bank(lin_bank(t)), ACT.Copy).then_inc(lin_copied, 1)

            act.wait_ge(flag_ready, 1)
            sparse = act.value_load(flag[0:1, 0:1], min_val=0, max_val=1)
            with act.If(sparse > 0):
                def end_steps(u):
                    if ended(u, TRANSPOSE) is not None:
                        act_transposed(ended(u, TRANSPOSE))
                    if ended(u, LINEAR) is not None:
                        act_linear(ended(u, LINEAR))

                def blend(u):
                    T, g = unit(u)
                    act.wait_ge(ew_ready, u + 1)
                    for k in range(GS):
                        if GS * u + k >= NE:
                            act.wait_ge(eg_used, GS * u + k - NE + 1)
                        for h in range(HEADS):
                            ins = nc.scalar.activation(EG[:, k % NE, h * D:(h + 1) * D], GB[u % NG][:, k, HD:HD + D],
                                                       ACT.Copy, scale=EW[:, T, g * GS + k, h:h + 1])
                        ins.then_inc(eg_ready, 1)
                        if k == 1:
                            end_steps(u + 1)

                for u in range(DRAINED):
                    if 1 <= u <= UNITS:
                        blend(u - 1)
                    else:
                        end_steps(u)
                    if u < UNITS:
                        s2 = sc[:, u % 2, 2, :]
                        act.wait_ge(score_ready, u + 1)
                        alink(nc.scalar.activation(s2, s2, ACT.Tanh, scale=0.125))
                        nc.scalar.activation(s2, s2, ACT.Exp, scale=8.0).then_inc(exp_ready, 1)
            with act.Else():
                with act.Fori(0, NT * (NP // GS)) as n:
                    s2 = sc[:, 0, 2, :]
                    act.wait_ge(f_score, n + 1)
                    nc.scalar.activation(s2, s2, ACT.Tanh, scale=0.125).then_inc(f_tanh, 1)
                    act.wait_ge(f_tanh, n + 1)
                    nc.scalar.activation(s2, s2, ACT.Exp, scale=8.0).then_inc(f_exp, 1)
                for t in range(NT):
                    act_transposed(t)
                    act_linear(t)

        @block.vector
        def _(dve):
            link = Link(dve, dve_self)
            nc.vector.memset(X[64:P, NT - 1, :], 0.0).then_inc(pads, 1)
            nc.vector.memset(A[64:P, NT - 1, 0:N], 0.0).then_inc(pads, 1)
            nc.vector.memset(A[:, :, N:NP], 0.0).then_inc(pads, 1)
            dve.wait_ge(ld_x, 32)
            dve_layernorm(dve, link, 0)
            for t in range(3):
                dve.wait_ge(ld_a[t], 16)
                dve_neighbours(link, t, SCR)
            dve.wait_ge(ld_w, 16 * N_WEIGHTS)
            dve_leaky(dve, 0, 0, 1)
            dve_neighbours(link, 3, SCR)
            dve_leaky(dve, 0, 0, 2)
            dve_neighbours(link, 4, SCR)
            dve_l3(dve, 0, 0, 0)
            dve_leaky(dve, 0, 1, 1)
            dve_neighbours(link, 5, SCR)
            for s in range(1, LAST_STAGE + 1):
                dve_rest(dve, s - 1, (s - 1) % 2)
                dve_neighbours(link, EARLY + s - 1, SCR)
                dve_stage(dve, s, s % 2)
            dve_rest(dve, LAST_STAGE, 0)

            def S(i, a=0, b=NT):
                return st[:, i, a:b]

            dve.wait_ge(rowsum_ready, NT)
            dve.wait_ge(consts, 3)
            nc.vector.tensor_scalar(S(DEG), S(ROWSUM), 1.0, None, ALU.add).then_inc(deg_ready, 1)
            nc.vector.tensor_tensor(S(RS2), S(ROWSUM), padone[:, :], ALU.add).then_inc(rs2_ready, 1)

            def add_layer0(c):
                a, b = CHUNKS[c]
                dve.wait_ge(u_ready, nth(LAST_STAGE, c) + 1)
                link(nc.vector.tensor_tensor(X[:, a:b, :], X[:, a:b, :], U[:, a:b, :], ALU.add))

            def by_degree(c):
                a, b = CHUNKS[c]
                if c == 0:
                    dve.wait_ge(degi_ready, 1)
                dve.wait_ge(h_ready, nth(1, c) + 1)
                for t in range(a, b):
                    nc.vector.tensor_scalar(XC[:, t, 0:D], H[:, t, :], S(DEGI, t, t + 1), None, ALU.mult)
                nc.vector.tensor_copy(XC[:, a:b, D:D + 1], S(DEGI, a, b).unsqueeze(2)).then_inc(ye_ready, 1)

            dve_layernorm(dve, link, 1, add_layer0, by_degree)
            dve.wait_ge(rsq_ready, NC)
            link(nc.vector.tensor_scalar(S(T_A), S(R2), -1.0, 1.0, ALU.mult, ALU.add))
            link(nc.vector.reciprocal(S(T_B), S(T_A)))
            link(nc.vector.tensor_scalar(S(GAM), S(T_B), 2.0, GAMMA_MAX, ALU.mult, ALU.min))
            link(nc.vector.tensor_scalar(S(T_C), S(GAM), -1.0, None, ALU.add))
            link(nc.vector.tensor_tensor(S(GM), S(T_C), S(DEGI), ALU.mult))
            link(nc.vector.tensor_tensor(S(GD), S(GAM), S(DEGI), ALU.mult))
            def root_argument(norms, a, b):
                dve.wait_ge(pow_out, norms)
                link(nc.vector.tensor_scalar(S(NS, a, b), S(AN, a, b), EPS, ONE_EPS, ALU.max, ALU.min))
                link(nc.vector.tensor_scalar(S(T_A, a, b), S(NS, a, b), -1.0, 1.0, ALU.mult, ALU.add))
                link(nc.vector.tensor_scalar(S(T_B, a, b), S(NS, a, b), 1.0, None, ALU.add))
                nc.vector.tensor_tensor(S(T_C, a, b), S(T_A, a, b), S(T_B, a, b), ALU.mult).then_inc(pow_in, 1)

            dve.wait_ge(ye_ready, NC)
            for t in range(NT):
                dve.wait_ge(ragg_done, t + 1)
                nc.vector.tensor_tensor(NX[:, t, :], bank(t % 6, D + 1), XC[:, t, :], ALU.add).then_inc(ragg_evac, 1)
                dve.wait_ge(ragg_evac, t + 1)
                link(nc.vector.tensor_scalar(S(T_F, t, t + 1), NX[:, t, D:D + 1], S(GM, t, t + 1), None, ALU.mult))
                link(nc.vector.reciprocal(S(T_E, t, t + 1), S(T_F, t, t + 1)))
                nc.vector.tensor_scalar(U[:, t, :], NX[:, t, 0:D], S(T_E, t, t + 1), S(GD, t, t + 1),
                                        ALU.mult, ALU.mult).then_inc(row_ready, 1)
                if t == NT - 2:
                    root_argument(NC - 1, 0, CHUNKS[-1][0])
                if t == 5:
                    for i in range(2):
                        link(nc.vector.tensor_tensor(SCR[:, 0:HD], GW[:, i, :], aB[:, :], ALU.mult))
                        link(nc.vector.reduce_sum(WPQ[:, i, :], SCR[:, 0:HD].rearrange("p (h d) -> p h d", d=D), AX.X))
                if t == 1:
                    dve_neighbours(link, NT - 1, SCR)
            root_argument(NC + 1, CHUNKS[-1][0], NT)
            dve.wait_ge(pow_out, NC + 2)
            dve.wait_ge(row_ready, NT)
            link(nc.vector.tensor_scalar(S(T_A), S(T_D), 1.0, None, ALU.add))
            link(nc.vector.reciprocal(S(T_B), S(T_A)))
            link(nc.vector.tensor_tensor(S(NN), S(AN), S(T_B), ALU.mult))
            link(nc.vector.tensor_scalar(S(NSB), S(NN), EPS, ONE_EPS, ALU.max, ALU.min))
            link(nc.vector.tensor_scalar(S(T_A), S(NSB), -1.0, 1.0, ALU.mult, ALU.add))
            link(nc.vector.reciprocal(S(T_C), S(T_A)))
            link(nc.vector.tensor_scalar(S(T_A), S(NSB), 1.0, None, ALU.add))
            nc.vector.tensor_tensor(S(QUO), S(T_A), S(T_C), ALU.mult).then_inc(q_ready, 1)
            dve.wait_ge(q_ready, 1)
            link(nc.vector.tensor_tensor(S(T_A), S(NSB), S(NSB), ALU.mult))
            link(nc.vector.tensor_scalar(S(SER), S(T_A), 1.0 / 17, None, ALU.mult))
            for k in (15, 13, 11, 9, 7, 5, 3):
                link(nc.vector.scalar_tensor_tensor(S(SER), S(SER), 1.0 / k, S(T_A), ALU.add, ALU.mult))
            link(nc.vector.tensor_scalar(S(SER), S(SER), 1.0, None, ALU.add))
            link(nc.vector.reciprocal(S(T_C), S(NSB)))
            link(nc.vector.tensor_scalar(mask[:, :], S(NSB), 0.25, None, ALU.is_lt))
            dve.wait_ge(ln_ready, 1)
            link(nc.vector.scalar_tensor_tensor(S(FAC), S(LNQ), 0.5, S(T_C), ALU.mult, ALU.mult))
            link(nc.vector.copy_predicated(S(FAC), mask[:, :], S(SER)))
            link(nc.vector.tensor_tensor(S(FAC), S(FAC), S(T_B), ALU.mult))
            for c, (a, b) in enumerate(CHUNKS):
                dve.wait_ge(prod_done, c + 1)
                for t in range(a, b):
                    ins = nc.vector.scalar_tensor_tensor(U[:, t, :], PS[:, c, (t - a) * D:(t - a + 1) * D],
                                                         S(FAC, t, t + 1), brow[:, 0, :], ALU.mult, ALU.add)
                link(ins)
                nc.vector.tensor_scalar(U[:, a:b, :], U[:, a:b, :], 0.0, None, ALU.max).then_inc(y_ready, 1)
            dve.wait_ge(pow_out, 2 * NC + 2)
            nc.vector.tensor_scalar(S(NS), S(YN), EPS, None, ALU.max).then_inc(yn_ready, 1)
            dve.wait_ge(yn_ready, 1)
            link(nc.vector.reciprocal(S(T_A), S(NS)))
            dve.wait_ge(tanh_ready, 1)
            link(nc.vector.tensor_tensor(S(EF), S(TH), S(T_A), ALU.mult))

            def add_layer1(c):
                a, b = CHUNKS[c]
                for t in range(a, b):
                    ins = nc.vector.scalar_tensor_tensor(X[:, t, :], U[:, t, :], S(EF, t, t + 1), X[:, t, :],
                                                         ALU.mult, ALU.add)
                ins.then_inc(x_ready, 1)
                dve.wait_ge(x_ready, c + 1)


            def by_root(c):
                a, b = CHUNKS[c]
                if c == 0:
                    dve.wait_ge(dl_ready, 1)
                dve.wait_ge(h_ready, nth(2, c) + 1)
                for t in range(a, b):
                    ins = nc.vector.tensor_scalar(XC[:, t, 0:D], H[:, t, :], S(DL, t, t + 1), None, ALU.mult)
                ins.then_inc(ys_ready, 1)

            dve_layernorm(dve, link, 2, add_layer1, by_root)
            link(nc.vector.tensor_scalar(c16[:, :, :], WG[:, :, :], 0.0, None, ALU.is_gt))
            link(nc.vector.reduce_sum(S(T_A), c16[:, :, :], AX.X))
            dve.wait_ge(cnt_ready, NT)
            link(nc.vector.tensor_tensor(S(T_B), S(T_A), CNT[:, :], ALU.not_equal))
            link(nc.vector.reduce_sum(tally[:, 0:1], S(T_B), AX.X))
            link(nc.vector.tensor_copy(S(OVF).unsqueeze(2), c16[:, :, MAIN:MAIN + 1]))
            link(nc.vector.reduce_sum(tally[:, 1:2], S(OVF), AX.X))
            link(nc.vector.memset(S(CUM, 0, 1), 0.0))
            for t in range(NT - 1):
                link(nc.vector.tensor_tensor(S(CUM, t + 1, t + 2), S(CUM, t, t + 1), S(OVF, t, t + 1), ALU.add))
            nc.vector.tensor_copy(IGF[:, :, :], IG[:, :, :]).then_inc(plan_ready, 1)
            dve.wait_ge(plan_ready, 1)
            link(nc.vector.tensor_scalar(away[:, :, :], c16[:, :, 0:MAIN], -float(FAR), float(FAR), ALU.mult, ALU.add))
            link(nc.vector.tensor_tensor(away[:, :, :], away[:, :, :], IGF[:, :, 0:MAIN], ALU.add))
            link(nc.vector.tensor_copy(IGU[:, 0:NT, :], away[:, :, :]))
            for c in range(NC):
                lo, hi = cols(c)
                dve.wait_ge(z_bias, c + 1)
                nc.vector.scalar_tensor_tensor(Z[:, lo:hi], Z[:, lo:hi], 0.1, Z[:, lo:hi],
                                               ALU.mult, ALU.max).then_inc(z_ready, 1)
                dve.wait_ge(z_ready, c + 1)
                nc.vector.tensor_scalar(T1[:, lo:hi], Z[:, lo:hi], 2.0, None, ALU.mult).then_inc(z2_ready, 1)

            for c in range(NC):
                lo, hi = cols(c)
                dve.wait_ge(sqb_evac, c + 1)
                nc.vector.tensor_tensor(SQ[TWO:TWO + 1, lo:hi], PS[TWO:TWO + 1, 3 + c, 0:hi - lo],
                                        SQ[TWO:TWO + 1, lo:hi].bitcast(F32), ALU.subtract).then_inc(sq_ready, 1)
            dve.wait_ge(nsq_evac, 1)

            def degrees(c):
                a, b = CHUNKS[c]
                dve.wait_ge(s4_ready, b)
                nc.vector.tensor_tensor(S(DD2I, a, b), S(RS2, a, b), S(SSUM, a, b), ALU.add).then_inc(ssum_ready, 1)

            def by_new_degree(c):
                a, b = CHUNKS[c]
                dve.wait_ge(dd_ready, c + 1)
                for t in range(a, b):
                    ins = nc.vector.tensor_scalar(U[:, t, :], H[:, t, :], S(DD, t, t + 1), None, ALU.mult)
                ins.then_inc(yd_ready, 1)

            for t in range(NT):
                key = PS[:, 3 * (t % 2):3 * (t % 2) + 3, :].rearrange("p b n -> p (b n)")[:, 0:N]
                dve.wait_ge(dist_done, t + 1)
                link(nc.vector.max(V8[:, t, :], key))
                nc.vector.max_index(I8[:, t, :], V8[:, t, :], key).then_inc(key_read, 1)
                link(nc.vector.tensor_scalar(S4[:, t, :], V8[:, t, 0:TOPK], S(NSQ, t, t + 1), 0.0, ALU.add, ALU.min))
                nc.vector.tensor_scalar(S4[:, t, :], S4[:, t, :], -1.0, 1e-10, ALU.mult, ALU.add).then_inc(d4_in, 1)
                if t in (5, 9):
                    degrees((t - 5) // 4)
                if t in (7, NT - 1):
                    by_new_degree((t - 7) // 3)
            degrees(NC - 1)
            by_new_degree(NC - 1)
            link(nc.vector.tensor_copy(S(T_A).unsqueeze(2), I8[:, :, 0:1]))
            link(nc.vector.tensor_tensor(S(T_A), S(T_A), own[:, :], ALU.not_equal))
            link(nc.vector.tensor_tensor(S(T_A), S(T_A), padone[:, :], ALU.subtract))
            nc.vector.reduce_sum(others[:, :], S(T_A), AX.X).then_inc(others_ready, 1)
            dve.wait_ge(plan_done, 1)
            link(nc.vector.tensor_scalar(within[:, 0:1], PS[0:1, 7, 0:1], 0.5, None, ALU.is_lt))
            link(nc.vector.tensor_scalar(within[:, 1:2], PS[0:1, 7, 1:2], P + 0.5, None, ALU.is_lt))
            nc.vector.tensor_tensor(flag[:, :], within[:, 0:1], within[:, 1:2], ALU.mult).then_inc(flag_ready, 1)
            dve.wait_ge(others_done, 1)
            nc.vector.tensor_scalar(selfs[:, :], PS[0:1, 6, 500:501], 0.5, None, ALU.is_lt).then_inc(selfs_ready, 1)
            link(nc.vector.tensor_copy(S(POS), PS[:, 7, 16:16 + NT]))
            for t in range(NT):
                ins = nc.vector.tensor_scalar(OH[:, t, :], iota[:, :], S(POS, t, t + 1), S(OVF, t, t + 1),
                                              ALU.is_equal, ALU.mult)
            ins.then_inc(oh_ready, 1)

            def residual(c):
                a, b = CHUNKS[c]
                dve.wait_ge(prod_done, NC + c + 1)
                for t in range(a, b):
                    ins = nc.vector.scalar_tensor_tensor(X[:, t, :], PS[:, c, (t - a) * D:(t - a + 1) * D],
                                                         S(DD, t, t + 1), X[:, t, :], ALU.mult, ALU.add)
                ins.then_inc(x_ready, 1)
                dve.wait_ge(x_ready, NC + c + 1)

            link(nc.vector.tensor_tensor(X[:, :, :], X[:, :, :], brow[:, 1:2, :].to_broadcast([P, NT, D]), ALU.add))
            for t in range(NT):
                dve.wait_ge(ragg_done, 2 * NT + t + 1)
                dve.wait_ge(near_here[t % NEAR], 16 * (TOPK - 1) * (t // NEAR + 1))
                if t == 0:
                    dve.wait_ge(self_ready, 1)
                nc.vector.scalar_tensor_tensor(XC[:, t, 0:D], SELF[:, t, :], S4[:, t, 0:1], bank(3 + t % 3, D),
                                               ALU.mult, ALU.add).then_inc(ragg_evac, 1)
                dve.wait_ge(ragg_evac, 2 * NT + t + 1)
                for k in range(1, TOPK):
                    ins = nc.vector.scalar_tensor_tensor(XC[:, t, 0:D], G2[:, t % NEAR, k - 1, :], S4[:, t, k:k + 1],
                                                         XC[:, t, 0:D], ALU.mult, ALU.add)
                    if k < TOPK - 1:
                        link(ins)
                ins.then_inc(row_ready, 1)
                if t == 3:
                    dve.wait_ge(over_done, 1)
                    link(nc.vector.tensor_copy(WGO[:, 0:NBR], PS[:, 7, 64:64 + NBR]))
                    link(nc.vector.tensor_scalar(away[:, 0, :], WGO[:, 0:MAIN], 0.0, float(FAR), ALU.is_le, ALU.mult))
                    link(nc.vector.tensor_tensor(away[:, 0, :], away[:, 0, :], WGO[:, MAIN:NBR], ALU.add))
                    nc.vector.tensor_copy(IGU[:, NT, :], away[:, 0, :]).then_inc(idx_ready, 1)
                if t in (5, 9):
                    residual((t - 5) // 4)
                    dve_center(link, 3, (t - 5) // 4)
                if t == 8:
                    dve_var(dve, 3, 0)
            dve_var(dve, 3, 1)
            for c in range(NC - 1):
                dve_norm(dve, 3, c)
            residual(NC - 1)
            dve_center(link, 3, NC - 1)
            dve_var(dve, 3, NC - 1)
            dve_norm(dve, 3, NC - 1)


            dve.wait_ge(h_ready, NC * 4)
            for t in range(NT):
                row = ROW[:, t % ROWS, :]
                if t >= ROWS:
                    dve.wait_ge(tab3_written[t % ROWS], 16 * (t // ROWS))
                nc.vector.tensor_copy(row[:, HD:HD + D], H[:, t, :])
                dve.wait_ge(x2_done, t + 1)
                nc.vector.tensor_copy(row[:, 0:HD], bank(3 + t % 3)).then_inc(x2_evac, 1)
                nc.vector.tensor_copy(row[:, HD + D:TW], PS[:, 6 + t % 2, HEADS:2 * HEADS])
                nc.vector.tensor_copy(PQ[:, t, :], PS[:, 6 + t % 2, 0:HEADS]).then_inc(row3_ready, 1)
            dve.wait_ge(row3_ready, NT)

            def dve_leaky_sum(t):
                LR = LRS[t % 2]
                dve.wait_ge(lin_copied, t + 1)
                nc.vector.scalar_tensor_tensor(LR, LR, SLOPE, LR, ALU.mult, ALU.max).then_inc(lin_ready, 1)

            def dve_out(t):
                dve.wait_ge(fin_done, t + 1)
                nc.vector.tensor_tensor(X[:, t, :], X[:, t, :], bank(lin_bank(t), D), ALU.add).then_inc(out_ready, 1)

            sparse = dve.value_load(flag[0:1, 0:1], min_val=0, max_val=1)
            with dve.If(sparse > 0):
                dve.wait_ge(xo_done, 1)
                link(nc.vector.tensor_copy(XO[:, :], bank(7)))
                nc.vector.tensor_copy(PO[:, :], PS[:, 6, 128:128 + HEADS]).then_inc(xo_read, 1)
                dve.wait_ge(xo_read, 1)

                def weigh(u):
                    T, g = unit(u)
                    w = WG[:, T, g * GS:(g + 1) * GS] if T < NT else WGO[:, g * GS:(g + 1) * GS]
                    dve.wait_ge(exp_ready, u + 1)
                    nc.vector.tensor_tensor(EW[:, T, g * GS:(g + 1) * GS, :],
                                            sc[:, u % 2, 2, :].rearrange("p (k h) -> p k h", h=HEADS),
                                            w.unsqueeze(2).to_broadcast([P, GS, HEADS]), ALU.mult).then_inc(ew_ready, 1)

                def den_sum(T):
                    dve.wait_ge(ew_ready, 2 * T + 4 if T < NT else 2)
                    return link.mark(nc.vector.reduce_sum(DEN[:, T, :], EW[:, T, :, :].rearrange("p k h -> p h k"), AX.X))

                def den_total(T, summed):
                    dve.wait_ge(num_done, T + 1)
                    link.after(summed)
                    n = link.mark(nc.vector.tensor_tensor(DEN[:, T, :], DEN[:, T, :],
                                                          PS[:, 7, 256:256 + HEADS], ALU.add))
                    if T == NT - 1:
                        link.after(n)
                        n = link.mark(nc.vector.tensor_scalar(DEN[:, T, :], DEN[:, T, :], padone[:, T:T + 1], None,
                                                              ALU.add))
                    return n

                def den_inverse(T, total):
                    link.after(total)
                    return link.mark(nc.vector.reciprocal(DEN[:, T, :], DEN[:, T, :]))

                def divide(T, inverse):
                    link.after(inverse)
                    nc.vector.tensor_tensor(NUM[:, T, :].rearrange("p (h d) -> p h d", d=D),
                                            bank(4 + T % 2).rearrange("p (h d) -> p h d", d=D),
                                            DEN[:, T, :].unsqueeze(2).to_broadcast([P, HEADS, D]),
                                            ALU.mult).then_inc(num_ready, 1)

                def relu_a(u, a, b, src):
                    for k in range(a, b):
                        for h in range(HEADS):
                            at = k * HEADS + h
                            ins = nc.vector.scalar_tensor_tensor(TT[:, k, h * D:(h + 1) * D], src[:, k - a, h * D:(h + 1) * D],
                                                                 0.0, aB[:, h * D:(h + 1) * D], ALU.max, ALU.mult,
                                                                 accum_out=sc[:, u % 2, 0, at:at + 1])
                    return ins

                link(nc.vector.tensor_scalar(aB[:, :], aB[:, :], 1.0 - SLOPE, None, ALU.mult))
                rest = summed = low = 0
                for u in range(UNITS):
                    T, g = unit(u)
                    n = on_pe(u)
                    G = GB[u % NG]
                    x1, p1 = (X1H[:, T, :], PQ[:, T, :]) if T < NT else (XO, PO[:, :])
                    s1, s2 = (sc[:, u % 2, i, :].rearrange("p (k h) -> p k h", h=HEADS) for i in (1, 2))
                    if u == 2:
                        dve.wait_ge(x1_evac, NT)
                    dve.wait_ge(g_here[u % NG], 16 * GS * (u // NG + 1))
                    link.mark(nc.vector.tensor_tensor(s1, G[:, :, HD + D:TW],
                                                      p1.unsqueeze(1).to_broadcast([P, GS, HEADS]), ALU.add))
                    if u >= 1:
                        link.after(rest)
                    rest = link.mark(nc.vector.tensor_tensor(TT[:, n:GS, :], G[:, n:GS, 0:HD],
                                                             x1.unsqueeze(1).to_broadcast([P, GS - n, HD]), ALU.add))
                    if u >= 6 and u % 2 == 0:
                        divide((u - 6) // 2, low)
                    if n:
                        dve.wait_ge(sums_ready, sums_before(u + 1))
                        relu_a(u, 0, n, PS[:, sum_bank(u):sum_bank(u) + 1, :]).then_inc(sums_used, 1)
                    if u >= 1:
                        weigh(u - 1)
                    link.after(rest)
                    rest = link.mark(relu_a(u, n, GS, TT[:, n:GS, :]))
                    if u >= 5 and u % 2 == 1:
                        summed = den_sum((u - 5) // 2)
                    if n:
                        dve.wait_ge(sums_used, sums_before(u + 1))
                    if u >= 5 and u % 2 == 1:
                        summed = den_total((u - 5) // 2, summed)
                    if ended(u, LINEAR) is not None:
                        dve_leaky_sum(ended(u, LINEAR))
                    if ended(u, FINAL) is not None:
                        dve_out(ended(u, FINAL))
                    link.after(rest)
                    nc.vector.scalar_tensor_tensor(s2, s1, SLOPE, sc[:, u % 2, 0, :].rearrange("p (k h) -> p k h", h=HEADS),
                                                   ALU.mult, ALU.add).then_inc(score_ready, 1)
                    if u >= 5 and u % 2 == 1:
                        low = den_inverse((u - 5) // 2, summed)
                    if u == 3:
                        den_sum(NT)
                        dve.wait_ge(eg_used, 2 * GS)
                        nc.vector.tensor_copy(NO, bank(3)).then_inc(no_ready, 1)
                divide(NT - 2, low)
                weigh(UNITS - 1)
                summed = den_sum(NT - 1)
                dve_leaky_sum(ended(UNITS, LINEAR))
                summed = den_total(NT - 1, summed)
                divide(NT - 1, den_inverse(NT - 1, summed))
                dve_out(ended(UNITS + 1, FINAL))
                for u in range(UNITS + 2, DRAINED):
                    if ended(u, LINEAR) is not None:
                        dve_leaky_sum(ended(u, LINEAR))
                    if ended(u, FINAL) is not None:
                        dve_out(ended(u, FINAL))
            with dve.Else():
                dve.wait_ge(x1_evac, NT)
                K = 6 + GS * HEADS

                def chain(ins, n, i):
                    ins.then_inc(f_self, 1)
                    dve.wait_ge(f_self, n * K + 2 + i)

                wait_table(dve, tab3_written)
                nc.vector.memset(NUM[:, :, :], 0.0).then_inc(f_self, 1)
                nc.vector.memset(DEN[:, :, :], 0.0).then_inc(f_self, 1)
                dve.wait_ge(f_self, 2)
                nc.vector.tensor_scalar(DEN[:, NT - 1, :], DEN[:, NT - 1, :], padone[:, NT - 1:NT], None, ALU.add)
                nc.vector.memset(EWF[:, :, :], 0.0).then_inc(f_used, 1)
                dve.wait_ge(f_used, 1)
                with dve.Fori(0, NT) as t:
                    with dve.Fori(0, NP // GS) as g:
                        n = t * (NP // GS) + g
                        s0, s1, s2 = (sc[:, 0, i, :].rearrange("p (k h) -> p k h", h=HEADS) for i in range(3))
                        dve.wait_ge(f_here, n * 16 + 16)
                        nc.vector.tensor_tensor(s1, Ga[:, :, HD + D:TW],
                                                PQ[:, bass.ds(t, 1), :].to_broadcast([P, GS, HEADS]), ALU.add)
                        chain(nc.vector.tensor_tensor(TT[:, :, :], Ga[:, :, 0:HD],
                                                      X1H[:, bass.ds(t, 1), :].to_broadcast([P, GS, HD]), ALU.add), n, 1)
                        chain(nc.vector.scalar_tensor_tensor(TT[:, :, :], TT[:, :, :], 0.0,
                                                             aB[:, :].unsqueeze(1).to_broadcast([P, GS, HD]),
                                                             ALU.max, ALU.mult), n, 2)
                        chain(nc.vector.reduce_sum(s0, TT[:, :, :].rearrange("p k (h d) -> p k h d", d=D), AX.X), n, 3)
                        chain(nc.vector.tensor_scalar(s0, s0, 1.0 - SLOPE, None, ALU.mult), n, 4)
                        nc.vector.scalar_tensor_tensor(s2, s1, SLOPE, s0, ALU.mult, ALU.add).then_inc(f_score, 1)
                        dve.wait_ge(f_exp, n + 1)
                        chain(nc.vector.tensor_tensor(EWF[:, :, :], s2,
                                                      A[:, bass.ds(t, 1), bass.ds(g * GS, GS)].rearrange("p o k -> p k o")
                                                      .to_broadcast([P, GS, HEADS]), ALU.mult), n, 5)
                        for k in range(GS):
                            for h in range(HEADS):
                                acc = NUM[:, bass.ds(t, 1), h * D:(h + 1) * D]
                                chain(nc.vector.scalar_tensor_tensor(acc, Ga[:, k:k + 1, HD:HD + D], EWF[:, k, h:h + 1],
                                                                     acc, ALU.mult, ALU.add), n, 6 + k * HEADS + h)
                        chain(nc.vector.reduce_sum(DENF[:, :], EWF[:, :, :].rearrange("p k h -> p h k"), AX.X), n, K)
                        nc.vector.tensor_tensor(DEN[:, bass.ds(t, 1), :], DEN[:, bass.ds(t, 1), :],
                                                DENF[:, :].unsqueeze(1), ALU.add).then_inc(f_used, 1)
                        dve.wait_ge(f_used, n + 2)
                nc.vector.reciprocal(DEN[:, 0:NT, :], DEN[:, 0:NT, :]).then_inc(f_used, 1)
                dve.wait_ge(f_used, NT * (NP // GS) + 2)
                for t in range(NT):
                    nc.vector.tensor_tensor(NUM[:, t, :].rearrange("p (h d) -> p h d", d=D),
                                            NUM[:, t, :].rearrange("p (h d) -> p h d", d=D),
                                            DEN[:, t, :].unsqueeze(2).to_broadcast([P, HEADS, D]),
                                            ALU.mult).then_inc(num_ready, 1)
                for t in range(NT):
                    dve_leaky_sum(t)
                    dve_out(t)

        @block.gpsimd
        def _(pool):
            plink = Link(pool, pool_self)
            pool.memset(mhalf[:, :], -0.5).then_inc(consts, 1)
            plink(pool.memset(ident[:, :], 0.0))
            pool.affine_select(out=ident[:, :], in_=ident[:, :], compare_op=ALU.not_equal, fill=1.0,
                               base=0, pattern=[[-1, P]], channel_multiplier=1).then_inc(consts, 1)
            pool.wait_ge(consts, 2)
            for c in range(NC):
                pool_rstd(pool, 0, c)
            plink(pool.memset(phalf[:, :], 0.5))
            plink(pool.memset(negs[:, :], -1.0))
            plink(pool.memset(ones[:, :], 1.0))
            plink(pool.memset(iota[:, :], 0.0))
            plink(pool.memset(iota[0:1, :], 1.0))
            plink(pool.memset(iota[TWO:TWO + 1, :], 1.0))
            plink(pool.tensor_copy(OW[:, :], iota[:, :]))
            plink(pool.affine_select(out=ltri[:, :], in_=ones[:, :], compare_op=ALU.is_gt, fill=0.0,
                                     base=0, pattern=[[1, P]], channel_multiplier=-1))
            plink(pool.iota(own[:, :], pattern=[[P, NT]], base=0, channel_multiplier=1,
                            allow_small_or_imprecise_dtypes=True))
            plink(pool.memset(padone[:, :], 0.0))
            plink(pool.affine_select(out=padone[:, :], in_=padone[:, :], compare_op=ALU.is_ge, fill=1.0,
                                     base=N - 1, pattern=[[-P, NT]], channel_multiplier=-1))
            pool.iota(iota[:, :], pattern=[[1, P]], base=0, channel_multiplier=0,
                      allow_small_or_imprecise_dtypes=True).then_inc(consts, 1)

            def power(dst, src, exponent, ready, value, said, n=NT):
                pool.wait_ge(ready, value)
                pool.tensor_tensor(dst, src, exponent[:, 0:n], ALU.pow).then_inc(said, 1)

            power(st[:, DEGI, :], st[:, DEG, :], mhalf, deg_ready, 1, degi_ready)
            power(st[:, DL, :], st[:, RS2, :], mhalf, rs2_ready, 1, dl_ready)
            for c in range(NC):
                pool_rstd(pool, 1, c)
            for c, (a, b) in enumerate(CHUNKS):
                power(st[:, AN, a:b], st[:, AN2, a:b], phalf, n2_ready, c + 1, pow_out, b - a)
                if c >= 1:
                    a = 0 if c == 1 else a
                    power(st[:, T_D, a:b], st[:, T_C, a:b], phalf, pow_in, c, pow_out, b - a)
            for c, (a, b) in enumerate(CHUNKS):
                power(st[:, YN, a:b], st[:, YN2, a:b], phalf, yn2_ready, c + 1, pow_out, b - a)

            for c in range(NC):
                pool_rstd(pool, 2, c)
            for t in range(NT):
                power(S4[:, t, :], S4[:, t, :], phalf, d4_in, t + 1, d4_out, TOPK)
                if t in (6, 10):
                    a, b = CHUNKS[(t - 6) // 4]
                    power(st[:, DD, a:b], st[:, DD2I, a:b], mhalf, ssum_ready, (t - 6) // 4 + 1, dd_ready, b - a)
            a, b = CHUNKS[NC - 1]
            power(st[:, DD, a:b], st[:, DD2I, a:b], mhalf, ssum_ready, NC, dd_ready, b - a)
            pool.wait_ge(tab2_written, 16 * NC)
            for t in range(NT):
                if t >= NEAR:
                    pool.wait_ge(row_ready, NT + t - NEAR + 1)
                for k in range(1, TOPK):
                    pool.indirect_dma_start(G2[:, t % NEAR, k - 1, :], None, TAB2[:, :],
                                            bass.IndirectOffsetOnAxis(ap=I8[:, t, k:k + 1], axis=0))\
                        .then_inc(near_here[t % NEAR], 16)
                if t == 0:
                    pool.wait_ge(self_copied, NC)
                    pool.wait_ge(selfs_ready, 1)
                    known = pool.value_load(selfs[0:1, 0:1], min_val=0, max_val=1)
                    with pool.If(known < 1):
                        for i in range(NT):
                            pool.indirect_dma_start(SELF[:, i, :], None, TAB2[:, :],
                                                    bass.IndirectOffsetOnAxis(ap=I8[:, i, 0:1], axis=0))\
                                .then_inc(self_here, 16)
                        pool.wait_ge(self_here, 16 * NT)
                    pool.memset(spare[:, :], 0.0).then_inc(self_ready, 1)

            for c in range(NC):
                pool_rstd(pool, 3, c)
            pool.wait_ge(flag_ready, 1)
            sparse = pool.value_load(flag[0:1, 0:1], min_val=0, max_val=1)
            with pool.If(sparse > 0):
                pool.wait_ge(idx_ready, 1)
                wait_table(pool, tab3_written)
                for u in range(UNITS):
                    T, g = unit(u)
                    if u >= NG:
                        pool.wait_ge(eg_ready, GS * (u - NG + 1))
                    for k in range(GS):
                        at = g * GS + k
                        pool.indirect_dma_start(GB[u % NG][:, k, :], None, TAB3[:, :],
                                                bass.IndirectOffsetOnAxis(ap=IGU[:, T, at:at + 1], axis=0),
                                                bounds_check=NP - 1, oob_is_err=False).then_inc(g_here[u % NG], 16)

        @block.tensor
        def _(pe):
            def transpose_tile(t):
                pe.wait_ge(ld_a[t], 16)
                for g, (a, b) in enumerate(CHUNKS):
                    if t > 0:
                        pe.wait_ge(tr_evac, nth(t - 1, g) + 1)
                    for j in range(a, b):
                        last = nc.tensor.transpose(PS[:, 3 + g, (j - a) * P:(j - a + 1) * P],
                                                   A[:, t, j * P:(j + 1) * P], ident[:, :])
                    last.then_inc(tr_done, 1)

            pe.wait_ge(consts, 2)
            pe.wait_ge(pads, 3)
            for t in range(0, 4):
                transpose_tile(t)
            pe.wait_ge(h_ready, NC)
            pe.wait_ge(tr_evac, 4 * NC)
            pe_agg(pe, 0, 0, 0, 0, NT, H)
            for t in range(4, 8):
                transpose_tile(t)
            pe.wait_ge(ld_w, 16 * N_WEIGHTS)
            pe_l1(pe, 0, 0, 0)
            pe.wait_ge(tr_evac, 8 * NC)
            pe_agg(pe, 0, 0, 1, 0, 5, H)
            pe_l2(pe, 0, 0, 0)
            pe_agg(pe, 0, 0, 1, 5, 8, H)
            for t in range(8, NT):
                transpose_tile(t)
            pe_l3(pe, 0, 0, 0)
            pe_agg(pe, 0, 0, 1, 8, NT, H)
            pe.wait_ge(tr_evac, NT * NC)
            pe_agg(pe, 0, 0, 2, 0, 5, H)
            pe_l1(pe, 0, 0, 1)
            pe_agg(pe, 0, 0, 2, 5, NT, H)
            with pe.Fori(0, ROUNDS - 1) as r:
                pe_stage(pe, 2 * r + 1, 1)
                pe_stage(pe, 2 * r + 2, 0)
            pe_rest(pe, LAST_STAGE, 0)

            def row_transpose(src, t, base):
                c = t // 4
                if t % 4 == 0 and base + c >= 2:
                    pe.wait_ge(rowT_evac, base + c - 1)
                ins = nc.tensor.transpose(PS[:, 6 + c % 2, (t % 4) * P:(t % 4 + 1) * P], src[:, t, :], ident[:, :])
                if t + 1 == CHUNKS[c][1]:
                    ins.then_inc(rowT_done, 1)

            def row_aggregate(src, n, base, t, ready, rbase):
                if base + t >= 6:
                    pe.wait_ge(ragg_evac, base + t - 5)
                for j in range(NT):
                    if t == 0 and j in (0, 4, 8):
                        pe.wait_ge(ready, rbase + j // 4 + 1)
                    last = nc.tensor.matmul(bank(t % 6, n), AT[:, j, t * P:(t + 1) * P], src[:, j, 0:n],
                                            start=(j == 0), stop=(j == NT - 1))
                last.then_inc(ragg_done, 1)

            def row_product(w, c, done):
                a, b = CHUNKS[c]
                for t in range(a, b):
                    last = nc.tensor.matmul(PS[:, c, (t - a) * D:(t - a + 1) * D], T2[:, t * P:(t + 1) * P],
                                            W12[:, w, :], start=True, stop=True)
                last.then_inc(done, 1)

            pe.wait_ge(l2_bias, nth(LAST_STAGE, 2) + 1)
            for h in range(HEADS):
                ins = nc.tensor.transpose(PS[:, 7, h * D:(h + 1) * D], WL[:, h, :], ident[:, :])
            ins.then_inc(wl_done, 1)
            for t in range(NT + 2):
                if t < NT:
                    row_aggregate(XC, D + 1, 0, t, ye_ready, 0)
                if t >= 2:
                    if t == 2:
                        pe.wait_ge(l3_sum, nth(LAST_STAGE, 2) + 1)
                    if t == 6:
                        pe.wait_ge(wl_evac, 1)
                    pe.wait_ge(row_ready, t - 1)
                    row_transpose(U, t - 2, 0)
            pe.wait_ge(ragg_evac, NT)
            for c in range(NC):
                pe.wait_ge(rowT_evac, c + 1)
                row_product(0, c, prod_done)

            for t in range(NT + 2):
                if t < NT:
                    row_aggregate(XC, D, NT, t, ys_ready, 0)
                if t >= 2:
                    pe.wait_ge(ragg_evac, NT + t - 1)
                    row_transpose(U, t - 2, NC)
            for c in range(NC):
                lo, hi = cols(c)
                pe.wait_ge(rowT_evac, NC + c + 1)
                nc.tensor.matmul(bank(c, hi - lo), W12[:, 1, :], T2[:, lo:hi], start=True, stop=True).then_inc(z_done, 1)
            for c in range(NC):
                lo, hi = cols(c)
                pe.wait_ge(zsq_ready, c + 1)
                nc.tensor.matmul(bank(3 + c, hi - lo), negs[:, :], T2[:, lo:hi], start=True, stop=True).then_inc(sqb_done, 1)
            for t in range(NT):
                ins = nc.tensor.matmul(PS[:, 6, t:t + 1], T2[:, t * P:(t + 1) * P], negs[:, 0:1], start=True, stop=True)
            ins.then_inc(nsq_done, 1)
            pe.wait_ge(rowT_evac, NC + 2)
            pe.wait_ge(plan_ready, 1)
            nc.tensor.matmul(PS[:, 7, 0:2], ones[:, :], tally[:, :], start=True, stop=True)
            nc.tensor.matmul(PS[:, 7, 16:16 + NT], ltri[:, :], st[:, OVF, :], start=True, stop=False)
            nc.tensor.matmul(PS[:, 7, 16:16 + NT], ones[:, :], st[:, CUM, :], start=False, stop=True)\
                .then_inc(plan_done, 1)
            pe.wait_ge(z2_ready, NC)
            for t in range(NT):
                if t == 0:
                    pe.wait_ge(z_bias, NC)
                    pe.wait_ge(sq_ready, NC)
                elif t >= 2:
                    pe.wait_ge(key_read, t - 1)
                for c in range(NC):
                    lo, hi = cols(c)
                    hi = min(hi, N)
                    b = bank(3 * (t % 2) + c, hi - lo)
                    nc.tensor.matmul(b, Z[:, t * P:(t + 1) * P], T1[:, lo:hi], start=True, stop=False)
                    ins = nc.tensor.matmul(b, OW[0:TWO + 1, :], SQ[0:TWO + 1, lo:hi], start=False, stop=True)
                ins.then_inc(dist_done, 1)
            pe.wait_ge(key_read, NT)
            for t in range(NT + 2):
                if t < NT:
                    if t >= 3:
                        pe.wait_ge(ragg_evac, 2 * NT + t - 2)
                    for j in range(NT):
                        if t == 0 and j in (0, 4, 8):
                            pe.wait_ge(yd_ready, j // 4 + 1)
                        ins = nc.tensor.matmul(bank(3 + t % 3, D), AT[:, j, t * P:(t + 1) * P], U[:, j, :],
                                               start=(j == 0), stop=(j == NT - 1))
                    ins.then_inc(ragg_done, 1)
                if t == 0:
                    pe.wait_ge(nsq_evac, 1)
                    pe.wait_ge(others_ready, 1)
                    nc.tensor.matmul(PS[:, 6, 500:501], ones[:, :], others[:, :], start=True, stop=True).then_inc(others_done, 1)
                if t == 2:
                    pe.wait_ge(oh_ready, 1)
                    for o, src in ((64, WG), (64 + MAIN, IGF)):
                        for j in range(NT):
                            ins = nc.tensor.matmul(PS[:, 7, o:o + MAIN], OH[:, j, :], src[:, j, MAIN:NBR],
                                                   start=(j == 0), stop=(j == NT - 1))
                    ins.then_inc(over_done, 1)
                if t >= 2:
                    if t == 2:
                        pe.wait_ge(selfs_ready, 1)
                    if t == 6:
                        pe.wait_ge(idx_ready, 1)
                    pe.wait_ge(row_ready, NT + t - 1)
                    row_transpose(XC[:, :, 0:D], t - 2, 2 * NC)
                if t in (6, 10):
                    c = (t - 6) // 4
                    pe.wait_ge(rowT_evac, 2 * NC + c + 1)
                    row_product(2, c, prod_done)
            pe.wait_ge(ragg_evac, 3 * NT)
            for c, (a, b) in enumerate(CHUNKS):
                for t in range(a, b):
                    ins = nc.tensor.transpose(PS[:, 3 + c, (t - a) * P:(t - a + 1) * P], OH[:, t, :], ident[:, :])
                ins.then_inc(oht_done, 1)
            pe.wait_ge(rowT_evac, 3 * NC)
            row_product(2, NC - 1, prod_done)

            for t in range(NT):
                if t in (0, 4, 8):
                    pe.wait_ge(h_ready, nth(3, t // 4) + 1)
                row_transpose(H, t, 3 * NC)
            pe.wait_ge(rowT_evac, 4 * NC)
            pe.wait_ge(oht_evac, NC)
            for t in range(NT):
                if t >= 2:
                    pe.wait_ge(row3_ready, t - 1)
                nc.tensor.matmul(PS[:, 6 + t % 2, 0:2 * HEADS], T2[:, t * P:(t + 1) * P],
                                 WPQ[:, :, :].rearrange("p i h -> p (i h)"), start=True, stop=True)
                if t >= 3:
                    pe.wait_ge(x2_evac, t - 2)
                nc.tensor.matmul(bank(3 + t % 3), T2[:, t * P:(t + 1) * P], GW[:, 1, :],
                                 start=True, stop=True).then_inc(x2_done, 1)
            pe.wait_ge(x_ready, 2 * NC)
            for t in range(NT):
                if t >= 3:
                    pe.wait_ge(x1_evac, t - 2)
                nc.tensor.matmul(bank(t % 3), T2[:, t * P:(t + 1) * P], GW[:, 0, :],
                                 start=True, stop=True).then_inc(x1_done, 1)
                if t == 2:
                    pe.wait_ge(row3_ready, NT)
                    for j in range(NT):
                        ins = nc.tensor.matmul(bank(7, P), H[:, j, :], OH[:, j, :], start=(j == 0), stop=(j == NT - 1))
                    ins.then_inc(ho_done, 1)
                if t == 8:
                    pe.wait_ge(ho_evac, 1)
                    nc.tensor.matmul(bank(7), HO, GW[:, 0, :], start=True, stop=True)
                    nc.tensor.matmul(PS[:, 6, 128:128 + HEADS], HO, WPQ[:, 0, :],
                                     start=True, stop=True).then_inc(xo_done, 1)
            pe.wait_ge(x1_evac, NT)
            pe.wait_ge(row3_ready, NT)

            def pe_transpose(t):
                pe.wait_ge(num_ready, t + 1)
                if t >= 1:
                    pe.wait_ge(numT_evac, t)
                for h in range(HEADS):
                    ins = nc.tensor.transpose(PS[:, 3, h * P:(h + 1) * P], NUM[:, t, h * D:(h + 1) * D], ident[:, :])
                ins.then_inc(numT_done, 1)

            def pe_linear(t):
                pe.wait_ge(numT_evac, t + 1)
                if 1 <= t < NT - 1:
                    pe.wait_ge(out_ready, t)
                for h in range(HEADS):
                    ins = nc.tensor.matmul(PS[:, lin_bank(t), h * P:(h + 1) * P], WLT[:, h, :],
                                           AGT[t % 2][:, h * P:(h + 1) * P], start=True, stop=True)
                ins.then_inc(lin_done, 1)

            def pe_final(t):
                pe.wait_ge(lin_ready, t + 1)
                for h in range(HEADS):
                    ins = nc.tensor.matmul(bank(lin_bank(t), D), LRS[t % 2][:, h * P:(h + 1) * P], WO[:, h, :],
                                           start=(h == 0), stop=(h == HEADS - 1))
                ins.then_inc(fin_done, 1)

            sparse = pe.value_load(flag[0:1, 0:1], min_val=0, max_val=1)
            with pe.If(sparse > 0):
                def sums(u):
                    T, g = unit(u)
                    x1 = X1H[:, T, :] if T < NT else XO
                    pe.wait_ge(g_here[u % NG], 16 * GS * (u // NG + 1))
                    if u == 0:
                        pe.wait_ge(xo_read, 1)
                    if u >= 2:
                        pe.wait_ge(sums_used, sums_before(u - 1))
                    nc.tensor.matmul(bank(sum_bank(u)), ident[:, :], x1, start=True, stop=False)
                    nc.tensor.matmul(bank(sum_bank(u)), ident[:, :], GB[u % NG][:, 0, 0:HD],
                                     start=False, stop=True).then_inc(sums_ready, 1)

                def numerators(u):
                    T, g = unit(u)
                    b = 3 if T == NT else 4 + T % 2
                    if T < NT and g == 0 and T >= 2:
                        pe.wait_ge(num_ready, T - 1)
                    for k in range(GS):
                        pe.wait_ge(eg_ready, GS * u + k + 1)
                        nc.tensor.matmul(bank(b), ident[:, :], EG[:, k % NE, :], start=(g == 0 and k == 0),
                                         stop=(T == NT and g == 1 and k == GS - 1)).then_inc(eg_used, 1)
                    if T < NT and g == 1:
                        if T == 0:
                            pe.wait_ge(no_ready, 1)
                        nc.tensor.matmul(bank(b), OHT[:, T, :], NO, start=False, stop=True)
                        if T >= 1:
                            pe.wait_ge(num_ready, T)
                        nc.tensor.matmul(PS[:, 7, 256:256 + HEADS], OHT[:, T, :], DEN[:, NT, :],
                                         start=True, stop=True).then_inc(num_done, 1)

                for u in range(DRAINED):
                    if u < UNITS:
                        if on_pe(u):
                            sums(u)
                        if u >= 2:
                            numerators(u - 2)
                    if ended(u, TRANSPOSE) is not None:
                        pe_transpose(ended(u, TRANSPOSE))
                    if UNITS <= u < UNITS + 2:
                        numerators(u - 2)
                    if ended(u, FINAL) is not None:
                        pe_final(ended(u, FINAL))
                    if ended(u, LINEAR) is not None:
                        pe_linear(ended(u, LINEAR))
            with pe.Else():
                for t in range(NT):
                    pe_transpose(t)
                    pe_linear(t)
                    pe_final(t)


_INS = ['x', 'adj', 'L0_gnn_v_node_feats', 'L0_gnn_uv_W1', 'L0_gnn_uv_b1', 'L0_gnn_uv_W2', 'L0_gnn_uv_b2',
        'L0_gnn_uv_W3', 'L0_gnn_uv_b3', 'L0_gnn_vu_W1', 'L0_gnn_vu_b1', 'L0_gnn_vu_W2', 'L0_gnn_vu_b2',
        'L0_gnn_vu_W3', 'L0_gnn_vu_b3', 'L1_gnn_W', 'L1_gnn_b', 'L2_gnn_W1', 'L2_gnn_b1', 'L2_gnn_W2',
        'L2_gnn_b2', 'L3_gnn_w1', 'L3_gnn_w2', 'L3_gnn_a', 'L3_gnn_Wlin', 'L3_gnn_w']


def kernel(**inputs):
    import numpy as _np
    import concourse.bacc as _bacc
    from concourse import mybir as _mybir
    from concourse.bass_utils import run_bass_kernel_spmd as _run

    nc = _bacc.Bacc("TRN2", target_bir_lowering=False, num_devices=1)
    arrays, args = {}, []
    for name in _INS:
        a = _np.ascontiguousarray(inputs[name])
        arrays[f"in_{name}"] = a
        args.append(nc.dram_tensor(f"in_{name}", a.shape, _mybir.dt.from_np(a.dtype), kind="ExternalInput").ap())
    args.append(nc.dram_tensor("out_0", (N, D), _mybir.dt.float32, kind="ExternalOutput").ap())
    build(nc, *args)
    r = _run(nc, [arrays], core_ids=[0])
    return r.results[0]["out_0"]
```
